# Optimizing a Trainium2 kernel written in Bass

```python
import numpy as np
import jax
import jax.numpy as jnp

def _softmax(x, axis=-1):
    return jax.nn.softmax(x, axis=axis)

def _gelu(x):
    return jax.nn.gelu(x, approximate=True)

def _silu(x):
    return jax.nn.silu(x)

def _sigmoid(x):
    return jax.nn.sigmoid(x)

def _layernorm(x, axis=-1, eps=1e-05):
    m = jnp.mean(x, axis=axis, keepdims=True)
    v = jnp.var(x, axis=axis, keepdims=True)
    return (x - m) / jnp.sqrt(v + eps)

def _scatter_add(tgt, idx, src, axis=0):
    return tgt.at[idx].add(src)

def _segment_sum(src, seg, n):
    return jax.ops.segment_sum(src, seg, n)
kernel_name = 'mk_flamingo_gated_d4_seqx_r8_4c2d30'

def setup_inputs(seed: int=0):
    np.random.seed(seed)
    _w = jnp.asarray

    def _rec_inputs():
        import jax
        import jax.numpy as jnp
        _rk = jax.random.key(seed)
        x = 7.22e-05 + 1 * jax.random.normal(jax.random.fold_in(_rk, 1), (16, 56, 256), jnp.float32)
        _lenS = 56 - jax.random.randint(jax.random.fold_in(_rk, 7), (16,), 0, max(1, 56 // 4) + 1, jnp.int32)
        _lenS2 = 1500 - jax.random.randint(jax.random.fold_in(_rk, 8), (16,), 0, max(1, 1500 // 4) + 1, jnp.int32)
        _ctx_512P = jax.random.normal(jax.random.fold_in(_rk, 11), (16, 16, 64), jnp.float32)
        _ctx_512c = jax.random.dirichlet(jax.random.fold_in(_rk, 511), 0.3 * jnp.ones((16,), jnp.float32), (16, 1500))
        _ctx_512t = jnp.einsum('bsk,bkd->bsd', _ctx_512c, _ctx_512P)
        _ctx_512t = _ctx_512t * jax.lax.rsqrt(jnp.mean(jnp.square(_ctx_512t)) + 1e-12) * 0.953939
        ctx_512 = -0.000514642 + 1.00011 * (_ctx_512t + 0.3 * jax.random.normal(jax.random.fold_in(_rk, 611), (16, 1500, 64), jnp.float32))
        _g = jax.random.normal(jax.random.fold_in(_rk, 9001), (2, 4), jnp.float32)
        _g = jnp.sign(_g) * jnp.maximum(jnp.abs(_g), 1.0) + (_g == 0) * 1.0
        g_xattn = _g[0]
        g_ffn = _g[1]
        return (x, ctx_512, g_xattn, g_ffn)
    x, ctx_512, g_xattn, g_ffn = _rec_inputs()

    def _L0_xattn_setup():
        import jax, jax.numpy as jnp
        import numpy as np
        B, S, H, NH, L = (2, 256, 256, 16, 64)
        HD = H // NH
        key = jax.random.key(seed)
        k1, k2, k3, k4, k5 = jax.random.split(key, 5)
        scale = 0.02
        return {'q': jax.random.normal(k1, (B, S, H), dtype=jnp.float32), 'latent_kv': jax.random.normal(k2, (B, S, L), dtype=jnp.float32), 'Wq': jax.random.normal(k3, (H, H), dtype=jnp.float32) * scale, 'Wkv_expand': jax.random.normal(k4, (2 * H, L), dtype=jnp.float32) * scale, 'Wout': jax.random.normal(k5, (H, H), dtype=jnp.float32) * scale}
    _L0_xattn_all = _L0_xattn_setup()
    _L0_xattn_in = {k: v for k, v in _L0_xattn_all.items() if k in ('Wq', 'Wkv_expand', 'Wout')}
    del _L0_xattn_all

    def _L0_ffn_setup():
        import jax, jax.numpy as jnp
        import numpy as np
        TOP_K = 8
        key = jax.random.key(seed)
        k1, k2, k3 = jax.random.split(key, 3)
        B, S, H, E = (4, 512, 256, 64)
        hidden_states = jax.random.normal(k1, (B, S, H), dtype=jnp.float32)
        router_weight = jax.random.normal(k2, (E, H), dtype=jnp.float32)
        router_bias = jnp.zeros((E,), dtype=jnp.float32)
        expert_bias = jax.random.normal(k3, (E, H), dtype=jnp.float32) * 0.1
        return {'hidden_states': hidden_states, 'router_weight': router_weight, 'router_bias': router_bias, 'expert_bias': expert_bias}
    _L0_ffn_all = _L0_ffn_setup()
    _L0_ffn_in = {k: v for k, v in _L0_ffn_all.items() if k in ('router_weight', 'router_bias', 'expert_bias')}
    del _L0_ffn_all

    def _L1_xattn_setup():
        import jax, jax.numpy as jnp
        import numpy as np
        B, S, L = (2, 128, 128)
        DIM_Q, H, K, D_C, D_CQ, R = (256, 16, 128, 64, 192, 64)

        def _rope_tables(seq_len, dim, dtype):
            inv_freq = 1.0 / 10000.0 ** (jnp.arange(0, dim, 2, dtype=dtype) / dim)
            t = jnp.arange(seq_len, dtype=dtype)
            freqs = t[:, None] * inv_freq[None, :]
            sin = jnp.repeat(jnp.sin(freqs), 2, axis=-1)
            cos = jnp.repeat(jnp.cos(freqs), 2, axis=-1)
            return (sin, cos)

        def _rotate_half(x):
            h = x.shape[-1] // 2
            return jnp.concatenate([-x[..., h:], x[..., :h]], axis=-1)
        key = jax.random.key(seed)
        ks = jax.random.split(key, 8)
        s_in = 1.0 / np.sqrt(DIM_Q)
        s_k = 1.0 / np.sqrt(K)
        s_cq = 1.0 / np.sqrt(D_CQ)
        s_c = 1.0 / np.sqrt(D_C)
        return {'hidden_q': jax.random.normal(ks[0], (B, S, DIM_Q), jnp.float32), 'kv_c': jax.random.normal(ks[1], (B, L, D_C), jnp.float32), 'Wq': jax.random.normal(ks[2], (H * K, DIM_Q), jnp.float32) * s_in, 'w_kc_q': jax.random.normal(ks[3], (H, K, D_CQ), jnp.float32) * s_k, 'w_kc_kv': jax.random.normal(ks[4], (H, K, D_C), jnp.float32) * s_k, 'W_qr': jax.random.normal(ks[5], (H, D_CQ, R), jnp.float32) * s_cq / np.sqrt(R), 'W_kr': jax.random.normal(ks[6], (H, D_C, R), jnp.float32) * s_c, 'Wo': jax.random.normal(ks[7], (DIM_Q, H * K), jnp.float32) * s_k}
    _L1_xattn_all = _L1_xattn_setup()
    _L1_xattn_in = {k: v for k, v in _L1_xattn_all.items() if k in ('Wq', 'w_kc_q', 'w_kc_kv', 'W_qr', 'W_kr', 'Wo')}
    del _L1_xattn_all

    def _L1_ffn_setup():
        import jax, jax.numpy as jnp
        import numpy as np
        EPS = 1e-05

        def fwht(x):
            orig_shape = x.shape
            n = orig_shape[-1]
            x = x.reshape(-1, n)
            h = 1
            while h < n:
                x = x.reshape(-1, n // (2 * h), 2, h)
                a, b = (x[:, :, 0, :], x[:, :, 1, :])
                x = jnp.stack([a + b, a - b], axis=2).reshape(-1, n)
                h *= 2
            return (x * (1.0 / np.sqrt(n))).reshape(orig_shape)

        def act_quant(x):
            scale = 127.0 / jnp.clip(jnp.max(jnp.abs(x), axis=-1, keepdims=True), EPS)
            q = jnp.clip(jnp.round(x * scale), -128.0, 127.0) / scale
            return x + jax.lax.stop_gradient(q - x)

        def weight_quant(w):
            scale = jnp.clip(jnp.mean(jnp.abs(w)), EPS)
            q = jnp.clip(jnp.round(w / scale), -1.0, 1.0) * scale
            return w + jax.lax.stop_gradient(q - w)

        def h_bitlinear(x, w):
            xq = act_quant(fwht(x))
            wq = weight_quant(w)
            return jnp.einsum('bsh,oh->bso', xq, wq)
        key = jax.random.key(seed)
        k1, k2, k3, k4 = jax.random.split(key, 4)
        H, I = (256, 1024)
        B, S = (2, 256)
        hidden_states = jax.random.normal(k1, (B, S, H), dtype=jnp.float32)
        w_gate = jax.random.normal(k2, (I, H), dtype=jnp.float32) * 0.02
        w_up = jax.random.normal(k3, (I, H), dtype=jnp.float32) * 0.02
        w_down = jax.random.normal(k4, (H, I), dtype=jnp.float32) * 0.02
        return {'hidden_states': hidden_states, 'w_gate': w_gate, 'w_up': w_up, 'w_down': w_down}
    _L1_ffn_all = _L1_ffn_setup()
    _L1_ffn_in = {k: v for k, v in _L1_ffn_all.items() if k in ('w_gate', 'w_up', 'w_down')}
    del _L1_ffn_all

    def _L2_xattn_setup():
        import jax, jax.numpy as jnp
        import numpy as np
        B, S, L = (2, 128, 128)
        DIM_Q, H, K, D_C, D_CQ, R = (256, 16, 128, 64, 192, 64)

        def _rope_tables(length, dim):
            inv = 1.0 / 10000.0 ** (jnp.arange(0, dim, 2, dtype=jnp.float32) / dim)
            f = jnp.arange(length, dtype=jnp.float32)[:, None] * inv[None, :]
            sin = jnp.repeat(jnp.sin(f), 2, axis=-1)
            cos = jnp.repeat(jnp.cos(f), 2, axis=-1)
            return (sin, cos)

        def _rotate_half(x):
            half = x.shape[-1] // 2
            return jnp.concatenate([-x[..., half:], x[..., :half]], axis=-1)

        def _apply_rope(x, sin, cos):
            return x * cos + _rotate_half(x) * sin
        key = jax.random.key(seed)
        ks = jax.random.split(key, 8)
        return {'hidden_q': jax.random.normal(ks[0], (B, S, DIM_Q), jnp.float32), 'kv_c': jax.random.normal(ks[1], (B, L, D_C), jnp.float32), 'Wq': jax.random.normal(ks[2], (H * K, DIM_Q), jnp.float32) / np.sqrt(DIM_Q).astype(np.float32), 'w_kc_q': jax.random.normal(ks[3], (H, K, D_CQ), jnp.float32) / np.sqrt(K).astype(np.float32), 'w_kc_kv': jax.random.normal(ks[4], (H, K, D_C), jnp.float32) / np.sqrt(K).astype(np.float32), 'W_qr': jax.random.normal(ks[5], (H, D_CQ, R), jnp.float32) / np.float32(np.sqrt(D_CQ) * np.sqrt(R)), 'W_kr': jax.random.normal(ks[6], (H, D_C, R), jnp.float32) / np.sqrt(D_C).astype(np.float32), 'Wo': jax.random.normal(ks[7], (DIM_Q, H * K), jnp.float32) / np.sqrt(H * K).astype(np.float32)}
    _L2_xattn_all = _L2_xattn_setup()
    _L2_xattn_in = {k: v for k, v in _L2_xattn_all.items() if k in ('Wq', 'w_kc_q', 'w_kc_kv', 'W_qr', 'W_kr', 'Wo')}
    del _L2_xattn_all

    def _L2_ffn_setup():
        import jax, jax.numpy as jnp
        import numpy as np
        HIDDEN = 256
        INTER = 1024
        SCALE = 64.0

        def fwht(x):
            orig_shape = x.shape
            n = orig_shape[-1]
            x = x.reshape(-1, n)
            h = 1
            while h < n:
                x = x.reshape(-1, n // (2 * h), 2, h)
                a, b = (x[:, :, 0, :], x[:, :, 1, :])
                x = jnp.stack([a + b, a - b], axis=2).reshape(-1, n)
                h *= 2
            return (x / jnp.sqrt(jnp.asarray(n, x.dtype))).reshape(orig_shape)
        key = jax.random.key(seed)
        ks = jax.random.split(key, 8)
        inp = jax.random.normal(ks[0], (4, 256, HIDDEN), dtype=jnp.float32)
        SU_ug = jnp.where(jax.random.bernoulli(ks[1], 0.5, (HIDDEN,)), 1.0, -1.0).astype(jnp.float32)
        SU_dp = jnp.where(jax.random.bernoulli(ks[2], 0.5, (INTER,)), 1.0, -1.0).astype(jnp.float32)
        Wscale_ug = jax.random.uniform(ks[3], (2 * INTER,), jnp.float32, 0.5, 1.5)
        Wscale_dp = jax.random.uniform(ks[4], (HIDDEN,), jnp.float32, 0.5, 1.5)
        W_up = jax.random.normal(ks[5], (INTER, HIDDEN), dtype=jnp.float32) * 0.02
        W_gate = jax.random.normal(ks[6], (INTER, HIDDEN), dtype=jnp.float32) * 0.02
        W_down = jax.random.normal(ks[7], (HIDDEN, INTER), dtype=jnp.float32) * 0.02
        return {'input': inp, 'SU_ug': SU_ug, 'SU_dp': SU_dp, 'Wscale_ug': Wscale_ug, 'Wscale_dp': Wscale_dp, 'W_up': W_up, 'W_gate': W_gate, 'W_down': W_down}
    _L2_ffn_all = _L2_ffn_setup()
    _L2_ffn_in = {k: v for k, v in _L2_ffn_all.items() if k in ('SU_ug', 'SU_dp', 'Wscale_ug', 'Wscale_dp', 'W_up', 'W_gate', 'W_down')}
    del _L2_ffn_all

    def _L3_xattn_setup():
        import jax, jax.numpy as jnp
        import numpy as np
        B, S, H, NH, L = (2, 256, 256, 16, 64)
        HD = H // NH
        key = jax.random.key(seed)
        k1, k2, k3, k4, k5 = jax.random.split(key, 5)
        scale = 0.02
        return {'q': jax.random.normal(k1, (B, S, H), dtype=jnp.float32), 'latent_kv': jax.random.normal(k2, (B, S, L), dtype=jnp.float32), 'Wq': jax.random.normal(k3, (H, H), dtype=jnp.float32) * scale, 'Wkv_expand': jax.random.normal(k4, (2 * H, L), dtype=jnp.float32) * scale, 'Wout': jax.random.normal(k5, (H, H), dtype=jnp.float32) * scale}
    _L3_xattn_all = _L3_xattn_setup()
    _L3_xattn_in = {k: v for k, v in _L3_xattn_all.items() if k in ('Wq', 'Wkv_expand', 'Wout')}
    del _L3_xattn_all

    def _L3_ffn_setup():
        import jax, jax.numpy as jnp
        import numpy as np
        B, S, D, F, E, K = (2, 256, 256, 512, 8, 1)

        def _silu_mul(gu):
            g, u = jnp.split(gu, 2, axis=-1)
            return jax.nn.silu(g) * u

        def _moe_forward(hidden_states, router_w, w_gate_up, w_down, shared_gate_up, shared_down, top_k=K):
            b, s, d = hidden_states.shape
            x = hidden_states.reshape(-1, d)
            router_logits = x @ router_w.T
            topk_vals, topk_ids = jax.lax.top_k(router_logits, top_k)
            gate = jax.nn.sigmoid(topk_vals.astype(jnp.float32)).astype(x.dtype)
            xs = (x[:, None, :] * gate[:, :, None]).reshape(-1, d)
            ids_flat = topk_ids.reshape(-1)
            n_experts = w_gate_up.shape[0]

            def body(acc, inp):
                wg, wd, e = inp
                h = _silu_mul(xs @ wg)
                o = h @ wd
                mask = (ids_flat == e)[:, None]
                return (acc + jnp.where(mask, o, jnp.zeros((), o.dtype)), None)
            acc0 = jnp.zeros_like(xs)
            routed, _ = jax.lax.scan(body, acc0, (w_gate_up, w_down, jnp.arange(n_experts)))
            routed = routed.reshape(-1, top_k, d).sum(1)
            shared = _silu_mul(x @ shared_gate_up) @ shared_down
            return (routed + shared).reshape(b, s, d)
        key = jax.random.key(seed)
        ks = jax.random.split(key, 6)
        scale = 0.02
        return {'hidden_states': jax.random.normal(ks[0], (B, S, D), jnp.float32), 'router_w': jax.random.normal(ks[1], (E, D), jnp.float32) * scale, 'w_gate_up': jax.random.normal(ks[2], (E, D, 2 * F), jnp.float32) * scale, 'w_down': jax.random.normal(ks[3], (E, F, D), jnp.float32) * scale, 'shared_gate_up': jax.random.normal(ks[4], (D, 2 * F), jnp.float32) * scale, 'shared_down': jax.random.normal(ks[5], (F, D), jnp.float32) * scale}
    _L3_ffn_all = _L3_ffn_setup()
    _L3_ffn_in = {k: v for k, v in _L3_ffn_all.items() if k in ('router_w', 'w_gate_up', 'w_down', 'shared_gate_up', 'shared_down')}
    del _L3_ffn_all
    return {'x': x, 'ctx_512': ctx_512, 'g_xattn': g_xattn, 'g_ffn': g_ffn, 'L0_xattn_Wq': _L0_xattn_in['Wq'], 'L0_xattn_Wkv_expand': _L0_xattn_in['Wkv_expand'], 'L0_xattn_Wout': _L0_xattn_in['Wout'], 'L0_ffn_router_weight': _L0_ffn_in['router_weight'], 'L0_ffn_router_bias': _L0_ffn_in['router_bias'], 'L0_ffn_expert_bias': _L0_ffn_in['expert_bias'], 'L1_xattn_Wq': _L1_xattn_in['Wq'], 'L1_xattn_w_kc_q': _L1_xattn_in['w_kc_q'], 'L1_xattn_w_kc_kv': _L1_xattn_in['w_kc_kv'], 'L1_xattn_W_qr': _L1_xattn_in['W_qr'], 'L1_xattn_W_kr': _L1_xattn_in['W_kr'], 'L1_xattn_Wo': _L1_xattn_in['Wo'], 'L1_ffn_w_gate': _L1_ffn_in['w_gate'], 'L1_ffn_w_up': _L1_ffn_in['w_up'], 'L1_ffn_w_down': _L1_ffn_in['w_down'], 'L2_xattn_Wq': _L2_xattn_in['Wq'], 'L2_xattn_w_kc_q': _L2_xattn_in['w_kc_q'], 'L2_xattn_w_kc_kv': _L2_xattn_in['w_kc_kv'], 'L2_xattn_W_qr': _L2_xattn_in['W_qr'], 'L2_xattn_W_kr': _L2_xattn_in['W_kr'], 'L2_xattn_Wo': _L2_xattn_in['Wo'], 'L2_ffn_SU_ug': _L2_ffn_in['SU_ug'], 'L2_ffn_SU_dp': _L2_ffn_in['SU_dp'], 'L2_ffn_Wscale_ug': _L2_ffn_in['Wscale_ug'], 'L2_ffn_Wscale_dp': _L2_ffn_in['Wscale_dp'], 'L2_ffn_W_up': _L2_ffn_in['W_up'], 'L2_ffn_W_gate': _L2_ffn_in['W_gate'], 'L2_ffn_W_down': _L2_ffn_in['W_down'], 'L3_xattn_Wq': _L3_xattn_in['Wq'], 'L3_xattn_Wkv_expand': _L3_xattn_in['Wkv_expand'], 'L3_xattn_Wout': _L3_xattn_in['Wout'], 'L3_ffn_router_w': _L3_ffn_in['router_w'], 'L3_ffn_w_gate_up': _L3_ffn_in['w_gate_up'], 'L3_ffn_w_down': _L3_ffn_in['w_down'], 'L3_ffn_shared_gate_up': _L3_ffn_in['shared_gate_up'], 'L3_ffn_shared_down': _L3_ffn_in['shared_down']}

def reference(x, ctx_512, g_xattn, g_ffn, L0_xattn_Wq, L0_xattn_Wkv_expand, L0_xattn_Wout, L0_ffn_router_weight, L0_ffn_router_bias, L0_ffn_expert_bias, L1_xattn_Wq, L1_xattn_w_kc_q, L1_xattn_w_kc_kv, L1_xattn_W_qr, L1_xattn_W_kr, L1_xattn_Wo, L1_ffn_w_gate, L1_ffn_w_up, L1_ffn_w_down, L2_xattn_Wq, L2_xattn_w_kc_q, L2_xattn_w_kc_kv, L2_xattn_W_qr, L2_xattn_W_kr, L2_xattn_Wo, L2_ffn_SU_ug, L2_ffn_SU_dp, L2_ffn_Wscale_ug, L2_ffn_Wscale_dp, L2_ffn_W_up, L2_ffn_W_gate, L2_ffn_W_down, L3_xattn_Wq, L3_xattn_Wkv_expand, L3_xattn_Wout, L3_ffn_router_w, L3_ffn_w_gate_up, L3_ffn_w_down, L3_ffn_shared_gate_up, L3_ffn_shared_down):
    import jax
    import jax.numpy as jnp

    def _L0_xattn_ref(q, latent_kv, Wq, Wkv_expand, Wout):
        import jax, jax.numpy as jnp
        import numpy as np
        B, S, H, NH, L = (2, 256, 256, 16, 64)
        HD = H // NH
        b, sq, _ = q.shape
        sk = latent_kv.shape[1]
        qp = q @ Wq.T
        kv = latent_kv @ Wkv_expand.T
        k, v = jnp.split(kv, 2, axis=-1)
        qh = qp.reshape(b, sq, NH, HD).transpose(0, 2, 1, 3)
        kh = k.reshape(b, sk, NH, HD).transpose(0, 2, 1, 3)
        vh = v.reshape(b, sk, NH, HD).transpose(0, 2, 1, 3)
        inv_sqrt_d = 1.0 / jnp.sqrt(jnp.float32(HD))
        scores = jnp.einsum('bhqd,bhkd->bhqk', qh, kh) * inv_sqrt_d
        causal = jnp.tril(jnp.ones((sq, sk), dtype=bool))
        scores = jnp.where(causal, scores, jnp.finfo(scores.dtype).min)
        attn = jax.nn.softmax(scores, axis=-1)
        out = jnp.einsum('bhqk,bhkd->bhqd', attn, vh)
        out = out.transpose(0, 2, 1, 3).reshape(b, sq, H)
        return out @ Wout.T

    def _L0_ffn_ref(hidden_states, router_weight, router_bias, expert_bias):
        import jax, jax.numpy as jnp
        import numpy as np
        TOP_K = 8
        B, S, H = hidden_states.shape
        flat = hidden_states.reshape(B * S, H)
        logits = jnp.einsum('th,eh->te', flat, router_weight) + router_bias
        scores = jax.nn.softmax(logits, axis=-1)
        topk_w, topk_idx = jax.lax.top_k(scores, TOP_K)
        gathered_bias = expert_bias[topk_idx]
        out = flat * jnp.sum(topk_w, axis=-1, keepdims=True) + jnp.einsum('tk,tkh->th', topk_w, gathered_bias)
        return out.reshape(B, S, H)

    def _L1_xattn_ref(hidden_q, kv_c, Wq, w_kc_q, w_kc_kv, W_qr, W_kr, Wo):
        import jax, jax.numpy as jnp
        import numpy as np
        B, S, L = (2, 128, 128)
        DIM_Q, H, K, D_C, D_CQ, R = (256, 16, 128, 64, 192, 64)

        def _rope_tables(seq_len, dim, dtype):
            inv_freq = 1.0 / 10000.0 ** (jnp.arange(0, dim, 2, dtype=dtype) / dim)
            t = jnp.arange(seq_len, dtype=dtype)
            freqs = t[:, None] * inv_freq[None, :]
            sin = jnp.repeat(jnp.sin(freqs), 2, axis=-1)
            cos = jnp.repeat(jnp.cos(freqs), 2, axis=-1)
            return (sin, cos)

        def _rotate_half(x):
            h = x.shape[-1] // 2
            return jnp.concatenate([-x[..., h:], x[..., :h]], axis=-1)
        b, s, _ = hidden_q.shape
        l = kv_c.shape[1]
        q_hk = (hidden_q @ Wq.T).reshape(b, s, H, K)
        q_big = jnp.einsum('bshk,hkq->bshq', q_hk, w_kc_q)
        sin, cos = _rope_tables(l, D_C, kv_c.dtype)
        kv_rope = kv_c * cos[None] + _rotate_half(kv_c) * sin[None]
        q_r = jnp.einsum('bshq,hqr->bhsr', q_big, W_qr)
        k_r = jnp.einsum('bld,hdr->bhlr', kv_rope, W_kr)
        scores = jnp.einsum('bhsr,bhlr->bhsl', q_r, k_r)
        attn = jax.nn.softmax(scores, axis=-1)
        ctx_c = jnp.einsum('bhsl,bld->bhsd', attn, kv_rope)
        ctx_lat = jnp.einsum('bhsd,hkd->bshk', ctx_c, w_kc_kv)
        out = ctx_lat.reshape(b, s, H * K) @ Wo.T
        return out

    def _L1_ffn_ref(hidden_states, w_gate, w_up, w_down):
        import jax, jax.numpy as jnp
        import numpy as np
        EPS = 1e-05

        def fwht(x):
            orig_shape = x.shape
            n = orig_shape[-1]
            x = x.reshape(-1, n)
            h = 1
            while h < n:
                x = x.reshape(-1, n // (2 * h), 2, h)
                a, b = (x[:, :, 0, :], x[:, :, 1, :])
                x = jnp.stack([a + b, a - b], axis=2).reshape(-1, n)
                h *= 2
            return (x * (1.0 / np.sqrt(n))).reshape(orig_shape)

        def act_quant(x):
            scale = 127.0 / jnp.clip(jnp.max(jnp.abs(x), axis=-1, keepdims=True), EPS)
            q = jnp.clip(jnp.round(x * scale), -128.0, 127.0) / scale
            return x + jax.lax.stop_gradient(q - x)

        def weight_quant(w):
            scale = jnp.clip(jnp.mean(jnp.abs(w)), EPS)
            q = jnp.clip(jnp.round(w / scale), -1.0, 1.0) * scale
            return w + jax.lax.stop_gradient(q - w)

        def h_bitlinear(x, w):
            xq = act_quant(fwht(x))
            wq = weight_quant(w)
            return jnp.einsum('bsh,oh->bso', xq, wq)
        gate = h_bitlinear(hidden_states, w_gate)
        up = h_bitlinear(hidden_states, w_up)
        return h_bitlinear(jax.nn.silu(gate) * up, w_down)

    def _L2_xattn_ref(hidden_q, kv_c, Wq, w_kc_q, w_kc_kv, W_qr, W_kr, Wo):
        import jax, jax.numpy as jnp
        import numpy as np
        B, S, L = (2, 128, 128)
        DIM_Q, H, K, D_C, D_CQ, R = (256, 16, 128, 64, 192, 64)

        def _rope_tables(length, dim):
            inv = 1.0 / 10000.0 ** (jnp.arange(0, dim, 2, dtype=jnp.float32) / dim)
            f = jnp.arange(length, dtype=jnp.float32)[:, None] * inv[None, :]
            sin = jnp.repeat(jnp.sin(f), 2, axis=-1)
            cos = jnp.repeat(jnp.cos(f), 2, axis=-1)
            return (sin, cos)

        def _rotate_half(x):
            half = x.shape[-1] // 2
            return jnp.concatenate([-x[..., half:], x[..., :half]], axis=-1)

        def _apply_rope(x, sin, cos):
            return x * cos + _rotate_half(x) * sin
        Bv, Sv, _ = hidden_q.shape
        _, Lv, _ = kv_c.shape
        q_hk = (hidden_q @ Wq.T).reshape(Bv, Sv, H, K)
        q_big = jnp.einsum('bshk,hkq->bshq', q_hk, w_kc_q)
        sin_q, cos_q = _rope_tables(Sv, D_CQ)
        q_big = _apply_rope(q_big, sin_q[None, :, None, :], cos_q[None, :, None, :])
        sin_k, cos_k = _rope_tables(Lv, D_C)
        kv_r = _apply_rope(kv_c, sin_k[None], cos_k[None])
        q_r = jnp.einsum('bshq,hqr->bhsr', q_big, W_qr)
        k_r = jnp.einsum('bld,hdr->bhlr', kv_r, W_kr)
        scores = jnp.einsum('bhsr,bhlr->bhsl', q_r, k_r)
        attn = jax.nn.softmax(scores, axis=-1)
        ctx_c = jnp.einsum('bhsl,bld->bhsd', attn, kv_r)
        ctx_lat = jnp.einsum('bhsd,hkd->bhsk', ctx_c, w_kc_kv)
        ctx = ctx_lat.transpose(0, 2, 1, 3).reshape(Bv, Sv, H * K)
        return ctx @ Wo.T

    def _L2_ffn_ref(input, SU_ug, SU_dp, Wscale_ug, Wscale_dp, W_up, W_gate, W_down):
        import jax, jax.numpy as jnp
        import numpy as np
        HIDDEN = 256
        INTER = 1024
        SCALE = 64.0

        def fwht(x):
            orig_shape = x.shape
            n = orig_shape[-1]
            x = x.reshape(-1, n)
            h = 1
            while h < n:
                x = x.reshape(-1, n // (2 * h), 2, h)
                a, b = (x[:, :, 0, :], x[:, :, 1, :])
                x = jnp.stack([a + b, a - b], axis=2).reshape(-1, n)
                h *= 2
            return (x / jnp.sqrt(jnp.asarray(n, x.dtype))).reshape(orig_shape)
        n = SU_ug.shape[0]
        x = input.reshape(-1, n)
        x = fwht(x * SU_ug) / SCALE
        x_up = x @ W_up.T * (Wscale_ug[:INTER] * SCALE)
        x_gate = x @ W_gate.T * (Wscale_ug[INTER:] * SCALE)
        x = jax.nn.silu(x_gate) * x_up
        x = fwht(x * SU_dp) / SCALE
        x = x @ W_down.T * (Wscale_dp * SCALE)
        return x.reshape(input.shape)

    def _L3_xattn_ref(q, latent_kv, Wq, Wkv_expand, Wout):
        import jax, jax.numpy as jnp
        import numpy as np
        B, S, H, NH, L = (2, 256, 256, 16, 64)
        HD = H // NH
        b, sq, _ = q.shape
        sk = latent_kv.shape[1]
        qp = q @ Wq.T
        kv = latent_kv @ Wkv_expand.T
        k, v = jnp.split(kv, 2, axis=-1)
        qh = qp.reshape(b, sq, NH, HD).transpose(0, 2, 1, 3)
        kh = k.reshape(b, sk, NH, HD).transpose(0, 2, 1, 3)
        vh = v.reshape(b, sk, NH, HD).transpose(0, 2, 1, 3)
        inv_sqrt_d = 1.0 / jnp.sqrt(jnp.float32(HD))
        scores = jnp.einsum('bhqd,bhkd->bhqk', qh, kh) * inv_sqrt_d
        causal = jnp.tril(jnp.ones((sq, sk), dtype=bool))
        scores = jnp.where(causal, scores, jnp.finfo(scores.dtype).min)
        attn = jax.nn.softmax(scores, axis=-1)
        out = jnp.einsum('bhqk,bhkd->bhqd', attn, vh)
        out = out.transpose(0, 2, 1, 3).reshape(b, sq, H)
        return out @ Wout.T

    def _L3_ffn_ref(hidden_states, router_w, w_gate_up, w_down, shared_gate_up, shared_down):
        import jax, jax.numpy as jnp
        import numpy as np
        B, S, D, F, E, K = (2, 256, 256, 512, 8, 1)

        def _silu_mul(gu):
            g, u = jnp.split(gu, 2, axis=-1)
            return jax.nn.silu(g) * u

        def _moe_forward(hidden_states, router_w, w_gate_up, w_down, shared_gate_up, shared_down, top_k=K):
            b, s, d = hidden_states.shape
            x = hidden_states.reshape(-1, d)
            router_logits = x @ router_w.T
            topk_vals, topk_ids = jax.lax.top_k(router_logits, top_k)
            gate = jax.nn.sigmoid(topk_vals.astype(jnp.float32)).astype(x.dtype)
            xs = (x[:, None, :] * gate[:, :, None]).reshape(-1, d)
            ids_flat = topk_ids.reshape(-1)
            n_experts = w_gate_up.shape[0]

            def body(acc, inp):
                wg, wd, e = inp
                h = _silu_mul(xs @ wg)
                o = h @ wd
                mask = (ids_flat == e)[:, None]
                return (acc + jnp.where(mask, o, jnp.zeros((), o.dtype)), None)
            acc0 = jnp.zeros_like(xs)
            routed, _ = jax.lax.scan(body, acc0, (w_gate_up, w_down, jnp.arange(n_experts)))
            routed = routed.reshape(-1, top_k, d).sum(1)
            shared = _silu_mul(x @ shared_gate_up) @ shared_down
            return (routed + shared).reshape(b, s, d)
        return _moe_forward(hidden_states, router_w, w_gate_up, w_down, shared_gate_up, shared_down)
    x = x + jnp.tanh(g_xattn[0]) * _L0_xattn_ref(_layernorm(x, axis=-1), ctx_512, L0_xattn_Wq, L0_xattn_Wkv_expand, L0_xattn_Wout)
    x = x + jnp.tanh(g_ffn[0]) * _L0_ffn_ref(_layernorm(x, axis=-1), L0_ffn_router_weight, L0_ffn_router_bias, L0_ffn_expert_bias)
    x = x + jnp.tanh(g_xattn[1]) * _L1_xattn_ref(_layernorm(x, axis=-1), ctx_512, L1_xattn_Wq, L1_xattn_w_kc_q, L1_xattn_w_kc_kv, L1_xattn_W_qr, L1_xattn_W_kr, L1_xattn_Wo)
    x = x + jnp.tanh(g_ffn[1]) * _L1_ffn_ref(_layernorm(x, axis=-1), L1_ffn_w_gate, L1_ffn_w_up, L1_ffn_w_down)
    x = x + jnp.tanh(g_xattn[2]) * _L2_xattn_ref(_layernorm(x, axis=-1), ctx_512, L2_xattn_Wq, L2_xattn_w_kc_q, L2_xattn_w_kc_kv, L2_xattn_W_qr, L2_xattn_W_kr, L2_xattn_Wo)
    x = x + jnp.tanh(g_ffn[2]) * _L2_ffn_ref(_layernorm(x, axis=-1), L2_ffn_SU_ug, L2_ffn_SU_dp, L2_ffn_Wscale_ug, L2_ffn_Wscale_dp, L2_ffn_W_up, L2_ffn_W_gate, L2_ffn_W_down)
    x = x + jnp.tanh(g_xattn[3]) * _L3_xattn_ref(_layernorm(x, axis=-1), ctx_512, L3_xattn_Wq, L3_xattn_Wkv_expand, L3_xattn_Wout)
    x = x + jnp.tanh(g_ffn[3]) * _L3_ffn_ref(_layernorm(x, axis=-1), L3_ffn_router_w, L3_ffn_w_gate_up, L3_ffn_w_down, L3_ffn_shared_gate_up, L3_ffn_shared_down)
    return x

_drawn_inputs = setup_inputs


def setup_inputs(seed=0):
    import zlib

    import numpy as np

    out = dict(_drawn_inputs(seed))
    spreads = {'L0_ffn_router_bias': (0.0, 0.8)}
    factors = {'g_ffn': 8.0,
     'L0_xattn_Wq': 8.0,
     'L0_xattn_Wkv_expand': 3.528,
     'L0_xattn_Wout': 3.38,
     'L1_ffn_w_gate': 6.359,
     'L1_ffn_w_up': 6.374,
     'L1_ffn_w_down': 6.417,
     'L2_ffn_Wscale_ug': 5.144,
     'L2_ffn_Wscale_dp': 7.194,
     'L3_xattn_Wq': 8.0,
     'L3_ffn_router_w': 7.578,
     'L3_ffn_w_gate_up': 7.242,
     'L3_ffn_w_down': 7.281,
     'L3_ffn_shared_gate_up': 2.766,
     'L3_ffn_shared_down': 2.795}
    for name, (base, spread) in spreads.items():
        noise = np.random.default_rng([zlib.crc32(name.encode()), seed]).standard_normal(out[name].shape)
        drawn = base * np.exp(spread * noise) if base else spread * noise
        out[name] = jnp.asarray(drawn.astype(out[name].dtype))
    for name, factor in factors.items():
        out[name] = (out[name] * factor).astype(out[name].dtype)
    return out
```

```python
from contextlib import ExitStack

import numpy as np

import concourse.bass as bass
from concourse import mybir

F32 = mybir.dt.float32
F32R = mybir.dt.float32r
BF16 = mybir.dt.bfloat16
ACT = mybir.ActivationFunctionType
ALU = mybir.AluOpType
X = mybir.AxisListType.X

B, S, C = 16, 56, 256
T = B * S
TP = 2 * S
NT = T // TP
HALF = T // 2
CC = C // 128
LK, DC = 1500, 64
NH = 16
HP = NH // 2
HD = C // NH
SK = 64
KT, KP = 12, 125
DQ = 192
QT = NH * DQ // 128
HK = 128
FF = 1024
EPS = 1e-5
MASKED = -3.0e38
ROUND = 12582912.0


def constants():
    def tables(length, dim):
        inv = (1.0 / 10000.0 ** (np.arange(0, dim, 2, dtype=np.float32) / np.float32(dim))).astype(np.float32)
        f = np.arange(length, dtype=np.float32)[:, None] * inv[None, :]
        return np.repeat(np.cos(f), 2, -1).astype(np.float32), np.repeat(np.sin(f), 2, -1).astype(np.float32)

    def hadamard(n):
        h = np.ones((1, 1), np.float32)
        while h.shape[0] < n:
            h = np.block([[h, h], [h, -h]])
        return np.ascontiguousarray(h, np.float32)

    c = {"ident": np.eye(128, dtype=np.float32), "had256": hadamard(256), "had128": hadamard(128)}
    cos, sin = tables(LK, DC)
    signed = np.concatenate([-sin[:, :DC // 2], sin[:, DC // 2:]], 1)
    c["rope_k"] = np.stack([cos, signed]).reshape(2, KP, KT * DC)
    cos, sin = tables(S, DQ)
    i = np.arange(QT * 128) % DQ
    turned = np.where(i < DQ // 2, 1, -1).astype(np.float32) * sin[:, (i + DQ // 2) % DQ]
    c["rope_q"] = np.ascontiguousarray(
        np.stack([cos[:, i], turned])[:, :, :3 * 128].reshape(2, S, 3, 128).transpose(3, 0, 2, 1)).astype(np.float32)
    q, k = np.arange(128)[:, None] % 64, np.arange(SK)[None, :]
    c["causal"] = np.where(k <= q, 0.0, MASKED).astype(np.float32)
    c["headmask"] = (np.arange(128)[:, None] // HD == np.arange(8)[None, :]).astype(np.float32)
    c["lanes"] = (np.arange(48)[:, None] // 16 == np.arange(3)[None, :]).astype(np.float32)
    c["later"] = np.tile(np.arange(8, dtype=np.float32), (128, 1))
    return c


class Chain:

    def __init__(self, eng, sem):
        self.eng, self.sem, self.n = eng, sem, 0

    def __call__(self, ins):
        self.n += 1
        ins.then_inc(self.sem, 1)
        self.eng.wait_ge(self.sem, self.n)


class Alloc:
    def __init__(self, nc, ctx, stage):
        self.nc, self.ctx, self.stage = nc, ctx, stage

    def sb(self, name, shape, dt=F32):
        return self.ctx.enter_context(self.nc.sbuf_tensor(f"{self.stage}_{name}", shape, dt))

    def ps(self, name, shape, dt=F32):
        return self.ctx.enter_context(self.nc.psum_tensor(f"{self.stage}_{name}", shape, dt))

    def sem(self, name):
        s = self.nc.alloc_semaphore(f"{self.stage}_{name}")
        USED.append(s)
        return s


USED = []


def clear_semaphores(nc):
    nc.clear_and_free_semaphores(list(USED))
    USED.clear()
    nc.all_engine_barrier()


class Norm:

    def __init__(self, nc, a, g, turned=None):
        self.nc, self.g = nc, g
        self.stats = a.sb("ln_stats", [TP, NT, 6])
        self.mv = a.sb("ln_mv", [TP, NT, 2])
        self.std = a.sb("ln_std", [TP, NT])
        self.rstd = a.sb("ln_rstd", [TP, NT])
        self.shift = a.sb("ln_shift", [TP, NT])
        self.turned = turned or a.ps("ln_turned", [128, 2, 512])
        self.stats_done = a.sem("ln_stats_done")
        self.mv_ready = a.sem("ln_mv_ready")
        self.std_ready = a.sem("ln_std_ready")
        self.scale_ready = a.sem("ln_scale_ready")
        self.xn_ready = a.sem("ln_xn_ready")
        self.turned_ready = a.sem("ln_turned_ready")
        self.xnT_ready = a.sem("ln_xnT_ready")

    def vector(self, dve):
        g = self.g
        for t in range(NT):
            dve.bn_stats(self.stats[:, t, :], g.x[:, t, :]).then_inc(self.stats_done, 1)
        for t in range(NT):
            dve.wait_ge(self.stats_done, t + 1)
            dve.bn_aggr(self.mv[:, t, :], self.stats[:, t, :]).then_inc(self.mv_ready, 1)
        dve.wait_ge(self.std_ready, 1)
        dve.reciprocal(self.rstd[:, :], self.std[:, :]).then_inc(self.scale_ready, 1)
        dve.wait_ge(self.scale_ready, 1)
        dve.scalar_tensor_tensor(out=self.shift[:, :], in0=self.mv[:, :, 0], scalar=-1.0,
                                 in1=self.rstd[:, :], op0=ALU.mult, op1=ALU.mult).then_inc(self.scale_ready, 1)
        dve.wait_ge(self.scale_ready, 2)
        for t in range(NT):
            dve.tensor_scalar(g.xn[:, t, :], g.x[:, t, :], self.rstd[:, t:t + 1], self.shift[:, t:t + 1],
                              ALU.mult, ALU.add).then_inc(self.xn_ready, 1)

    def scalar(self, act):
        g = self.g
        act.wait_ge(self.mv_ready, NT)
        act.activation(self.std[:, :], self.mv[:, :, 1], ACT.Sqrt, bias=g.eps[0:TP, 0:1]).then_inc(self.std_ready, 1)
        for t in range(NT):
            act.wait_ge(self.turned_ready, t + 1)
            act.copy(g.xnT[:, :, t * TP:(t + 1) * TP],
                     self.turned[:, t % 2, 0:2 * TP].rearrange("p (c n) -> p c n", c=CC)).then_inc(self.xnT_ready, 1)

    def tensor(self, pe):
        g = self.g
        for t in range(NT):
            pe.wait_ge(self.xn_ready, t + 1)
            if t >= 2:
                pe.wait_ge(self.xnT_ready, t - 1)
            for c in range(CC):
                last = pe.transpose(self.turned[:, t % 2, c * TP:(c + 1) * TP],
                                    g.xn[:, t, c * 128:(c + 1) * 128], g.ident[0:TP, 0:TP])
            last.then_inc(self.turned_ready, 1)


def begin(nc, g, d):
    with ExitStack() as ctx:
        a = Alloc(nc, ctx, "begin")
        came = a.sem("came")
        set_ = a.sem("set")
        done = a.sem("done")
        raw = a.sb("gates_raw", [128, 8])
        with nc.Block() as block:

            @block.sync
            def _(sp):
                sp.dma_start(g.x[:, :, :], d["x"].rearrange("(t p) c -> p t c", p=TP)).then_inc(came, 16)
                sp.dma_start(g.ident[:, :], d["ident"]).then_inc(came, 16)
                sp.dma_start(raw[:, 0:4], d["g_xattn"].partition_broadcast(128)).then_inc(came, 16)
                sp.dma_start(raw[:, 4:8], d["g_ffn"].partition_broadcast(128)).then_inc(came, 16)

            @block.vector
            def _(dve):
                dve.memset(g.eps[:, :], EPS).then_inc(set_, 1)

            @block.scalar
            def _(act):
                act.wait_ge(came, 64)
                act.activation(g.gates[:, :], raw[:, :], ACT.Tanh).then_inc(done, 1)


def finish(nc, g, out):
    with ExitStack() as ctx:
        a = Alloc(nc, ctx, "finish")
        stored = a.sem("stored")
        with nc.Block() as block:

            @block.sync
            def _(sp):
                sp.dma_start(out.rearrange("(t p) c -> p t c", p=TP), g.x[:, :, :]).then_inc(stored, 16)
                sp.wait_ge(stored, 16)


def causal_attention(nc, g, d, layer, magnitudes=None):
    gate = g.gates[0:TP, layer:layer + 1]
    NP = B // 2
    with ExitStack() as ctx:
        a = Alloc(nc, ctx, f"xattn{layer}")
        wq = a.sb("wq", [128, CC, C])
        wkv = a.sb("wkv", [DC, 2 * C])
        wo = a.sb("wo", [128, CC, C])
        ctxT = a.sb("ctxT", [DC, B, 2, SK])
        causal = a.sb("causal", [128, SK])
        headmask = a.sb("headmask", [128, 8])
        kT = a.sb("kT", [128, CC, B, SK])
        values = a.sb("values", [128, B, HP, 2, HD])
        qT = a.sb("qT", [128, CC, T + 8])
        keys = a.sb("keys", [128, 4, 8, SK])
        sc = a.sb("scores", [128, 2, NH, SK])
        mx = a.sb("mx", [128, 2, NH])
        den = a.sb("den", [128, 2, NH])
        wT = a.sb("weightsT", [128, 2, HP, 128])
        oT = a.sb("outT", [128, CC, T])
        if magnitudes is not None:
            lanes = a.sb("lanes", [48, FF * C // 16])
            lanes_came = a.sem("lanes_came")
            lanes_summed = a.sem("lanes_summed")
        norm = Norm(nc, a, g)
        ps_a = a.ps("ps_a", [128, 2, 512])
        ps_t = a.ps("ps_t", [128, 2, 512])
        ps_o = a.ps("ps_o", [128, 512])
        ps_y = a.ps("ps_y", [128, 512])
        came = a.sem("came")
        zeroed = a.sem("zeroed")
        prod = a.sem("prod")
        taken = a.sem("taken")
        keys_ready = a.sem("keys_ready")
        scores_done = a.sem("scores_done")
        masked = a.sem("masked")
        shifted = a.sem("shifted")
        exp_done = a.sem("exp_done")
        weights_ready = a.sem("weights_ready")
        turned = a.sem("turned")
        wT_ready = a.sem("wT_ready")
        o_done = a.sem("o_done")
        o_taken = a.sem("o_taken")
        y_done = a.sem("y_done")
        x_done = a.sem("x_done")
        chain = a.sem("dve_chain")
        KV, VV, QQ = 4, 16, 4
        with nc.Block() as block:

            @block.sync
            def _(sp):
                sp.dma_start(wkv[:, :], d[f"L{layer}_kv"]).then_inc(came, 16)
                sp.dma_start(ctxT[:, :, :, :], d["ctx_first"].rearrange("d (b e k) -> d b e k", b=B, e=2)).then_inc(came, 16)
                sp.dma_start(wq[:, :, :], d[f"L{layer}_wq"].rearrange("(c p) n -> p c n", p=128)).then_inc(came, 16)
                sp.dma_start(wo[:, :, :], d[f"L{layer}_wo"].rearrange("(c p) n -> p c n", p=128)).then_inc(came, 16)
                sp.dma_start(causal[:, :], d["causal"]).then_inc(came, 16)
                sp.dma_start(headmask[:, :], d["headmask"]).then_inc(came, 16)
                if magnitudes is not None:
                    sp.dma_start(lanes[:, :], d["L1_lanes"]).then_inc(lanes_came, 16)

            @block.gpsimd
            def _(pool):
                pool.memset(values[:, :, :, :, :], 0.0).then_inc(zeroed, 1)
                pool.memset(qT[:, :, T:T + 8], 0.0).then_inc(zeroed, 1)
                pool.wait_ge(came, 96)
                pool.wait_ge(taken, KV)
                for n in range(2 * B):
                    b, c = n // 2, n % 2
                    if n >= 4:
                        pool.wait_ge(scores_done, (n - 4) // 4 + 1)
                    pool.tensor_tensor(keys[:, n % 4, :, :],
                                       kT[:, c, b, :].unsqueeze(1).to_broadcast([128, 8, SK]),
                                       headmask[:, :].unsqueeze(2).to_broadcast([128, 8, SK]),
                                       ALU.mult).then_inc(keys_ready, 1)

            @block.tensor
            def _(pe):
                pe.wait_ge(came, 96)
                n = 0
                for c in range(CC):
                    for h in range(2):
                        if n >= 2:
                            pe.wait_ge(taken, n - 1)
                        pe.matmul(ps_a[:, n % 2, :], wkv[:, c * 128:(c + 1) * 128],
                                  ctxT[:, 8 * h:8 * h + 8, 0, :], start=True, stop=True).then_inc(prod, 1)
                        n += 1
                for b in range(B):
                    pe.wait_ge(taken, n - 1)
                    pe.matmul(ps_a[:, n % 2, 0:C], ctxT[:, b, :, :], wkv[:, C:2 * C],
                              start=True, stop=True).then_inc(prod, 1)
                    n += 1
                norm.tensor(pe)
                pe.wait_ge(norm.xnT_ready, NT)
                for m in range(CC):
                    for h in range(2):
                        pe.wait_ge(taken, n - 1)
                        for c in range(CC):
                            last = pe.matmul(ps_a[:, n % 2, 0:HALF], wq[:, c, m * 128:(m + 1) * 128],
                                             g.xnT[:, c, h * HALF:(h + 1) * HALF], start=(c == 0), stop=(c == CC - 1))
                        last.then_inc(prod, 1)
                        n += 1
                pe.wait_ge(taken, n)
                pe.wait_ge(zeroed, 2)

                def scores(p):
                    pe.wait_ge(keys_ready, 4 * p + 4)
                    if p >= 1:
                        pe.wait_ge(masked, p)
                    for e in range(2):
                        b = 2 * p + e
                        for c in range(CC):
                            last = pe.matmul(ps_a[64 * e:64 * e + 64, c, :], qT[:, c, b * S:b * S + 64],
                                             keys[:, 2 * e + c, :, :], start=True, stop=True)
                    last.then_inc(scores_done, 1)

                def output(p):
                    pe.wait_ge(weights_ready, p + 1)
                    for j in range(HP):
                        if j % 4 == 0 and p >= 1:
                            pe.wait_ge(wT_ready, 2 * p)
                        last = pe.transpose(ps_t[:, j // 4, (j % 4) * 128:(j % 4) * 128 + 128],
                                            sc[:, p % 2, 2 * j:2 * j + 2, :], g.ident[:, :])
                        if j % 4 == 3:
                            last.then_inc(turned, 1)
                    pe.wait_ge(wT_ready, 2 * p + 2)
                    if p >= 1:
                        pe.wait_ge(o_taken, p)
                    for e in range(2):
                        for j in range(HP):
                            c, r = j // 4, 32 * (j % 4)
                            last = pe.matmul(ps_o[r:r + 32, c * 128 + e * 64:c * 128 + e * 64 + 64],
                                             values[:, 2 * p + e, j, :, :], wT[:, p % 2, j, e * 64:e * 64 + 64],
                                             start=True, stop=True, tile_position=(0, r))
                    last.then_inc(o_done, 1)

                def project(p):
                    pe.wait_ge(o_taken, p + 1)
                    if p >= 1:
                        pe.wait_ge(x_done, p)
                    for c in range(CC):
                        last = pe.matmul(ps_y[0:TP, 0:C], oT[:, c, p * TP:(p + 1) * TP], wo[:, c, :],
                                         start=(c == 0), stop=(c == CC - 1))
                    last.then_inc(y_done, 1)

                for p in range(NP + 2):
                    if p < NP:
                        scores(p)
                    if 1 <= p <= NP:
                        output(p - 1)
                    if p >= 2:
                        project(p - 2)

            @block.scalar
            def _(act):
                n = 0
                for c in range(CC):
                    for h in range(2):
                        act.wait_ge(prod, n + 1)
                        act.copy(kT[:, c, 8 * h:8 * h + 8, :],
                                 ps_a[:, n % 2, :].rearrange("p (b k) -> p b k", k=SK)).then_inc(taken, 1)
                        n += 1
                act.wait_ge(zeroed, 1)
                for b in range(B):
                    act.wait_ge(prod, n + 1)
                    v = ps_a[:, n % 2, 0:C].rearrange("p (j e k) -> p j e k", j=HP, e=2)
                    act.copy(values[0:64, b, :, 0, :], v[0:64, :, 0, :])
                    act.copy(values[64:128, b, :, 1, :], v[64:128, :, 1, :]).then_inc(taken, 1)
                    n += 1
                norm.scalar(act)
                for m in range(CC):
                    for h in range(2):
                        act.wait_ge(prod, n + 1)
                        act.mul(qT[:, m, h * HALF:(h + 1) * HALF], ps_a[:, n % 2, 0:HALF], HD ** -0.5).then_inc(taken, 1)
                        n += 1

                def exp(p):
                    act.wait_ge(shifted, p + 1)
                    act.activation(sc[:, p % 2, :, :], sc[:, p % 2, :, :], ACT.Exp).then_inc(exp_done, 1)

                def take(p):
                    for h in range(2):
                        act.wait_ge(turned, 2 * p + h + 1)
                        if p >= 2 and h == 0:
                            act.wait_ge(o_done, p - 1)
                        act.copy(wT[:, p % 2, 4 * h:4 * h + 4, :],
                                 ps_t[:, h, :].rearrange("p (j n) -> p j n", j=4)).then_inc(wT_ready, 1)
                    act.wait_ge(o_done, p + 1)
                    act.copy(oT[:, :, p * TP:(p + 1) * TP].rearrange("q c (e s) -> q c e s", e=2),
                             ps_o[:, 0:256].rearrange("q (c e s) -> q c e s", c=2, e=2)[:, :, :, 0:S]).then_inc(o_taken, 1)

                for p in range(NP + 1):
                    if p < NP:
                        exp(p)
                    if p >= 1:
                        take(p - 1)

            @block.vector
            def _(dve):
                norm.vector(dve)
                step = Chain(dve, chain)
                if magnitudes is not None:
                    dve.wait_ge(lanes_came, 16)
                    dve.tensor_reduce(magnitudes, lanes[:, :], X, ALU.add, apply_absolute_value=True).then_inc(lanes_summed, 1)

                def soft(p):
                    u = p % 2
                    dve.wait_ge(scores_done, p + 1)
                    if p >= 2:
                        dve.wait_ge(turned, 2 * p - 2)
                    ins = dve.tensor_tensor(sc[:, u, :, :], ps_a[:, :, :].rearrange("p c (h k) -> p (c h) k", k=SK),
                                            causal[:, :].unsqueeze(1).to_broadcast([128, NH, SK]), ALU.add)
                    ins.then_inc(masked, 1)
                    dve.wait_ge(masked, p + 1)
                    step(dve.tensor_reduce(mx[:, u, :], sc[:, u, :, :], X, ALU.max))
                    dve.tensor_tensor(sc[:, u, :, :], sc[:, u, :, :],
                                      mx[:, u, :].unsqueeze(2).to_broadcast([128, NH, SK]),
                                      ALU.subtract).then_inc(shifted, 1)

                def normalise(p):
                    u = p % 2
                    dve.wait_ge(exp_done, p + 1)
                    step(dve.tensor_reduce(den[:, u, :], sc[:, u, :, :], X, ALU.add))
                    step(dve.reciprocal(mx[:, u, :], den[:, u, :]))
                    dve.tensor_tensor(sc[:, u, :, :], sc[:, u, :, :],
                                      mx[:, u, :].unsqueeze(2).to_broadcast([128, NH, SK]),
                                      ALU.mult).then_inc(weights_ready, 1)

                def add(p):
                    dve.wait_ge(y_done, p + 1)
                    dve.scalar_tensor_tensor(out=g.x[:, p, :], in0=ps_y[0:TP, 0:C], scalar=gate, in1=g.x[:, p, :],
                                             op0=ALU.mult, op1=ALU.add).then_inc(x_done, 1)

                dve.wait_ge(came, 96)
                for p in range(NP + 2):
                    if p < NP:
                        soft(p)
                        normalise(p)
                    if p >= 2:
                        add(p - 2)


def top8_ffn(nc, g, d):
    E = 64
    gate = g.gates[0:TP, 4:5]
    with ExitStack() as ctx:
        a = Alloc(nc, ctx, "ffn0")
        rw = a.sb("rw", [128, CC, E])
        bias = a.sb("bias", [TP, E])
        eb = a.sb("eb", [E, C])
        e = a.sb("e", [TP, NT, E])
        rest = a.sb("rest", [TP, NT, E])
        m8 = a.sb("m8", [TP, NT, 8])
        mx = a.sb("mx", [TP, NT])
        den = a.sb("den", [TP, NT])
        top = a.sb("top", [TP, NT])
        wT = a.sb("wT", [E, NT, TP])
        y = a.sb("y", [TP, NT, C])
        norm = Norm(nc, a, g)
        ps_l = a.ps("ps_l", [128, 512])
        ps_t = a.ps("ps_t", [128, 2, 512])
        ps_y = a.ps("ps_y", [128, 2, 512])
        came = a.sem("came")
        logits = a.sem("logits")
        shifted = a.sem("shifted")
        exp_done = a.sem("exp_done")
        w_ready = a.sem("w_ready")
        turned = a.sem("turned")
        wT_ready = a.sem("wT_ready")
        y_done = a.sem("y_done")
        y_taken = a.sem("y_taken")
        chain = a.sem("dve_chain")
        with nc.Block() as block:

            @block.sync
            def _(sp):
                sp.dma_start(rw[:, :, :], d["L0_rw"].rearrange("(c p) n -> p c n", p=128)).then_inc(came, 16)
                sp.dma_start(bias[:, :], d["L0_rb"].partition_broadcast(TP)).then_inc(came, 16)
                sp.dma_start(eb[:, :], d["L0_eb"]).then_inc(came, 16)

            @block.tensor
            def _(pe):
                norm.tensor(pe)
                pe.wait_ge(came, 48)
                for t in range(NT):
                    pe.wait_ge(norm.xnT_ready, t + 1)
                    for c in range(CC):
                        last = pe.matmul(ps_l[0:TP, t * E:(t + 1) * E], g.xnT[:, c, t * TP:(t + 1) * TP], rw[:, c, :],
                                         start=(c == 0), stop=(c == CC - 1))
                last.then_inc(logits, 1)
                pe.wait_ge(w_ready, 1)
                for t in range(NT):
                    if t >= 2:
                        pe.wait_ge(wT_ready, t - 1)
                    pe.transpose(ps_t[0:E, t % 2, 0:TP], e[:, t, :], g.ident[0:TP, 0:TP]).then_inc(turned, 1)
                    pe.wait_ge(wT_ready, t + 1)
                    if t >= 2:
                        pe.wait_ge(y_taken, t - 1)
                    pe.matmul(ps_y[0:TP, t % 2, 0:C], wT[:, t, :], eb[:, :], start=True, stop=True).then_inc(y_done, 1)

            @block.scalar
            def _(act):
                norm.scalar(act)
                act.wait_ge(shifted, 1)
                act.activation(e[:, :, :], e[:, :, :], ACT.Exp).then_inc(exp_done, 1)
                for t in range(NT):
                    act.wait_ge(turned, t + 1)
                    act.copy(wT[:, t, :], ps_t[0:E, t % 2, 0:TP]).then_inc(wT_ready, 1)

            @block.vector
            def _(dve):
                norm.vector(dve)
                step = Chain(dve, chain)
                wide = lambda v: v.unsqueeze(2).to_broadcast([TP, NT, E])
                dve.wait_ge(came, 48)
                dve.wait_ge(logits, 1)
                step(dve.tensor_tensor(e[:, :, :], ps_l[0:TP, :].rearrange("p (t e) -> p t e", e=E),
                                       bias[:, :].unsqueeze(1).to_broadcast([TP, NT, E]), ALU.add))
                step(dve.tensor_reduce(mx[:, :], e[:, :, :], X, ALU.max))
                dve.tensor_tensor(e[:, :, :], e[:, :, :], wide(mx[:, :]), ALU.subtract).then_inc(shifted, 1)
                dve.wait_ge(exp_done, 1)
                step(dve.tensor_reduce(den[:, :], e[:, :, :], X, ALU.add))
                step(dve.reciprocal(mx[:, :], den[:, :]))
                for t in range(NT):
                    step(dve.max(m8[:, t, :], e[:, t, :]))
                    step(dve.match_replace(rest[:, t, :], m8[:, t, :], e[:, t, :], 0.0))
                step(dve.tensor_tensor(e[:, :, :], e[:, :, :], rest[:, :, :], ALU.subtract))
                dve.tensor_tensor(e[:, :, :], e[:, :, :], wide(mx[:, :]), ALU.mult).then_inc(w_ready, 1)
                step(dve.tensor_reduce(top[:, :], m8[:, :, :], X, ALU.add))
                step(dve.tensor_tensor(top[:, :], top[:, :], mx[:, :], ALU.mult))
                for t in range(NT):
                    dve.wait_ge(y_done, t + 1)
                    ins = dve.scalar_tensor_tensor(out=y[:, t, :], in0=g.xn[:, t, :], scalar=top[:, t:t + 1],
                                                   in1=ps_y[0:TP, t % 2, 0:C], op0=ALU.mult, op1=ALU.add)
                    ins.then_inc(y_taken, 1)
                    dve.wait_ge(y_taken, t + 1)
                    step(dve.scalar_tensor_tensor(out=g.x[:, t, :], in0=y[:, t, :], scalar=gate, in1=g.x[:, t, :],
                                                  op0=ALU.mult, op1=ALU.add))


def wait_from(eng, sem, value):
    if not (isinstance(value, int) and value <= 0):
        eng.wait_ge(sem, value)


def latent_outputs(a):
    return dict(ps=a.ps("ps_fold", [128, 2, 512]), folded=a.sem("folded"), taken=a.sem("folded_taken"))


def out_weights_tensor(pe, f, wkv, wo):
    for j in range(HP):
        if j >= 2:
            pe.wait_ge(f["taken"], j - 1)
        for e in range(2):
            last = pe.matmul(f["ps"][64 * e:64 * e + 64, j % 2, 0:C], wkv[:, 2 * j + e, :], wo[:, 2 * j + e, :],
                             start=True, stop=True)
        last.then_inc(f["folded"], 1)


def out_weights_scalar(act, f, fold):
    for j in range(HP):
        act.wait_ge(f["folded"], j + 1)
        act.copy(fold[:, j, :], f["ps"][:, j % 2, 0:C]).then_inc(f["taken"], 1)


def queries_plain(nc, g, d, q, fold):
    IC = DQ // 2
    with ExitStack() as ctx:
        a = Alloc(nc, ctx, "q1")
        wq = a.sb("wq", [128, NH, C])
        wcqT = a.sb("wcqT", [IC, 2, NH, HK])
        wqrT = a.sb("wqrT", [64, NH, DQ])
        wkrT = a.sb("wkrT", [64, NH, DC])
        wkv = a.sb("wkv", [128, NH, DC])
        wo = a.sb("wo", [128, NH, C])
        z = a.sb("z", [IC, 2, 2, 2, DC])
        y = a.sb("y", [128, 2, 2, DC])
        aw = a.sb("a", [128, HP, CC, 2, DC])
        norm = Norm(nc, a, g)
        f = latent_outputs(a)
        ps_z = a.ps("ps_z", [128, 512])
        ps_y = a.ps("ps_y", [128, 512])
        ps_q = a.ps("ps_q", [128, 2, 512])
        came, came_o = a.sem("came"), a.sem("came_o")
        z_done, z_ready, y_done, y_ready, a_done, a_ready, q_done, q_taken = (
            a.sem(n) for n in ("z_done", "z_ready", "y_done", "y_ready", "a_done", "a_ready", "q_done", "q_taken"))
        with nc.Block() as block:

            @block.sync
            def _(sp):
                sp.dma_start(wqrT[:, :, :], d["L1_wqrT"].rearrange("r (h i) -> r h i", h=NH)).then_inc(came, 16)
                sp.dma_start(wkrT[:, :, :], d["L1_wkrT"].rearrange("r (h e) -> r h e", h=NH)).then_inc(came, 16)
                sp.dma_start(wcqT[:, :, :, :], d["L1_wcqT"].rearrange("i (u h k) -> i u h k", u=2, h=NH)).then_inc(came, 16)
                sp.dma_start(wq[:, :, :], d["L1_wq"].rearrange("k (h n) -> k h n", h=NH)).then_inc(came, 16)
                sp.dma_start(wkv[:, :, :], d["L1_wkv"].rearrange("k (h n) -> k h n", h=NH)).then_inc(came_o, 16)
                sp.dma_start(wo[:, :, :], d["L1_wo"].rearrange("k (h n) -> k h n", h=NH)).then_inc(came_o, 16)

            @block.tensor
            def _(pe):
                pe.wait_ge(came, 64)
                for j in range(HP):
                    if j >= 1:
                        pe.wait_ge(z_ready, j)
                    for e in range(2):
                        for u in range(2):
                            at = (2 * e + u) * DC
                            last = pe.matmul(ps_z[0:IC, at:at + DC], wqrT[:, 2 * j + e, u * IC:(u + 1) * IC],
                                             wkrT[:, 2 * j + e, :], start=True, stop=True)
                    last.then_inc(z_done, 1)
                    pe.wait_ge(z_ready, j + 1)
                    if j >= 1:
                        pe.wait_ge(a_ready, j)
                    for e in range(2):
                        for u in range(2):
                            last = pe.matmul(ps_y[:, e * DC:(e + 1) * DC], wcqT[:, u, 2 * j + e, :], z[:, j % 2, e, u, :],
                                             start=(u == 0), stop=(u == 1))
                    last.then_inc(y_done, 1)
                    pe.wait_ge(y_ready, j + 1)
                    for c in range(CC):
                        for e in range(2):
                            at = 128 + (2 * c + e) * DC
                            last = pe.matmul(ps_y[:, at:at + DC], wq[:, 2 * j + e, c * 128:(c + 1) * 128],
                                             y[:, j % 2, e, :], start=True, stop=True)
                    last.then_inc(a_done, 1)
                pe.wait_ge(came_o, 32)
                out_weights_tensor(pe, f, wkv, wo)
                norm.tensor(pe)
                pe.wait_ge(norm.xnT_ready, NT)
                pe.wait_ge(a_ready, HP)
                n = 0
                for j in range(HP):
                    for h in range(2):
                        if n >= 2:
                            pe.wait_ge(q_taken, n - 1)
                        for c in range(CC):
                            last = pe.matmul(ps_q[:, n % 2, 0:HALF], aw[:, j, c, :, :], g.xnT[:, c, h * HALF:(h + 1) * HALF],
                                             start=(c == 0), stop=(c == CC - 1))
                        last.then_inc(q_done, 1)
                        n += 1

            @block.scalar
            def _(act):
                for j in range(HP):
                    act.wait_ge(z_done, j + 1)
                    if j >= 2:
                        act.wait_ge(y_done, j - 1)
                    act.copy(z[:, j % 2, :, :, :], ps_z[0:IC, 0:4 * DC].rearrange("p (e u n) -> p e u n", e=2, u=2)).then_inc(z_ready, 1)
                    act.wait_ge(y_done, j + 1)
                    act.copy(y[:, j % 2, :, :], ps_y[:, 0:2 * DC].rearrange("p (e n) -> p e n", e=2)).then_inc(y_ready, 1)
                    act.wait_ge(a_done, j + 1)
                    act.copy(aw[:, j, :, :, :], ps_y[:, 128:128 + 4 * DC].rearrange("p (c e n) -> p c e n", c=2, e=2)).then_inc(a_ready, 1)
                out_weights_scalar(act, f, fold)
                norm.scalar(act)
                for n in range(2 * HP):
                    j, h = n // 2, n % 2
                    act.wait_ge(q_done, n + 1)
                    act.copy(q[:, j, h * HALF:(h + 1) * HALF], ps_q[:, n % 2, 0:HALF]).then_inc(q_taken, 1)

            @block.vector
            def _(dve):
                norm.vector(dve)


def queries_roped(nc, g, d, q, fold):
    with ExitStack() as ctx:
        a = Alloc(nc, ctx, "q2")
        wq = a.sb("wq", [128, NH, C])
        wcq = a.sb("wcq", [128, NH, DQ])
        wqrT = a.sb("wqrT", [64, 2, NH, DQ])
        wkrT = a.sb("wkrT", [64, NH, DC])
        wkv = a.sb("wkv", [128, NH, DC])
        wo = a.sb("wo", [128, NH, C])
        rope = a.sb("rope", [128, 2, 3, S])
        G = a.sb("G", [128, CC, NH * DQ])
        z = a.sb("z", [128, HP, 3, 2, 2, DC])
        ur = a.sb("u_roped", [128, 2, 2, HALF])
        norm = Norm(nc, a, g)
        f = latent_outputs(a)
        ps_g = a.ps("ps_g", [128, 2, 512])
        ps_q = a.ps("ps_q", [128, 2, 512])
        came, came_o = a.sem("came"), a.sem("came_o")
        zeroed, z_done, z_ready, g_done, g_ready, u_done, u_ready, q_done, q_taken, u_used = (
            a.sem(n) for n in ("zeroed", "z_done", "z_ready", "g_done", "g_ready", "u_done", "u_ready", "q_done", "q_taken", "u_used"))
        with nc.Block() as block:

            @block.sync
            def _(sp):
                sp.dma_start(wqrT[:, :, :, :], d["L2_wqrT"].rearrange("r (v h i) -> r v h i", v=2, h=NH)).then_inc(came, 16)
                sp.dma_start(wkrT[:, :, :], d["L2_wkrT"].rearrange("r (h e) -> r h e", h=NH)).then_inc(came, 16)
                sp.dma_start(wcq[:, :, :], d["L2_wcq"].rearrange("k (h i) -> k h i", h=NH)).then_inc(came, 16)
                sp.dma_start(wq[:, :, :], d["L2_wq"].rearrange("k (h n) -> k h n", h=NH)).then_inc(came, 16)
                sp.dma_start(rope[:, :, :, :], d["rope_q"]).then_inc(came, 16)
                sp.dma_start(wkv[:, :, :], d["L2_wkv"].rearrange("k (h n) -> k h n", h=NH)).then_inc(came_o, 16)
                sp.dma_start(wo[:, :, :], d["L2_wo"].rearrange("k (h n) -> k h n", h=NH)).then_inc(came_o, 16)

            @block.gpsimd
            def _(pool):
                pool.memset(z[:, :, :, :, :, :], 0.0).then_inc(zeroed, 1)

            @block.tensor
            def _(pe):
                pe.wait_ge(came, 80)
                for j in range(HP):
                    if j >= 2:
                        pe.wait_ge(z_ready, j - 1)
                    for v in range(2):
                        for t, e, i0, i1, row in ((0, 0, 0, 128, 0), (1, 0, 128, 192, 0), (1, 1, 0, 64, 64), (2, 1, 64, 192, 0)):
                            at = (2 * t + v) * DC
                            last = pe.matmul(ps_g[row:row + i1 - i0, j % 2, at:at + DC], wqrT[:, v, 2 * j + e, i0:i1],
                                             wkrT[:, 2 * j + e, :], start=True, stop=True)
                    last.then_inc(z_done, 1)
                pe.wait_ge(z_ready, HP)
                for n in range(2 * NH):
                    h, c = n // 2, n % 2
                    if n >= 2:
                        pe.wait_ge(g_ready, n - 1)
                    pe.matmul(ps_g[:, n % 2, 0:DQ], wq[:, h, c * 128:(c + 1) * 128], wcq[:, h, :],
                              start=True, stop=True).then_inc(g_done, 1)
                pe.wait_ge(came_o, 32)
                out_weights_tensor(pe, f, wkv, wo)
                norm.tensor(pe)
                pe.wait_ge(norm.xnT_ready, NT)
                pe.wait_ge(g_ready, 2 * NH)

                def wide(n):
                    j, h, t = n // 6, n // 3 % 2, n % 3
                    if n >= 2:
                        pe.wait_ge(u_ready, 2 * n - 2)
                    for c in range(CC):
                        at = (3 * j + t) * 128
                        last = pe.matmul(ps_g[:, n % 2, 0:HALF], G[:, c, at:at + 128], g.xnT[:, c, h * HALF:(h + 1) * HALF],
                                         start=(c == 0), stop=(c == CC - 1))
                    last.then_inc(u_done, 1)

                def narrow(n):
                    j, h, t = n // 6, n // 3 % 2, n % 3
                    pe.wait_ge(u_ready, 2 * n + 2)
                    if t == 0 and n // 3 >= 2:
                        pe.wait_ge(q_taken, n // 3 - 1)
                    for v in range(2):
                        last = pe.matmul(ps_q[:, n // 3 % 2, 0:HALF], z[:, j, t, v, :, :], ur[:, n % 2, v, :],
                                         start=(t == 0 and v == 0), stop=(t == 2 and v == 1))
                    last.then_inc(u_used, 1)

                for n in range(6 * HP + 1):
                    if n < 6 * HP:
                        wide(n)
                    if n >= 1:
                        narrow(n - 1)

            @block.scalar
            def _(act):
                act.wait_ge(zeroed, 1)
                for j in range(HP):
                    act.wait_ge(z_done, j + 1)
                    src = ps_g[:, j % 2, 0:6 * DC].rearrange("p (t v n) -> p t v n", t=3, v=2)
                    act.copy(z[:, j, 0, :, 0, :], src[:, 0, :, :])
                    act.copy(z[:, j, 2, :, 1, :], src[:, 2, :, :])
                    act.copy(z[0:64, j, 1, :, 0, :], src[0:64, 1, :, :])
                    act.copy(z[64:128, j, 1, :, 1, :], src[64:128, 1, :, :]).then_inc(z_ready, 1)
                for n in range(2 * NH):
                    h, c = n // 2, n % 2
                    act.wait_ge(g_done, n + 1)
                    act.copy(G[:, c, h * DQ:(h + 1) * DQ], ps_g[:, n % 2, 0:DQ]).then_inc(g_ready, 1)
                out_weights_scalar(act, f, fold)
                norm.scalar(act)
                for n in range(2 * HP):
                    act.wait_ge(u_used, 3 * n + 3)
                    act.copy(q[:, n // 2, (n % 2) * HALF:(n % 2 + 1) * HALF], ps_q[:, n % 2, 0:HALF]).then_inc(q_taken, 1)

            @block.vector
            def _(dve):
                norm.vector(dve)
                dve.wait_ge(came, 80)
                for n in range(6 * HP):
                    dve.wait_ge(u_done, n + 1)
                    if n >= 2:
                        dve.wait_ge(u_used, n - 1)
                    for v in range(2):
                        dve.tensor_tensor(ur[:, n % 2, v, :].rearrange("p (b s) -> p b s", s=S),
                                          ps_g[:, n % 2, 0:HALF].rearrange("p (b s) -> p b s", s=S),
                                          rope[:, v, n % 3, :].unsqueeze(1).to_broadcast([128, B // 2, S]),
                                          ALU.mult).then_inc(u_ready, 1)


def latent_attention(nc, g, d, layer, q):
    G8 = NH * S
    GH = G8 // 2
    QTL = G8 // 128
    with ExitStack() as ctx:
        a = Alloc(nc, ctx, f"latent{layer}")
        rope = a.sb("rope", [KP, 2, KT, DC])
        raw = [a.sb(f"raw{u}", [KP, KT, DC]) for u in range(2)]
        turned_half = a.sb("turned_half", [KP, KT, DC])
        val = [a.sb(f"val{u}", [KP, KT, 128]) for u in range(2)]
        split = a.sb("split", [KP, KT, 128])
        kA = [a.sb(f"kA{u}", [128, LK], F32R) for u in range(2)]
        kB = [a.sb(f"kB{u}", [128, LK], F32R) for u in range(2)]
        qA = [a.sb(f"qA{u}", [128, G8], F32R) for u in range(2)]
        qB = [a.sb(f"qB{u}", [128, G8], F32R) for u in range(2)]
        w = [a.sb(f"w{u}", [KP, G8]) for u in range(2)]
        mx = a.sb("mx", [128, 2, QTL])
        osb = a.sb("osb", [128, G8])
        rec = a.sb("rec", [64, G8])
        psW = a.ps("psW", [128, 3, 512])
        psS = a.ps("psS", [128, 2, 512])
        psO = a.ps("psO", [128, 2, 512])
        raw_came = [a.sem(f"raw_came{u}") for u in range(2)]
        names = ("tables", "ones", "roped", "hi_ready", "split_ready", "k_turned", "kA_ready", "kB_ready", "qA_ready", "qB_ready",
                 "max_scores", "max_ready", "row_turned", "row_ready", "scores_done", "exp_done", "av_done",
                 "o_copied", "rec_ready", "o_ready", "pool_chain")
        (tables, ones, roped, hi_ready, split_ready, k_turned, kA_ready, kB_ready, qA_ready, qB_ready,
         max_scores, max_ready, row_turned, row_ready, scores_done, exp_done, av_done,
         o_copied, rec_ready, o_ready, pool_chain) = (a.sem(n) for n in names)

        def each_batch(eng, body):
            body(0, 0)
            body(1, 1)
            with eng.Fori(1, B // 2 - 1) as i:
                body(2 * i, 0)
                body(2 * i + 1, 1)
            body(B - 2, 0)
            body(B - 1, 1)

        with nc.Block() as block:

            @block.sync
            def _(sp):
                ctx_rows = d["ctx"].rearrange("b (p n) -> p b n", p=KP)

                def load(b, u):
                    wait_from(sp, roped, b - 1)
                    sp.dma_start(raw[u][:, :, :].rearrange("p t e -> p (t e)"),
                                 ctx_rows[:, bass.ds(b, 1), :].rearrange("p b n -> p (b n)")).then_inc(raw_came[u], 16)

                sp.dma_start(rope[:, :, :, :], d["rope_k"].rearrange("v p (t e) -> p v t e", t=KT)).then_inc(tables, 16)
                each_batch(sp, load)

            @block.gpsimd
            def _(pool):
                for u in range(2):
                    pool.memset(val[u][:, :, DC:128], 1.0).then_inc(ones, 1)
                pool.wait_ge(tables, 16)

                def rope_rows(b, u):
                    pool.wait_ge(raw_came[u], (b // 2 if isinstance(b, int) else (b - u) // 2) * 16 + 16)
                    wait_from(pool, av_done, b - 1)
                    wait_from(pool, split_ready, b)
                    v = val[u][:, :, 0:DC]
                    pool.tensor_tensor(v, raw[u][:, :, :], rope[:, 0, :, :], ALU.mult)
                    for lo, hi in ((0, 32), (32, 0)):
                        last = pool.tensor_tensor(turned_half[:, :, lo:lo + 32], raw[u][:, :, hi:hi + 32],
                                                  rope[:, 1, :, lo:lo + 32], ALU.mult)
                    last.then_inc(pool_chain, 1)
                    pool.wait_ge(pool_chain, b + 1)
                    pool.tensor_tensor(v, v, turned_half[:, :, :], ALU.add).then_inc(roped, 1)

                each_batch(pool, rope_rows)

            @block.tensor
            def _(pe):
                def turn_context(b, u):
                    pe.wait_ge(split_ready, b + 1)
                    wait_from(pe, row_ready, b)
                    for t in range(KT):
                        last = pe.transpose(psW[:, t // 4, (t % 4) * KP:(t % 4 + 1) * KP], split[:, t, :], g.ident[0:KP, 0:KP])
                    last.then_inc(k_turned, 1)

                def score_for_max(b, u, j):
                    if j == 0:
                        pe.wait_ge(kA_ready, b + 1)
                        pe.wait_ge(qA_ready, b + 1)
                    else:
                        pe.wait_ge(max_ready, b * QTL + j)
                    for m in range(3):
                        last = pe.matmul(psW[:, m, 0:500], qA[u][:, j * 128:(j + 1) * 128], kA[u][:, m * 500:(m + 1) * 500],
                                         start=True, stop=True)
                    last.then_inc(max_scores, 1)

                def turn_maxima(b, u):
                    pe.wait_ge(max_ready, b * QTL + QTL)
                    flat = psW[:, :, :].rearrange("p a n -> p (a n)")
                    for j in range(QTL):
                        last = pe.transpose(flat[0:1, j * 128:(j + 1) * 128], mx[:, u, j:j + 1], g.ident[:, :])
                    last.then_inc(row_turned, 1)

                def scores(b, u, t):
                    if t == 0:
                        pe.wait_ge(row_ready, b + 1)
                        pe.wait_ge(kB_ready, b + 1)
                        pe.wait_ge(qB_ready, b + 1)
                    wait_from(pe, exp_done, b * KT + t)
                    at = slice(t * KP, (t + 1) * KP)
                    for h in range(2):
                        pe.matmul(psS[0:KP, h, 0:GH], kA[u][:, at], qA[u][:, h * GH:(h + 1) * GH], start=True, stop=False)
                        last = pe.matmul(psS[0:KP, h, 0:GH], kB[u][:, at], qB[u][:, h * GH:(h + 1) * GH], start=False, stop=True)
                    last.then_inc(scores_done, 1)

                def attend(b, u, t):
                    pe.wait_ge(exp_done, b * KT + t + 1)
                    if t == 0:
                        wait_from(pe, o_copied, 2 * b)
                    for h in range(2):
                        last = pe.matmul(psO[:, h, 0:GH], val[u][:, t, :], w[t % 2][:, h * GH:(h + 1) * GH],
                                         start=(t == 0), stop=(t == KT - 1))
                    if t == KT - 1:
                        last.then_inc(av_done, 1)

                def batch(b, u):
                    ahead = not (isinstance(b, int) and b == B - 1)
                    for t in range(KT + 1):
                        if t < KT:
                            scores(b, u, t)
                        if t >= 1:
                            attend(b, u, t - 1)
                        if ahead and t == 1:
                            turn_context(b + 1, 1 - u)
                        if ahead and 3 <= t < 3 + QTL:
                            score_for_max(b + 1, 1 - u, t - 3)
                        if ahead and t == 11:
                            turn_maxima(b + 1, 1 - u)

                turn_context(0, 0)
                for j in range(QTL):
                    score_for_max(0, 0, j)
                turn_maxima(0, 0)
                each_batch(pe, batch)

            @block.scalar
            def _(act):
                def spread_queries(b, u):
                    wait_from(act, scores_done, (b - 1) * KT)
                    for e in range(2):
                        src = q[e * 64:e * 64 + 64, :, bass.ds(b * S, S)]
                        for r in range(2):
                            last = act.copy(qA[u][r * 64:r * 64 + 64, :].rearrange("p (j e s) -> p j e s", e=2, s=S)[:, :, e, :], src)
                    last.then_inc(qA_ready, 1)

                def take_context(b, u):
                    act.wait_ge(k_turned, b + 1)
                    act.copy(kA[u][:, :].rearrange("p (m n) -> p m n", m=3), psW[:, :, 0:500]).then_inc(kA_ready, 1)

                def take_maxima(b, u):
                    act.wait_ge(row_turned, b + 1)
                    act.wait_ge(ones, 6)
                    act.mul(qB[u][64:65, :], psW[:, :, :].rearrange("p a n -> p (a n)")[0:1, 0:G8], -1.0).then_inc(row_ready, 1)

                def exp(b, u, t):
                    act.wait_ge(scores_done, b * KT + t + 1)
                    if t == 0:
                        wait_from(act, av_done, b)
                    act.activation(w[t % 2][:, :].rearrange("p (h n) -> p h n", h=2), psS[0:KP, :, 0:GH],
                                   ACT.Exp).then_inc(exp_done, 1)

                def batch(b, u):
                    ahead = not (isinstance(b, int) and b == B - 1)
                    for t in range(KT):
                        exp(b, u, t)
                        if ahead and t == 0:
                            spread_queries(b + 1, 1 - u)
                        if ahead and t == 2:
                            take_context(b + 1, 1 - u)
                    if ahead:
                        take_maxima(b + 1, 1 - u)
                    act.wait_ge(av_done, b + 1)
                    wait_from(act, o_ready, 2 * b)
                    act.copy(osb[:, 0:GH], psO[:, 0, 0:GH]).then_inc(o_copied, 1)

                spread_queries(0, 0)
                take_context(0, 0)
                take_maxima(0, 0)
                each_batch(act, batch)

            @block.vector
            def _(dve):
                for u in range(2):
                    dve.memset(kB[u][64:128, :].bitcast(F32), 0.0).then_inc(ones, 1)
                    dve.memset(qB[u][64:128, :].bitcast(F32), 0.0).then_inc(ones, 1)
                dve.wait_ge(ones, 6)
                for u in range(2):
                    dve.memset(kB[u][64:65, :].bitcast(F32), 1.0).then_inc(ones, 1)

                def split_context(b, u):
                    dve.wait_ge(roped, b + 1)
                    wait_from(dve, k_turned, b)
                    v = val[u][:, :, 0:DC]
                    dve.tensor_copy(split[:, :, 0:DC].bitcast(F32R), v).then_inc(hi_ready, 1)
                    dve.wait_ge(hi_ready, b + 1)
                    dve.tensor_tensor(split[:, :, DC:128], v, split[:, :, 0:DC], ALU.subtract).then_inc(split_ready, 1)

                def split_queries(b, u):
                    dve.wait_ge(qA_ready, b + 1)
                    for e in range(2):
                        hi = qA[u][e * 64:e * 64 + 64, :].rearrange("p (j e s) -> p j e s", e=2, s=S)[:, :, e, :]
                        last = dve.tensor_tensor(qB[u][0:64, :].rearrange("p (j e s) -> p j e s", e=2, s=S)[:, :, e, :],
                                                 q[e * 64:e * 64 + 64, :, bass.ds(b * S, S)], hi.bitcast(F32), ALU.subtract)
                    last.then_inc(qB_ready, 1)

                def copy_keys(b, u):
                    dve.wait_ge(kA_ready, b + 1)
                    dve.tensor_copy(kB[u][0:64, :], kA[u][0:64, :].bitcast(F32)).then_inc(kB_ready, 1)

                def maximum(b, u, j):
                    dve.wait_ge(max_scores, b * QTL + j + 1)
                    dve.tensor_reduce(mx[:, u, j:j + 1], psW[:, :, 0:500], mybir.AxisListType.XY, ALU.max).then_inc(max_ready, 1)

                def prepare(b, u):
                    split_context(b, u)
                    split_queries(b, u)
                    copy_keys(b, u)
                    for j in range(QTL):
                        maximum(b, u, j)

                def attended(b, u):
                    dve.wait_ge(av_done, b + 1)
                    wait_from(dve, o_ready, 2 * b)
                    dve.tensor_copy(osb[:, GH:G8], psO[:, 1, 0:GH]).then_inc(o_copied, 1)
                    dve.wait_ge(o_copied, 2 * b + 2)
                    dve.reciprocal(rec[:, :], osb[64:128, :]).then_inc(rec_ready, 1)
                    dve.wait_ge(rec_ready, b + 1)
                    for e in range(2):
                        pick = lambda v: v.rearrange("p (j e s) -> p j e s", e=2, s=S)[:, :, e, :]
                        dve.tensor_tensor(q[e * 64:e * 64 + 64, :, bass.ds(b * S, S)], pick(osb[0:64, :]), pick(rec[:, :]),
                                          ALU.mult).then_inc(o_ready, 1)

                def batch(b, u):
                    if not (isinstance(b, int) and b == B - 1):
                        prepare(b + 1, 1 - u)
                    attended(b, u)

                prepare(0, 0)
                each_batch(dve, batch)


def latent_output(nc, g, layer, q, fold):
    gate = g.gates[0:TP, layer:layer + 1]
    with ExitStack() as ctx:
        a = Alloc(nc, ctx, f"out{layer}")
        ps = a.ps("ps", [128, 2, 512])
        y_done, x_done = a.sem("y_done"), a.sem("x_done")
        with nc.Block() as block:

            @block.tensor
            def _(pe):
                for t in range(NT):
                    if t >= 2:
                        pe.wait_ge(x_done, t - 1)
                    for j in range(HP):
                        last = pe.matmul(ps[0:TP, t % 2, 0:C], q[:, j, t * TP:(t + 1) * TP], fold[:, j, :],
                                         start=(j == 0), stop=(j == HP - 1))
                    last.then_inc(y_done, 1)

            @block.vector
            def _(dve):
                for t in range(NT):
                    dve.wait_ge(y_done, t + 1)
                    dve.scalar_tensor_tensor(out=g.x[:, t, :], in0=ps[0:TP, t % 2, 0:C], scalar=gate, in1=g.x[:, t, :],
                                             op0=ALU.mult, op1=ALU.add).then_inc(x_done, 1)


def latent_layer(nc, g, d, layer, queries):
    with ExitStack() as ctx:
        a = Alloc(nc, ctx, f"layer{layer}")
        q = a.sb("q", [128, HP, T])
        fold = a.sb("fold", [128, HP, C])
        queries(nc, g, d, q, fold)
        latent_attention(nc, g, d, layer, q)
        latent_output(nc, g, layer, q, fold)



def butterflies(eng, step, v, w):
    src, dst = v, w
    for h in (4, 2, 1):
        pick = lambda t, k: t.rearrange("p (a u h) n -> p u a h n", u=2, h=h)[:, k, :, :, :]
        for k, op in ((0, ALU.add), (1, ALU.subtract)):
            last = eng.tensor_tensor(pick(dst, k), pick(src, 0), pick(src, 1), op)
            step(last)
        src, dst = dst, src
    return src


def ternary_ffn(nc, g, d):
    gate = g.gates[0:TP, 5:6]
    NF = FF // 128
    with ExitStack() as ctx:
        a = Alloc(nc, ctx, "ffn1")
        wf = a.sb("wf", [128, 3, 2 * FF])
        wb = a.sb("wb", [128, 3, 2 * FF], BF16)
        had256 = a.sb("had256", [128, CC, C])
        had128 = a.sb("had128", [128, 128])
        identb = a.sb("identb", [128, 128], BF16)
        onesm = a.sb("onesm", [128, 128])
        part = a.sb("part", [48, 3])
        ws = a.sb("ws", [128, 3])
        rws = a.sb("rws", [128, 3])
        xh = a.sb("xh", [TP, NT, C])
        xq = a.sb("xq", [TP, NT, C], BF16)
        xqT = a.sb("xqT", [128, CC, T], BF16)
        sx = a.sb("sx", [TP, NT])
        rx = a.sb("rx", [TP, NT])
        su = a.sb("su", [TP, 2, NT])
        s2 = a.sb("s2", [TP, NT])
        r2 = a.sb("r2", [TP, NT])
        h = a.sb("h", [TP, 2, FF])
        h2 = a.sb("h2", [TP, 2, FF])
        hT = a.sb("hT", [128, NF, TP])
        yq = a.sb("yq", [TP, FF], BF16)
        yqT = a.sb("yqT", [128, NF, TP], BF16)
        ps_gu = a.ps("ps_gu", [128, 4, 512])
        ps_t = a.ps("ps_t", [128, 2, 512])
        ps_y = a.ps("ps_y", [128, 2, 512])
        norm = Norm(nc, a, g, ps_t)
        came, came_w = a.sem("came"), a.sem("came_w")
        (ready, sums, w_ready, xh_done, xh_taken, xq_ready, xq_turned, xqT_ready, gu_done, silu_done, h_ready,
         h_turned, hT_ready, y_done, yq_ready, yq_turned, yqT_ready, o_done, x_done, chain) = (
            a.sem(n) for n in ("ready", "sums", "w_ready", "xh_done", "xh_taken", "xq_ready", "xq_turned", "xqT_ready",
                               "gu_done", "silu_done", "h_ready", "h_turned", "hT_ready", "y_done", "yq_ready",
                               "yq_turned", "yqT_ready", "o_done", "x_done", "dve_chain"))
        with nc.Block() as block:

            @block.sync
            def _(sp):
                sp.dma_start(wf[:, 0, :].rearrange("p (c n) -> p c n", c=CC), d["L1_gate"].rearrange("(c p) n -> p c n", p=128)).then_inc(came_w, 16)
                sp.dma_start(wf[:, 1, :].rearrange("p (c n) -> p c n", c=CC), d["L1_up"].rearrange("(c p) n -> p c n", p=128)).then_inc(came_w, 16)
                sp.dma_start(wf[:, 2, :].rearrange("p (c n) -> p c n", c=NF), d["L1_down"].rearrange("(c p) n -> p c n", p=128)).then_inc(came_w, 16)
                sp.dma_start(had256[:, :, :], d["had256"].rearrange("(c p) n -> p c n", p=128)).then_inc(came, 16)
                sp.dma_start(had128[:, :], d["had128"]).then_inc(came, 16)
                sp.dma_start(part[:, :], d["lanes"]).then_inc(came, 16)

            @block.gpsimd
            def _(pool):
                pool.memset(onesm[:, :], 1.0).then_inc(ready, 1)
                pool.tensor_copy(identb[:, :], g.ident[:, :]).then_inc(ready, 1)

            @block.tensor
            def _(pe):
                pe.wait_ge(ready, 3)
                pe.matmul(ps_gu[:, 0, 0:3], onesm[0:48, :], part[:, :], start=True, stop=True).then_inc(sums, 1)
                norm.tensor(pe)
                pe.wait_ge(came, 48)
                for t in range(NT):
                    pe.wait_ge(norm.xnT_ready, t + 1)
                    if t >= 2:
                        pe.wait_ge(xh_taken, t - 1)
                    for c in range(CC):
                        last = pe.matmul(ps_y[0:TP, t % 2, 0:C], g.xnT[:, c, t * TP:(t + 1) * TP], had256[:, c, :],
                                         start=(c == 0), stop=(c == CC - 1))
                    last.then_inc(xh_done, 1)
                pe.wait_ge(xq_ready, 1)
                for t in range(NT):
                    if t >= 2:
                        pe.wait_ge(xqT_ready, t - 1)
                    tb = ps_t[:, t % 2, :].bitcast(BF16)
                    for c in range(CC):
                        last = pe.transpose(tb[:, c * TP:(c + 1) * TP], xq[:, t, c * 128:(c + 1) * 128], identb[0:TP, 0:TP])
                    last.then_inc(xq_turned, 1)
                pe.wait_ge(xqT_ready, NT)
                pe.wait_ge(w_ready, 2)

                def inner(t):
                    if t >= 1:
                        pe.wait_ge(h_ready, t)
                    for m in range(2):
                        for n in range(2):
                            for c in range(CC):
                                last = pe.matmul(ps_gu[0:TP, 2 * m + n, :], xqT[:, c, t * TP:(t + 1) * TP],
                                                 wb[:, m, c * FF + n * 512:c * FF + n * 512 + 512],
                                                 start=(c == 0), stop=(c == CC - 1))
                    last.then_inc(gu_done, 1)

                def rotate(t):
                    pe.wait_ge(h_ready, t + 1)
                    if t >= 1:
                        pe.wait_ge(yqT_ready, t)
                    for k in range(NF):
                        last = pe.transpose(ps_t[:, k // 4, (k % 4) * TP:(k % 4 + 1) * TP], h2[:, t % 2, k * 128:(k + 1) * 128],
                                            g.ident[0:TP, 0:TP])
                    last.then_inc(h_turned, 1)
                    pe.wait_ge(hT_ready, t + 1)
                    if t >= 1:
                        pe.wait_ge(x_done, t)
                    for k in range(NF):
                        last = pe.matmul(ps_y[0:TP, k // 4, (k % 4) * 128:(k % 4 + 1) * 128], hT[:, k, :], had128[:, :],
                                         start=True, stop=True)
                    last.then_inc(y_done, 1)

                def down(t):
                    pe.wait_ge(yq_ready, t + 1)
                    tb = ps_t[:, 0, :].bitcast(BF16)
                    for k in range(NF):
                        last = pe.transpose(tb[:, k * TP:(k + 1) * TP], yq[:, k * 128:(k + 1) * 128], identb[0:TP, 0:TP])
                    last.then_inc(yq_turned, 1)
                    pe.wait_ge(yqT_ready, t + 1)
                    for k in range(NF):
                        last = pe.matmul(ps_y[0:TP, 0, 0:C], yqT[:, k, :], wb[:, 2, k * C:(k + 1) * C],
                                         start=(k == 0), stop=(k == NF - 1))
                    last.then_inc(o_done, 1)

                inner(0)
                for t in range(NT):
                    if t + 1 < NT:
                        inner(t + 1)
                    rotate(t)
                    if t == 0:
                        pe.wait_ge(w_ready, 3)
                    down(t)

            @block.scalar
            def _(act):
                norm.scalar(act)
                for t in range(NT):
                    act.wait_ge(xh_done, t + 1)
                    act.copy(xh[:, t, :], ps_y[0:TP, t % 2, 0:C]).then_inc(xh_taken, 1)
                for t in range(NT):
                    act.wait_ge(xq_turned, t + 1)
                    act.copy(xqT[:, :, t * TP:(t + 1) * TP],
                             ps_t[:, t % 2, :].bitcast(BF16)[:, 0:2 * TP].rearrange("p (c n) -> p c n", c=CC)).then_inc(xqT_ready, 1)

                def silu(t):
                    act.wait_ge(gu_done, t + 1)
                    if t >= 2:
                        act.wait_ge(h_ready, t - 1)
                    act.activation(h[:, t % 2, :].rearrange("p (n m) -> p n m", n=2), ps_gu[0:TP, 0:2, :], ACT.Silu,
                                   scale=su[:, 0, t:t + 1]).then_inc(silu_done, 1)

                act.wait_ge(w_ready, 2)
                silu(0)
                for t in range(NT):
                    if t + 1 < NT:
                        silu(t + 1)
                    act.wait_ge(h_turned, t + 1)
                    act.copy(hT[:, :, :].rearrange("p (u k) n -> p u (k n)", u=2), ps_t[:, :, 0:4 * TP]).then_inc(hT_ready, 1)
                    act.wait_ge(yq_turned, t + 1)
                    act.copy(yqT[:, :, :].rearrange("p k n -> p (k n)"), ps_t[:, 0, :].bitcast(BF16)[:, 0:NF * TP]).then_inc(yqT_ready, 1)

            @block.vector
            def _(dve):
                step = Chain(dve, chain)
                norm.vector(dve)
                dve.wait_ge(came_w, 48)
                dve.wait_ge(came, 48)
                dve.tensor_scalar(part[:, :], part[:, :], g.magnitudes[:, :], None, ALU.mult).then_inc(ready, 1)
                dve.wait_ge(sums, 1)
                step(dve.tensor_scalar(ws[:, :], ps_gu[:, 0, 0:3], 1.0 / (FF * C), 1e-5, ALU.mult, ALU.max))
                step(dve.reciprocal(rws[:, :], ws[:, :]))

                def quantise_weights(m):
                    step(dve.tensor_scalar(wf[:, m, :], wf[:, m, :], rws[:, m:m + 1], 1.0, ALU.mult, ALU.min))
                    step(dve.tensor_scalar(wf[:, m, :], wf[:, m, :], -1.0, ROUND, ALU.max, ALU.add))
                    dve.tensor_scalar(wb[:, m, :], wf[:, m, :], -ROUND, None, ALU.add).then_inc(w_ready, 1)

                def quantise_scales(s, r, most, root):
                    step(dve.tensor_scalar(s, most, 1.0 / root, 1e-5, ALU.mult, ALU.max))
                    step(dve.reciprocal(r, s))
                    step(dve.tensor_scalar(r, r, 127.0, 1.0 / root, ALU.mult, ALU.mult))
                    step(dve.tensor_scalar(s, s, 1.0 / 127.0, None, ALU.mult))

                dve.wait_ge(xh_taken, NT)
                step(dve.tensor_reduce(rx[:, :], xh[:, :, :], X, ALU.max, apply_absolute_value=True))
                quantise_scales(sx[:, :], rx[:, :], rx[:, :], 16.0)
                step(dve.tensor_tensor(xh[:, :, :], xh[:, :, :], rx[:, :].unsqueeze(2).to_broadcast([TP, NT, C]), ALU.mult))
                step(dve.tensor_scalar(xh[:, :, :], xh[:, :, :], 127.0, -128.0, ALU.min, ALU.max))
                dve.tensor_scalar(xq[:, :, :], xh[:, :, :], ROUND, -ROUND, ALU.add, ALU.add).then_inc(xq_ready, 1)
                for m in range(2):
                    step(dve.tensor_scalar(su[:, m, :], sx[:, :], ws[0:TP, m:m + 1], None, ALU.mult))
                quantise_weights(0)
                quantise_weights(1)
                step(dve.tensor_scalar(ws[:, 2:3], ws[:, 2:3], g.gates[:, 5:6], None, ALU.mult))

                def product(t):
                    u = t % 2
                    dve.wait_ge(silu_done, t + 1)
                    step(dve.scalar_tensor_tensor(out=h[:, u, :].rearrange("p (n m) -> p n m", n=2), in0=ps_gu[0:TP, 2:4, :],
                                                  scalar=su[:, 1, t:t + 1], in1=h[:, u, :].rearrange("p (n m) -> p n m", n=2),
                                                  op0=ALU.mult, op1=ALU.mult))
                    if t >= 2:
                        dve.wait_ge(h_turned, t - 1)
                    v, w = (z[:, u, :].rearrange("p (k n) -> p k n", n=128) for z in (h, h2))
                    butterflies(dve, step, v, w)
                    dve.tensor_copy(ws[0:1, 0:1], ws[0:1, 0:1]).then_inc(h_ready, 1)
                    dve.wait_ge(h_ready, t + 1)

                def quantise(t):
                    at = slice(t, t + 1)
                    dve.wait_ge(y_done, t + 1)
                    step(dve.tensor_reduce(r2[:, at], ps_y[0:TP, :, :], mybir.AxisListType.XY, ALU.max, apply_absolute_value=True))
                    quantise_scales(s2[:, at], r2[:, at], r2[:, at], 32.0)
                    step(dve.tensor_scalar(s2[:, at], s2[:, at], ws[0:TP, 2:3], None, ALU.mult))
                    wide = xh[:, 0:4, :].rearrange("p a n -> p (a n)")
                    step(dve.tensor_scalar(wide.rearrange("p (a n) -> p a n", a=2), ps_y[0:TP, :, :], r2[:, at], 127.0, ALU.mult, ALU.min))
                    step(dve.tensor_scalar(wide, wide, -128.0, ROUND, ALU.max, ALU.add))
                    if t >= 1:
                        dve.wait_ge(yq_turned, t)
                    dve.tensor_scalar(yq[:, :], wide, -ROUND, None, ALU.add).then_inc(yq_ready, 1)

                def add(t):
                    dve.wait_ge(o_done, t + 1)
                    dve.scalar_tensor_tensor(out=g.x[:, t, :], in0=ps_y[0:TP, 0, 0:C], scalar=s2[:, t:t + 1], in1=g.x[:, t, :],
                                             op0=ALU.mult, op1=ALU.add).then_inc(x_done, 1)

                dve.wait_ge(w_ready, 2)
                product(0)
                for t in range(NT):
                    if t + 1 < NT:
                        product(t + 1)
                    if t == 0:
                        quantise_weights(2)
                    quantise(t)
                    add(t)


def hadamard_ffn(nc, g, d):
    gate = g.gates[0:TP, 6:7]
    NF = FF // 128
    with ExitStack() as ctx:
        a = Alloc(nc, ctx, "ffn2")
        had256 = a.sb("had256", [128, CC, C])
        had128 = a.sb("had128", [128, 128])
        su_ug = a.sb("su_ug", [128, CC])
        su_dp = a.sb("su_dp", [128, NF])
        sc_ug = a.sb("sc_ug", [128, 2 * NF])
        sc_dp = a.sb("sc_dp", [128, C])
        wu = a.sb("wu", [128, CC, FF])
        wg = a.sb("wg", [128, CC, FF])
        wd = a.sb("wd", [128, NF, C])
        wd2 = a.sb("wd2", [128, NF, C])
        xr = a.sb("xr", [128, CC, T])
        s = a.sb("s", [128, 2, HALF])
        hT = a.sb("hT", [128, NF, T])
        ps_u = a.ps("ps_u", [128, 2, 512])
        ps_g = a.ps("ps_g", [128, 2, 512])
        ps_d = a.ps("ps_d", [128, 2, 512])
        norm = Norm(nc, a, g)
        came = a.sem("came")
        (had_ready, wd_ready, fold_done, fold_ready, xr_done, xr_ready, u_done, g_done, s_ready, h_ready, y_done, x_done,
         pool_chain, chain) = (a.sem(n) for n in ("had_ready", "wd_ready", "fold_done", "fold_ready", "xr_done", "xr_ready",
                                                  "u_done", "g_done", "s_ready", "h_ready", "y_done", "x_done", "pool_chain", "dve_chain"))
        with nc.Block() as block:

            @block.sync
            def _(sp):
                chunks = lambda v: v.rearrange("(c p) n -> p c n", p=128)
                for dst, src in ((wd[:, :, :], chunks(d["L2_down"])), (had128[:, :], d["had128"]), (had256[:, :, :], chunks(d["had256"])),
                                 (su_ug[:, :], d["L2_su_ug"]), (su_dp[:, :], d["L2_su_dp"]), (sc_ug[:, :], d["L2_sc_ug"]),
                                 (sc_dp[:, :], d["L2_sc_dp"].partition_broadcast(128)),
                                 (wu[:, :, :], chunks(d["L2_up"])), (wg[:, :, :], chunks(d["L2_gate"]))):
                    sp.dma_start(dst, src).then_inc(came, 16)

            @block.gpsimd
            def _(pool):
                pool.wait_ge(came, 144)
                got = butterflies(pool, Chain(pool, pool_chain), wd[:, :, :], wd2[:, :, :])
                pool.memset(s[:, :, :], 0.0).then_inc(wd_ready, 1)

            @block.tensor
            def _(pe):
                pe.wait_ge(wd_ready, 1)
                for k in range(NF):
                    if k >= 2:
                        pe.wait_ge(fold_ready, k - 1)
                    pe.matmul(ps_d[:, k % 2, 0:C], had128[:, :], wd2[:, k, :], start=True, stop=True).then_inc(fold_done, 1)
                norm.tensor(pe)
                pe.wait_ge(norm.xnT_ready, NT)
                pe.wait_ge(had_ready, CC)
                for n in range(4):
                    m, h = n // 2, n % 2
                    if n >= 2:
                        pe.wait_ge(xr_ready, n - 1)
                    for c in range(CC):
                        last = pe.matmul(ps_u[:, n % 2, 0:HALF], had256[:, c, m * 128:(m + 1) * 128],
                                         g.xnT[:, c, h * HALF:(h + 1) * HALF], start=(c == 0), stop=(c == CC - 1))
                    last.then_inc(xr_done, 1)
                pe.wait_ge(xr_ready, 4)
                for n in range(2 * NF):
                    m, h = n // 2, n % 2
                    if n >= 2:
                        pe.wait_ge(h_ready, n - 1)
                    for w, ps, done in ((wg, ps_g, g_done), (wu, ps_u, u_done)):
                        for c in range(CC):
                            last = pe.matmul(ps[:, n % 2, 0:HALF], w[:, c, m * 128:(m + 1) * 128],
                                             xr[:, c, h * HALF:(h + 1) * HALF], start=(c == 0), stop=(c == CC - 1))
                        last.then_inc(done, 1)
                pe.wait_ge(fold_ready, NF)
                pe.wait_ge(h_ready, 2 * NF)
                for t in range(NT):
                    if t >= 2:
                        pe.wait_ge(x_done, t - 1)
                    for k in range(NF):
                        last = pe.matmul(ps_d[0:TP, t % 2, 0:C], hT[:, k, t * TP:(t + 1) * TP], wd[:, k, :],
                                         start=(k == 0), stop=(k == NF - 1))
                    last.then_inc(y_done, 1)

            @block.scalar
            def _(act):
                norm.scalar(act)
                for n in range(4):
                    m, h = n // 2, n % 2
                    act.wait_ge(xr_done, n + 1)
                    act.copy(xr[:, m, h * HALF:(h + 1) * HALF], ps_u[:, n % 2, 0:HALF]).then_inc(xr_ready, 1)
                act.wait_ge(had_ready, CC + 2)
                for n in range(2 * NF):
                    act.wait_ge(g_done, n + 1)
                    if n >= 2:
                        act.wait_ge(h_ready, n - 1)
                    act.activation(s[:, n % 2, :], ps_g[:, n % 2, 0:HALF], ACT.Silu, scale=sc_ug[:, NF + n // 2:NF + n // 2 + 1]).then_inc(s_ready, 1)

            @block.vector
            def _(dve):
                step = Chain(dve, chain)
                dve.wait_ge(came, 144)
                for c in range(CC):
                    dve.tensor_scalar(had256[:, c, :], had256[:, c, :], su_ug[:, c:c + 1], None, ALU.mult).then_inc(had_ready, 1)
                step(dve.tensor_scalar(sc_ug[:, :], sc_ug[:, :], 1.0 / 16.0, None, ALU.mult))
                dve.tensor_tensor(sc_ug[:, 0:NF], sc_ug[:, 0:NF], su_dp[:, :], ALU.mult).then_inc(had_ready, 1)
                dve.tensor_scalar(sc_dp[:, :], sc_dp[:, :], 1.0 / 32.0, None, ALU.mult).then_inc(had_ready, 1)
                dve.wait_ge(had_ready, CC + 2)
                for k in range(NF):
                    dve.wait_ge(fold_done, k + 1)
                    dve.tensor_tensor(wd[:, k, :], ps_d[:, k % 2, 0:C], sc_dp[:, :], ALU.mult).then_inc(fold_ready, 1)
                norm.vector(dve)
                dve.wait_ge(wd_ready, 1)
                for n in range(2 * NF):
                    m, h = n // 2, n % 2
                    dve.wait_ge(s_ready, n + 1)
                    dve.wait_ge(u_done, n + 1)
                    dve.scalar_tensor_tensor(out=hT[:, m, h * HALF:(h + 1) * HALF], in0=ps_u[:, n % 2, 0:HALF], scalar=sc_ug[:, m:m + 1],
                                             in1=s[:, n % 2, :], op0=ALU.mult, op1=ALU.mult).then_inc(h_ready, 1)
                for t in range(NT):
                    dve.wait_ge(y_done, t + 1)
                    dve.scalar_tensor_tensor(out=g.x[:, t, :], in0=ps_d[0:TP, t % 2, 0:C], scalar=gate, in1=g.x[:, t, :],
                                             op0=ALU.mult, op1=ALU.add).then_inc(x_done, 1)


def experts_ffn(nc, g, d):
    NE, F4 = 8, 4
    with ExitStack() as ctx:
        a = Alloc(nc, ctx, "ffn3")
        rw = a.sb("rw", [128, CC, NE])
        later = a.sb("later", [128, NE])
        lg = a.sb("lg", [TP, NT, NE])
        eq = a.sb("eq", [TP, NT, NE])
        top = a.sb("top", [TP, NT])
        first = a.sb("first", [TP, NT])
        coef = a.sb("coef", [TP, NT, NE])
        sg = a.sb("sg", [TP, NT])
        xsT = a.sb("xsT", [128, CC, T])
        wgu = a.sb("wgu", [128, 2, CC, FF])
        wdn = a.sb("wdn", [128, 2, F4, C])
        s = a.sb("s", [128, 2, HALF])
        hT = a.sb("hT", [128, F4, T])
        ps_l = a.ps("ps_l", [128, 512])
        ps_u = a.ps("ps_u", [128, 2, 512])
        ps_g = a.ps("ps_g", [128, 2, 512])
        ps_d = a.ps("ps_d", [128, 512])
        norm = Norm(nc, a, g)
        came = a.sem("came")
        w_came = [a.sem(f"w_came{u}") for u in range(2)]
        (l_done, top_ready, sg_ready, xs_ready, xs_turned, xsT_ready, g_done, u_done, s_ready, h_ready, y_done, x_done, chain) = (
            a.sem(n) for n in ("l_done", "top_ready", "sg_ready", "xs_ready", "xs_turned", "xsT_ready", "g_done", "u_done",
                               "s_ready", "h_ready", "y_done", "x_done", "dve_chain"))
        NN = NE + 1
        with nc.Block() as block:

            @block.sync
            def _(sp):
                sp.dma_start(rw[:, :, :], d["L3_rw"].rearrange("(c p) n -> p c n", p=128)).then_inc(came, 16)
                sp.dma_start(later[:, :], d["later"]).then_inc(came, 16)
                for e in range(NN):
                    if e >= 2:
                        sp.wait_ge(y_done, (e - 1) * NT)
                    gu = d["L3_gu"][e] if e < NE else d["L3_sgu"]
                    dn = d["L3_dn"][e] if e < NE else d["L3_sdn"]
                    sp.dma_start(wgu[:, e % 2, :, :], gu.rearrange("(c p) n -> p c n", p=128)).then_inc(w_came[e % 2], 16)
                    sp.dma_start(wdn[:, e % 2, :, :], dn.rearrange("(c p) n -> p c n", p=128)).then_inc(w_came[e % 2], 16)

            @block.tensor
            def _(pe):
                norm.tensor(pe)
                pe.wait_ge(came, 32)
                for t in range(NT):
                    pe.wait_ge(norm.xnT_ready, t + 1)
                    for c in range(CC):
                        last = pe.matmul(ps_l[0:TP, t * NE:(t + 1) * NE], g.xnT[:, c, t * TP:(t + 1) * TP], rw[:, c, :],
                                         start=(c == 0), stop=(c == CC - 1))
                last.then_inc(l_done, 1)
                for t in range(NT):
                    pe.wait_ge(xs_ready, t + 1)
                    if t >= 2:
                        pe.wait_ge(xsT_ready, t - 1)
                    for c in range(CC):
                        last = pe.transpose(norm.turned[:, t % 2, c * TP:(c + 1) * TP], g.xn[:, t, c * 128:(c + 1) * 128],
                                            g.ident[0:TP, 0:TP])
                    last.then_inc(xs_turned, 1)
                pe.wait_ge(xsT_ready, NT)
                n = 0
                for e in range(NN):
                    xT = xsT if e < NE else g.xnT
                    pe.wait_ge(w_came[e % 2], 32 * (e // 2 + 1))
                    for m in range(F4):
                        for h in range(2):
                            if n >= 2:
                                pe.wait_ge(h_ready, n - 1)
                            for off, ps, done in ((0, ps_g, g_done), (FF // 2, ps_u, u_done)):
                                for c in range(CC):
                                    last = pe.matmul(ps[:, n % 2, 0:HALF], wgu[:, e % 2, c, off + m * 128:off + (m + 1) * 128],
                                                     xT[:, c, h * HALF:(h + 1) * HALF], start=(c == 0), stop=(c == CC - 1))
                                last.then_inc(done, 1)
                            n += 1
                    pe.wait_ge(h_ready, n)
                    for t in range(NT):
                        wait_from(pe, x_done, e * NT + t)
                        for k in range(F4):
                            last = pe.matmul(ps_d[0:TP, 0:C], hT[:, k, t * TP:(t + 1) * TP], wdn[:, e % 2, k, :],
                                             start=(k == 0), stop=(k == F4 - 1))
                        last.then_inc(y_done, 1)

            @block.scalar
            def _(act):
                norm.scalar(act)
                act.wait_ge(top_ready, 1)
                act.activation(sg[:, :], top[:, :], ACT.Sigmoid).then_inc(sg_ready, 1)
                for t in range(NT):
                    act.wait_ge(xs_turned, t + 1)
                    act.copy(xsT[:, :, t * TP:(t + 1) * TP], norm.turned[:, t % 2, 0:2 * TP].rearrange("p (c n) -> p c n", c=CC)).then_inc(xsT_ready, 1)
                for n in range(2 * F4 * NN):
                    act.wait_ge(g_done, n + 1)
                    if n >= 2:
                        act.wait_ge(h_ready, n - 1)
                    act.activation(s[:, n % 2, :], ps_g[:, n % 2, 0:HALF], ACT.Silu).then_inc(s_ready, 1)

            @block.vector
            def _(dve):
                step = Chain(dve, chain)
                norm.vector(dve)
                dve.wait_ge(came, 32)
                dve.wait_ge(l_done, 1)
                wide = lambda v: v.unsqueeze(2).to_broadcast([TP, NT, NE])
                lat = later[0:TP, :].unsqueeze(1).to_broadcast([TP, NT, NE])
                step(dve.tensor_copy(lg[:, :, :], ps_l[0:TP, 0:NT * NE].rearrange("p (t e) -> p t e", e=NE)))
                dve.tensor_reduce(top[:, :], lg[:, :, :], X, ALU.max).then_inc(top_ready, 1)
                dve.wait_ge(top_ready, 1)
                step(dve.tensor_tensor(eq[:, :, :], lg[:, :, :], wide(top[:, :]), ALU.is_lt))
                step(dve.scalar_tensor_tensor(out=eq[:, :, :], in0=eq[:, :, :], scalar=float(NE), in1=lat, op0=ALU.mult, op1=ALU.add))
                step(dve.tensor_reduce(first[:, :], eq[:, :, :], X, ALU.min))
                step(dve.tensor_tensor(coef[:, :, :], lat, wide(first[:, :]), ALU.is_equal))
                step(dve.tensor_scalar(coef[:, :, :], coef[:, :, :], g.gates[0:TP, 7:8], None, ALU.mult))
                dve.wait_ge(sg_ready, 1)
                for t in range(NT):
                    dve.tensor_scalar(g.xn[:, t, :], g.xn[:, t, :], sg[:, t:t + 1], None, ALU.mult).then_inc(xs_ready, 1)
                n = 0
                for e in range(NN):
                    for m in range(F4):
                        for h in range(2):
                            dve.wait_ge(s_ready, n + 1)
                            dve.wait_ge(u_done, n + 1)
                            if m == 0 and h == 0:
                                wait_from(dve, y_done, e * NT)
                            dve.tensor_tensor(hT[:, m, h * HALF:(h + 1) * HALF], ps_u[:, n % 2, 0:HALF], s[:, n % 2, :],
                                              ALU.mult).then_inc(h_ready, 1)
                            n += 1
                    for t in range(NT):
                        dve.wait_ge(y_done, e * NT + t + 1)
                        wait_from(dve, x_done, (e - 1) * NT + t + 1)
                        c = coef[:, t, e:e + 1] if e < NE else g.gates[0:TP, 7:8]
                        dve.scalar_tensor_tensor(out=g.x[:, t, :], in0=ps_d[0:TP, 0:C], scalar=c, in1=g.x[:, t, :],
                                                 op0=ALU.mult, op1=ALU.add).then_inc(x_done, 1)



def program(nc, d, out, upto=8):
    USED.clear()
    with ExitStack() as ctx:
        g = Shared()
        a = Alloc(nc, ctx, "all")
        g.x = a.sb("x", [TP, NT, C])
        g.xn = a.sb("xn", [TP, NT, C])
        g.xnT = a.sb("xnT", [128, CC, T])
        g.ident = a.sb("ident", [128, 128])
        g.gates = a.sb("gates", [128, 8])
        g.eps = a.sb("eps", [128, 1])
        g.magnitudes = a.sb("magnitudes", [48, 1])
        begin(nc, g, d)
        stages = [lambda: causal_attention(nc, g, d, 0, g.magnitudes[:, :]), lambda: top8_ffn(nc, g, d),
                  lambda: latent_layer(nc, g, d, 1, queries_plain),
                  lambda: ternary_ffn(nc, g, d),
                  lambda: latent_layer(nc, g, d, 2, queries_roped), lambda: hadamard_ffn(nc, g, d),
                  lambda: causal_attention(nc, g, d, 3), lambda: experts_ffn(nc, g, d)]
        for n, stage in enumerate(stages[:upto]):
            stage()
            if n in (2, 5):
                clear_semaphores(nc)
        finish(nc, g, out)


class Shared:
    pass


def layouts(i):
    f = lambda v: np.ascontiguousarray(v)
    r = {"x": f(i["x"].reshape(T, C)), "g_xattn": f(i["g_xattn"].reshape(1, 4)), "g_ffn": f(i["g_ffn"].reshape(1, 4))}
    first = i["ctx_512"][:, :SK].transpose(2, 0, 1)
    r["ctx_first"] = f(np.stack([first, first], 2).reshape(DC, B * 2 * SK))
    for n in (0, 3):
        r[f"L{n}_wq"] = f(i[f"L{n}_xattn_Wq"].T)
        r[f"L{n}_kv"] = f(i[f"L{n}_xattn_Wkv_expand"].T)
        r[f"L{n}_wo"] = f(i[f"L{n}_xattn_Wout"].T)
    r["L0_rw"] = f(i["L0_ffn_router_weight"].T)
    r["L0_rb"] = f(i["L0_ffn_router_bias"].reshape(1, 64))
    r["L0_eb"] = f(i["L0_ffn_expert_bias"])
    r["ctx"] = f(i["ctx_512"].reshape(B, LK * DC))
    for n in (1, 2):
        w = {k: i[f"L{n}_xattn_{k}"] for k in ("Wq", "w_kc_q", "w_kc_kv", "W_qr", "W_kr", "Wo")}
        r[f"L{n}_wq"] = f(w["Wq"].reshape(NH, HK, C).transpose(1, 0, 2).reshape(HK, NH * C))
        r[f"L{n}_wkrT"] = f(w["W_kr"].transpose(2, 0, 1).reshape(64, NH * DC))
        r[f"L{n}_wkv"] = f(w["w_kc_kv"].transpose(1, 0, 2).reshape(HK, NH * DC))
        r[f"L{n}_wo"] = f(w["Wo"].reshape(C, NH, HK).transpose(2, 1, 0).reshape(HK, NH * C))
        wqrT = w["W_qr"].transpose(2, 0, 1)
        if n == 1:
            r["L1_wqrT"] = f(wqrT.reshape(64, NH * DQ))
            r["L1_wcqT"] = f(w["w_kc_q"].transpose(2, 0, 1).reshape(2, DQ // 2, NH, HK).transpose(1, 0, 2, 3).reshape(DQ // 2, 2 * NH * HK))
        else:
            half = DQ // 2
            turned = np.concatenate([wqrT[:, :, half:], wqrT[:, :, :half]], 2)
            r["L2_wqrT"] = f(np.stack([wqrT, turned], 1).reshape(64, 2 * NH * DQ))
            r["L2_wcq"] = f(w["w_kc_q"].transpose(1, 0, 2).reshape(HK, NH * DQ))
    r["L1_gate"], r["L1_up"], r["L1_down"] = (f(i[f"L1_ffn_w_{k}"].T) for k in ("gate", "up", "down"))
    r["L1_lanes"] = f(np.concatenate([i[f"L1_ffn_w_{k}"].reshape(-1, 16).T for k in ("gate", "up", "down")]))
    r["L2_gate"], r["L2_up"], r["L2_down"] = (f(i[f"L2_ffn_W_{k}"].T) for k in ("gate", "up", "down"))
    r["L2_su_ug"] = f(i["L2_ffn_SU_ug"].reshape(CC, 128).T)
    r["L2_su_dp"] = f(i["L2_ffn_SU_dp"].reshape(FF // 128, 128).T)
    r["L2_sc_ug"] = f(i["L2_ffn_Wscale_ug"].reshape(2 * FF // 128, 128).T)
    r["L2_sc_dp"] = f(i["L2_ffn_Wscale_dp"].reshape(1, C))
    r["L3_rw"] = f(i["L3_ffn_router_w"].T)
    r["L3_gu"], r["L3_dn"] = f(i["L3_ffn_w_gate_up"]), f(i["L3_ffn_w_down"])
    r["L3_sgu"], r["L3_sdn"] = f(i["L3_ffn_shared_gate_up"]), f(i["L3_ffn_shared_down"])
    return r


def kernel(**inputs):
    import concourse.bacc as bacc
    from concourse.bass_utils import run_bass_kernel_spmd

    nc = bacc.Bacc("TRN2", target_bir_lowering=False, num_devices=1)
    arrays = layouts({k: np.asarray(v) for k, v in inputs.items()}) | constants()
    d = {k: nc.dram_tensor(f"in_{k}", v.shape, mybir.dt.from_np(v.dtype), kind="ExternalInput").ap()
         for k, v in arrays.items()}
    out = nc.dram_tensor("out_x", (T, C), F32, kind="ExternalOutput").ap()
    program(nc, d, out)
    r = run_bass_kernel_spmd(nc, [{f"in_{k}": v for k, v in arrays.items()}], core_ids=[0])
    return r.results[0]["out_x"].reshape(B, S, C)
```

```python
from contextlib import ExitStack

import numpy as np

import concourse.bass as bass
from concourse import mybir

F32 = mybir.dt.float32
F32R = mybir.dt.float32r
BF16 = mybir.dt.bfloat16
ACT = mybir.ActivationFunctionType
ALU = mybir.AluOpType
X = mybir.AxisListType.X

B, S, C = 16, 56, 256
T = B * S
TP = 2 * S
NT = T // TP
HALF = T // 2
CC = C // 128
LK, DC = 1500, 64
NH = 16
HP = NH // 2
HD = C // NH
SK = 64
KT, KP = 12, 125
DQ = 192
QT = NH * DQ // 128
HK = 128
NE, F3 = 8, 512
SLOT_TILES = (T - NE) // 128 + NE
FF = 1024
EPS = 1e-5
MASKED = -3.0e38
ROUND = 12582912.0


def constants():
    def tables(length, dim):
        inv = (1.0 / 10000.0 ** (np.arange(0, dim, 2, dtype=np.float32) / np.float32(dim))).astype(np.float32)
        f = np.arange(length, dtype=np.float32)[:, None] * inv[None, :]
        return np.repeat(np.cos(f), 2, -1).astype(np.float32), np.repeat(np.sin(f), 2, -1).astype(np.float32)

    def hadamard(n):
        h = np.ones((1, 1), np.float32)
        while h.shape[0] < n:
            h = np.block([[h, h], [h, -h]])
        return np.ascontiguousarray(h, np.float32)

    c = {"ident": np.eye(128, dtype=np.float32), "had256": hadamard(256), "had128": hadamard(128)}
    cos, sin = tables(LK, DC)
    signed = np.concatenate([-sin[:, :DC // 2], sin[:, DC // 2:]], 1)
    c["rope_kT"] = np.ascontiguousarray(
        np.concatenate([cos.T, signed.T]).reshape(2 * DC, KP, KT).transpose(0, 2, 1).reshape(2 * DC, LK))
    c["rope_k"] = np.stack([cos, signed]).reshape(2, KP, KT * DC)
    cos, sin = tables(S, DQ)
    i = np.arange(QT * 128) % DQ
    turned = np.where(i < DQ // 2, 1, -1).astype(np.float32) * sin[:, (i + DQ // 2) % DQ]
    c["rope_q"] = np.ascontiguousarray(
        np.stack([cos[:, i], turned])[:, :, :3 * 128].reshape(2, S, 3, 128).transpose(3, 0, 2, 1)).astype(np.float32)
    q, k = np.arange(128)[:, None] % 64, np.arange(SK)[None, :]
    c["causal"] = np.where(k <= q, 0.0, MASKED).astype(np.float32)
    c["headmask"] = (np.arange(128)[:, None] // HD == np.arange(8)[None, :]).astype(np.float32)
    c["lanes"] = (np.arange(48)[:, None] // 16 == np.arange(3)[None, :]).astype(np.float32)
    c["before"] = (np.arange(TP)[:, None] < np.arange(TP)[None, :]).astype(np.float32)
    c["numbers"] = np.arange(SLOT_TILES, dtype=np.float32).reshape(1, SLOT_TILES)
    c["later"] = np.tile(np.arange(8, dtype=np.float32), (128, 1))
    return c


class Chain:

    def __init__(self, eng, sem):
        self.eng, self.sem, self.n = eng, sem, 0

    def __call__(self, ins):
        self.n += 1
        ins.then_inc(self.sem, 1)
        self.eng.wait_ge(self.sem, self.n)


class Alloc:
    def __init__(self, nc, ctx, stage):
        self.nc, self.ctx, self.stage = nc, ctx, stage

    def sb(self, name, shape, dt=F32):
        return self.ctx.enter_context(self.nc.sbuf_tensor(f"{self.stage}_{name}", shape, dt))

    def ps(self, name, shape, dt=F32):
        return self.ctx.enter_context(self.nc.psum_tensor(f"{self.stage}_{name}", shape, dt))

    def sem(self, name):
        s = self.nc.alloc_semaphore(f"{self.stage}_{name}")
        USED.append(s)
        return s


USED = []


def clear_semaphores(nc):
    nc.clear_and_free_semaphores(list(USED))
    USED.clear()
    nc.all_engine_barrier()


class Norm:

    def __init__(self, nc, a, g, turned=None):
        self.nc, self.g = nc, g
        self.stats = a.sb("ln_stats", [TP, NT, 6])
        self.mv = a.sb("ln_mv", [TP, NT, 2])
        self.std = a.sb("ln_std", [TP, NT])
        self.rstd = a.sb("ln_rstd", [TP, NT])
        self.shift = a.sb("ln_shift", [TP, NT])
        self.turned = turned or a.ps("ln_turned", [128, 2, 512])
        self.stats_done = a.sem("ln_stats_done")
        self.mv_ready = a.sem("ln_mv_ready")
        self.std_ready = a.sem("ln_std_ready")
        self.scale_ready = a.sem("ln_scale_ready")
        self.xn_ready = a.sem("ln_xn_ready")
        self.turned_ready = a.sem("ln_turned_ready")
        self.xnT_ready = a.sem("ln_xnT_ready")

    def vector(self, dve):
        g = self.g
        for t in range(NT):
            dve.bn_stats(self.stats[:, t, :], g.x[:, t, :]).then_inc(self.stats_done, 1)
        for t in range(NT):
            dve.wait_ge(self.stats_done, t + 1)
            dve.bn_aggr(self.mv[:, t, :], self.stats[:, t, :]).then_inc(self.mv_ready, 1)
        dve.wait_ge(self.std_ready, 1)
        dve.reciprocal(self.rstd[:, :], self.std[:, :]).then_inc(self.scale_ready, 1)
        dve.wait_ge(self.scale_ready, 1)
        dve.scalar_tensor_tensor(out=self.shift[:, :], in0=self.mv[:, :, 0], scalar=-1.0,
                                 in1=self.rstd[:, :], op0=ALU.mult, op1=ALU.mult).then_inc(self.scale_ready, 1)
        dve.wait_ge(self.scale_ready, 2)
        for t in range(NT):
            dve.tensor_scalar(g.xn[:, t, :], g.x[:, t, :], self.rstd[:, t:t + 1], self.shift[:, t:t + 1],
                              ALU.mult, ALU.add).then_inc(self.xn_ready, 1)

    def scalar(self, act):
        g = self.g
        act.wait_ge(self.mv_ready, NT)
        act.activation(self.std[:, :], self.mv[:, :, 1], ACT.Sqrt, bias=g.eps[0:TP, 0:1]).then_inc(self.std_ready, 1)
        for t in range(NT):
            act.wait_ge(self.turned_ready, t + 1)
            act.copy(g.xnT[:, :, t * TP:(t + 1) * TP],
                     self.turned[:, t % 2, 0:2 * TP].rearrange("p (c n) -> p c n", c=CC)).then_inc(self.xnT_ready, 1)

    def tensor(self, pe):
        g = self.g
        for t in range(NT):
            pe.wait_ge(self.xn_ready, t + 1)
            if t >= 2:
                pe.wait_ge(self.xnT_ready, t - 1)
            for c in range(CC):
                last = pe.transpose(self.turned[:, t % 2, c * TP:(c + 1) * TP],
                                    g.xn[:, t, c * 128:(c + 1) * 128], g.ident[0:TP, 0:TP])
            last.then_inc(self.turned_ready, 1)


def begin(nc, g, d):
    with ExitStack() as ctx:
        a = Alloc(nc, ctx, "begin")
        came = a.sem("came")
        set_ = a.sem("set")
        done = a.sem("done")
        raw = a.sb("gates_raw", [128, 8])
        with nc.Block() as block:

            @block.sync
            def _(sp):
                sp.dma_start(g.x[:, :, :], d["x"].rearrange("(t p) c -> p t c", p=TP)).then_inc(came, 16)
                sp.dma_start(g.ident[:, :], d["ident"]).then_inc(came, 16)
                sp.dma_start(raw[:, 0:4], d["g_xattn"].partition_broadcast(128)).then_inc(came, 16)
                sp.dma_start(raw[:, 4:8], d["g_ffn"].partition_broadcast(128)).then_inc(came, 16)

            @block.vector
            def _(dve):
                dve.memset(g.eps[:, :], EPS).then_inc(set_, 1)

            @block.scalar
            def _(act):
                act.wait_ge(came, 64)
                act.activation(g.gates[:, :], raw[:, :], ACT.Tanh).then_inc(done, 1)


def finish(nc, g, out):
    with ExitStack() as ctx:
        a = Alloc(nc, ctx, "finish")
        stored = a.sem("stored")
        with nc.Block() as block:

            @block.sync
            def _(sp):
                sp.dma_start(out.rearrange("(t p) c -> p t c", p=TP), g.x[:, :, :]).then_inc(stored, 16)
                sp.wait_ge(stored, 16)


def causal_attention(nc, g, d, layer, magnitudes=None, ahead=None):
    gate = g.gates[0:TP, layer:layer + 1]
    NP = B // 2
    with ExitStack() as ctx:
        a = Alloc(nc, ctx, f"xattn{layer}")
        wq = a.sb("wq", [128, CC, C])
        wkv = a.sb("wkv", [DC, 2 * C])
        wo = a.sb("wo", [128, CC, C])
        ctxT = a.sb("ctxT", [DC, B, 2, SK])
        causal = a.sb("causal", [128, SK])
        headmask = a.sb("headmask", [128, 8])
        kT = a.sb("kT", [128, CC, B, SK])
        values = a.sb("values", [128, B, HP, 2, HD])
        qT = a.sb("qT", [128, CC, T + 8])
        keys = a.sb("keys", [128, 8, 8, SK])
        sc = a.sb("scores", [128, 3, NH, SK])
        mx = a.sb("mx", [128, 2, NH])
        den = a.sb("den", [128, 2, NH])
        wT = a.sb("weightsT", [128, 2, HP, 128])
        oT = a.sb("outT", [128, CC, T])
        if magnitudes is not None:
            lanes = a.sb("lanes", [48, FF * C // 16])
            lanes_came = a.sem("lanes_came")
            lanes_summed = a.sem("lanes_summed")
        norm = Norm(nc, a, g)
        ps_a = a.ps("ps_a", [128, 2, 512])
        ps_t = a.ps("ps_t", [128, 2, 512])
        ps_o = a.ps("ps_o", [128, 512])
        ps_y = a.ps("ps_y", [128, 512])
        came = a.sem("came")
        zeroed = a.sem("zeroed")
        prod = a.sem("prod")
        taken = a.sem("taken")
        keys_ready = a.sem("keys_ready")
        scores_done = a.sem("scores_done")
        masked = a.sem("masked")
        shifted = a.sem("shifted")
        exp_done = a.sem("exp_done")
        weights_ready = a.sem("weights_ready")
        turned = a.sem("turned")
        wT_ready = a.sem("wT_ready")
        o_done = a.sem("o_done")
        o_taken = a.sem("o_taken")
        y_done = a.sem("y_done")
        x_done = a.sem("x_done")
        chain = a.sem("dve_chain")
        KV, VV, QQ = 4, 16, 4
        with nc.Block() as block:

            @block.sync
            def _(sp):
                sp.dma_start(wkv[:, :], d[f"L{layer}_kv"]).then_inc(came, 16)
                sp.dma_start(ctxT[:, :, :, :], d["ctx_first"].rearrange("d (b e k) -> d b e k", b=B, e=2)).then_inc(came, 16)
                sp.dma_start(wq[:, :, :], d[f"L{layer}_wq"].rearrange("(c p) n -> p c n", p=128)).then_inc(came, 16)
                sp.dma_start(wo[:, :, :], d[f"L{layer}_wo"].rearrange("(c p) n -> p c n", p=128)).then_inc(came, 16)
                sp.dma_start(causal[:, :], d["causal"]).then_inc(came, 16)
                sp.dma_start(headmask[:, :], d["headmask"]).then_inc(came, 16)
                if magnitudes is not None:
                    sp.dma_start(lanes[:, :], d["L1_lanes"]).then_inc(lanes_came, 16)
                if ahead is not None:
                    ahead(sp)

            @block.gpsimd
            def _(pool):
                pool.memset(values[:, :, :, :, :], 0.0).then_inc(zeroed, 1)
                pool.memset(qT[:, :, T:T + 8], 0.0).then_inc(zeroed, 1)
                pool.wait_ge(came, 96)
                pool.wait_ge(taken, KV)
                for n in range(2 * B):
                    b, c = n // 2, n % 2
                    if n >= 8:
                        pool.wait_ge(scores_done, (n - 8) // 4 + 1)
                    pool.tensor_tensor(keys[:, n % 8, :, :],
                                       kT[:, c, b, :].unsqueeze(1).to_broadcast([128, 8, SK]),
                                       headmask[:, :].unsqueeze(2).to_broadcast([128, 8, SK]),
                                       ALU.mult).then_inc(keys_ready, 1)

            @block.tensor
            def _(pe):
                pe.wait_ge(came, 96)
                n = 0
                for c in range(CC):
                    for h in range(2):
                        if n >= 2:
                            pe.wait_ge(taken, n - 1)
                        pe.matmul(ps_a[:, n % 2, :], wkv[:, c * 128:(c + 1) * 128],
                                  ctxT[:, 8 * h:8 * h + 8, 0, :], start=True, stop=True).then_inc(prod, 1)
                        n += 1
                for b in range(B):
                    pe.wait_ge(taken, n - 1)
                    pe.matmul(ps_a[:, n % 2, 0:C], ctxT[:, b, :, :], wkv[:, C:2 * C],
                              start=True, stop=True).then_inc(prod, 1)
                    n += 1
                norm.tensor(pe)
                pe.wait_ge(norm.xnT_ready, NT)
                for m in range(CC):
                    for h in range(2):
                        pe.wait_ge(taken, n - 1)
                        for c in range(CC):
                            last = pe.matmul(ps_a[:, n % 2, 0:HALF], wq[:, c, m * 128:(m + 1) * 128],
                                             g.xnT[:, c, h * HALF:(h + 1) * HALF], start=(c == 0), stop=(c == CC - 1))
                        last.then_inc(prod, 1)
                        n += 1
                pe.wait_ge(taken, n)
                pe.wait_ge(zeroed, 2)

                def scores(p):
                    pe.wait_ge(keys_ready, 4 * p + 4)
                    if p >= 1:
                        pe.wait_ge(masked, p)
                    for e in range(2):
                        b = 2 * p + e
                        for c in range(CC):
                            last = pe.matmul(ps_a[64 * e:64 * e + 64, c, :], qT[:, c, b * S:b * S + 64],
                                             keys[:, (4 * p + 2 * e + c) % 8, :, :], start=True, stop=True)
                    last.then_inc(scores_done, 1)

                def output(p):
                    pe.wait_ge(weights_ready, p + 1)
                    for j in range(HP):
                        if j % 4 == 0 and p >= 1:
                            pe.wait_ge(wT_ready, 2 * p)
                        last = pe.transpose(ps_t[:, j // 4, (j % 4) * 128:(j % 4) * 128 + 128],
                                            sc[:, p % 3, 2 * j:2 * j + 2, :], g.ident[:, :])
                        if j % 4 == 3:
                            last.then_inc(turned, 1)
                    pe.wait_ge(wT_ready, 2 * p + 2)
                    if p >= 1:
                        pe.wait_ge(o_taken, p)
                    for e in range(2):
                        for j in range(HP):
                            c, r = j // 4, 32 * (j % 4)
                            last = pe.matmul(ps_o[r:r + 32, c * 128 + e * 64:c * 128 + e * 64 + 64],
                                             values[:, 2 * p + e, j, :, :], wT[:, p % 2, j, e * 64:e * 64 + 64],
                                             start=True, stop=True, tile_position=(0, r))
                    last.then_inc(o_done, 1)

                def project(p):
                    pe.wait_ge(o_taken, p + 1)
                    if p >= 1:
                        pe.wait_ge(x_done, p)
                    for c in range(CC):
                        last = pe.matmul(ps_y[0:TP, 0:C], oT[:, c, p * TP:(p + 1) * TP], wo[:, c, :],
                                         start=(c == 0), stop=(c == CC - 1))
                    last.then_inc(y_done, 1)

                for p in range(NP + 3):
                    if p < NP:
                        scores(p)
                    if 2 <= p < NP + 2:
                        output(p - 2)
                    if p >= 3:
                        project(p - 3)

            @block.scalar
            def _(act):
                n = 0
                for c in range(CC):
                    for h in range(2):
                        act.wait_ge(prod, n + 1)
                        act.copy(kT[:, c, 8 * h:8 * h + 8, :],
                                 ps_a[:, n % 2, :].rearrange("p (b k) -> p b k", k=SK)).then_inc(taken, 1)
                        n += 1
                act.wait_ge(zeroed, 1)
                for b in range(B):
                    act.wait_ge(prod, n + 1)
                    v = ps_a[:, n % 2, 0:C].rearrange("p (j e k) -> p j e k", j=HP, e=2)
                    act.copy(values[0:64, b, :, 0, :], v[0:64, :, 0, :])
                    act.copy(values[64:128, b, :, 1, :], v[64:128, :, 1, :]).then_inc(taken, 1)
                    n += 1
                norm.scalar(act)
                for m in range(CC):
                    for h in range(2):
                        act.wait_ge(prod, n + 1)
                        act.mul(qT[:, m, h * HALF:(h + 1) * HALF], ps_a[:, n % 2, 0:HALF], HD ** -0.5).then_inc(taken, 1)
                        n += 1

                def exp(p):
                    act.wait_ge(shifted, p + 1)
                    act.activation(sc[:, p % 3, :, :], sc[:, p % 3, :, :], ACT.Exp).then_inc(exp_done, 1)

                def take(p):
                    for h in range(2):
                        act.wait_ge(turned, 2 * p + h + 1)
                        if p >= 2 and h == 0:
                            act.wait_ge(o_done, p - 1)
                        act.copy(wT[:, p % 2, 4 * h:4 * h + 4, :],
                                 ps_t[:, h, :].rearrange("p (j n) -> p j n", j=4)).then_inc(wT_ready, 1)
                    act.wait_ge(o_done, p + 1)
                    act.copy(oT[:, :, p * TP:(p + 1) * TP].rearrange("q c (e s) -> q c e s", e=2),
                             ps_o[:, 0:256].rearrange("q (c e s) -> q c e s", c=2, e=2)[:, :, :, 0:S]).then_inc(o_taken, 1)

                for p in range(NP + 2):
                    if p >= 2:
                        take(p - 2)
                    if p < NP:
                        exp(p)

            @block.vector
            def _(dve):
                norm.vector(dve)
                step = Chain(dve, chain)
                if magnitudes is not None:
                    dve.wait_ge(lanes_came, 16)
                    dve.tensor_reduce(magnitudes, lanes[:, :], X, ALU.add, apply_absolute_value=True).then_inc(lanes_summed, 1)

                def soft(p):
                    u = p % 2
                    dve.wait_ge(scores_done, p + 1)
                    if p >= 3:
                        dve.wait_ge(turned, 2 * p - 4)
                    ins = dve.tensor_tensor(sc[:, p % 3, :, :], ps_a[:, :, :].rearrange("p c (h k) -> p (c h) k", k=SK),
                                            causal[:, :].unsqueeze(1).to_broadcast([128, NH, SK]), ALU.add)
                    ins.then_inc(masked, 1)
                    dve.wait_ge(masked, p + 1)
                    step(dve.tensor_reduce(mx[:, u, :], sc[:, p % 3, :, :], X, ALU.max))
                    dve.tensor_tensor(sc[:, p % 3, :, :], sc[:, p % 3, :, :],
                                      mx[:, u, :].unsqueeze(2).to_broadcast([128, NH, SK]),
                                      ALU.subtract).then_inc(shifted, 1)

                def normalise(p):
                    u = p % 2
                    dve.wait_ge(exp_done, p + 1)
                    step(dve.tensor_reduce(den[:, u, :], sc[:, p % 3, :, :], X, ALU.add))
                    step(dve.reciprocal(mx[:, u, :], den[:, u, :]))
                    dve.tensor_tensor(sc[:, p % 3, :, :], sc[:, p % 3, :, :],
                                      mx[:, u, :].unsqueeze(2).to_broadcast([128, NH, SK]),
                                      ALU.mult).then_inc(weights_ready, 1)

                def add(p):
                    dve.wait_ge(y_done, p + 1)
                    dve.scalar_tensor_tensor(out=g.x[:, p, :], in0=ps_y[0:TP, 0:C], scalar=gate, in1=g.x[:, p, :],
                                             op0=ALU.mult, op1=ALU.add).then_inc(x_done, 1)

                dve.wait_ge(came, 96)
                for p in range(NP + 4):
                    if p < NP:
                        soft(p)
                    if p >= 4:
                        add(p - 4)
                    if 1 <= p <= NP:
                        normalise(p - 1)


def top8_ffn(nc, g, d):
    E = 64
    gate = g.gates[0:TP, 4:5]
    with ExitStack() as ctx:
        a = Alloc(nc, ctx, "ffn0")
        rw = a.sb("rw", [128, CC, E])
        bias = a.sb("bias", [TP, E])
        eb = a.sb("eb", [E, C])
        e = a.sb("e", [TP, NT, E])
        rest = a.sb("rest", [TP, NT, E])
        m8 = a.sb("m8", [TP, NT, 8])
        mx = a.sb("mx", [TP, NT])
        den = a.sb("den", [TP, NT])
        top = a.sb("top", [TP, NT])
        wT = a.sb("wT", [E, NT, TP])
        y = a.sb("y", [TP, NT, C])
        norm = Norm(nc, a, g)
        ps_l = a.ps("ps_l", [128, 512])
        ps_t = a.ps("ps_t", [128, 2, 512])
        ps_y = a.ps("ps_y", [128, 2, 512])
        came = a.sem("came")
        logits = a.sem("logits")
        shifted = a.sem("shifted")
        exp_done = a.sem("exp_done")
        w_ready = a.sem("w_ready")
        turned = a.sem("turned")
        wT_ready = a.sem("wT_ready")
        y_done = a.sem("y_done")
        y_taken = a.sem("y_taken")
        chain = a.sem("dve_chain")
        with nc.Block() as block:

            @block.sync
            def _(sp):
                sp.dma_start(rw[:, :, :], d["L0_rw"].rearrange("(c p) n -> p c n", p=128)).then_inc(came, 16)
                sp.dma_start(bias[:, :], d["L0_rb"].partition_broadcast(TP)).then_inc(came, 16)
                sp.dma_start(eb[:, :], d["L0_eb"]).then_inc(came, 16)

            @block.tensor
            def _(pe):
                norm.tensor(pe)
                pe.wait_ge(came, 48)
                for t in range(NT):
                    pe.wait_ge(norm.xnT_ready, t + 1)
                    for c in range(CC):
                        last = pe.matmul(ps_l[0:TP, t * E:(t + 1) * E], g.xnT[:, c, t * TP:(t + 1) * TP], rw[:, c, :],
                                         start=(c == 0), stop=(c == CC - 1))
                last.then_inc(logits, 1)
                pe.wait_ge(w_ready, 1)
                for t in range(NT):
                    if t >= 2:
                        pe.wait_ge(wT_ready, t - 1)
                    pe.transpose(ps_t[0:E, t % 2, 0:TP], e[:, t, :], g.ident[0:TP, 0:TP]).then_inc(turned, 1)
                    pe.wait_ge(wT_ready, t + 1)
                    if t >= 2:
                        pe.wait_ge(y_taken, t - 1)
                    pe.matmul(ps_y[0:TP, t % 2, 0:C], wT[:, t, :], eb[:, :], start=True, stop=True).then_inc(y_done, 1)

            @block.scalar
            def _(act):
                norm.scalar(act)
                act.wait_ge(shifted, 1)
                act.activation(e[:, :, :], e[:, :, :], ACT.Exp).then_inc(exp_done, 1)
                for t in range(NT):
                    act.wait_ge(turned, t + 1)
                    act.copy(wT[:, t, :], ps_t[0:E, t % 2, 0:TP]).then_inc(wT_ready, 1)

            @block.vector
            def _(dve):
                norm.vector(dve)
                step = Chain(dve, chain)
                wide = lambda v: v.unsqueeze(2).to_broadcast([TP, NT, E])
                dve.wait_ge(came, 48)
                dve.wait_ge(logits, 1)
                step(dve.tensor_tensor(e[:, :, :], ps_l[0:TP, :].rearrange("p (t e) -> p t e", e=E),
                                       bias[:, :].unsqueeze(1).to_broadcast([TP, NT, E]), ALU.add))
                step(dve.tensor_reduce(mx[:, :], e[:, :, :], X, ALU.max))
                dve.tensor_tensor(e[:, :, :], e[:, :, :], wide(mx[:, :]), ALU.subtract).then_inc(shifted, 1)
                dve.wait_ge(exp_done, 1)
                step(dve.tensor_reduce(den[:, :], e[:, :, :], X, ALU.add))
                step(dve.reciprocal(mx[:, :], den[:, :]))
                for t in range(NT):
                    step(dve.max(m8[:, t, :], e[:, t, :]))
                    step(dve.match_replace(rest[:, t, :], m8[:, t, :], e[:, t, :], 0.0))
                step(dve.tensor_tensor(e[:, :, :], e[:, :, :], rest[:, :, :], ALU.subtract))
                dve.tensor_tensor(e[:, :, :], e[:, :, :], wide(mx[:, :]), ALU.mult).then_inc(w_ready, 1)
                step(dve.tensor_reduce(top[:, :], m8[:, :, :], X, ALU.add))
                step(dve.tensor_tensor(top[:, :], top[:, :], mx[:, :], ALU.mult))
                for t in range(NT):
                    dve.wait_ge(y_done, t + 1)
                    ins = dve.scalar_tensor_tensor(out=y[:, t, :], in0=g.xn[:, t, :], scalar=top[:, t:t + 1],
                                                   in1=ps_y[0:TP, t % 2, 0:C], op0=ALU.mult, op1=ALU.add)
                    ins.then_inc(y_taken, 1)
                    dve.wait_ge(y_taken, t + 1)
                    step(dve.scalar_tensor_tensor(out=g.x[:, t, :], in0=y[:, t, :], scalar=gate, in1=g.x[:, t, :],
                                                  op0=ALU.mult, op1=ALU.add))


def wait_from(eng, sem, value):
    if not (isinstance(value, int) and value <= 0):
        eng.wait_ge(sem, value)


def latent_outputs(a, norm):
    return dict(ps=norm.turned, folded=a.sem("folded"), taken=a.sem("folded_taken"))


def out_weights_tensor(pe, f, wkv, wo):
    for j in range(HP):
        if j >= 2:
            pe.wait_ge(f["taken"], j - 1)
        for e in range(2):
            last = pe.matmul(f["ps"][64 * e:64 * e + 64, j % 2, 0:C], wkv[:, 2 * j + e, :], wo[:, 2 * j + e, :],
                             start=True, stop=True)
        last.then_inc(f["folded"], 1)


def out_weights_scalar(act, f, fold):
    for j in range(HP):
        act.wait_ge(f["folded"], j + 1)
        act.copy(fold[:, j, :], f["ps"][:, j % 2, 0:C]).then_inc(f["taken"], 1)


def queries_plain(nc, g, d, q, fold):
    IC = DQ // 2
    with ExitStack() as ctx:
        a = Alloc(nc, ctx, "q1")
        wq = a.sb("wq", [128, NH, C])
        wcqT = a.sb("wcqT", [IC, 2, NH, HK])
        wqrT = a.sb("wqrT", [128, HP, DQ])
        wkrT = a.sb("wkrT", [128, HP, 2, DC])
        wkv = a.sb("wkv", [128, NH, DC])
        wo = a.sb("wo", [128, NH, C])
        z = a.sb("z", [IC, 2, 2, 2, DC])
        y = a.sb("y", [128, 2, 2, 2, DC])
        aw = a.sb("a", [128, HP, CC, 2, DC])
        norm = Norm(nc, a, g)
        f = latent_outputs(a, norm)
        ps_z = a.ps("ps_z", [128, 2, 512])
        ps_y = a.ps("ps_y", [128, 2, 512])
        ps_q = a.ps("ps_q", [128, 2, 512])
        zeroed, came_r, came, came_o = a.sem("zeroed"), a.sem("came_r"), a.sem("came"), a.sem("came_o")
        z_done, z_ready, y_done, y_ready, a_done, a_ready, q_done, q_taken = (
            a.sem(n) for n in ("z_done", "z_ready", "y_done", "y_ready", "a_done", "a_ready", "q_done", "q_taken"))
        with nc.Block() as block:

            @block.sync
            def _(sp):
                for e in range(2):
                    sp.dma_start(wqrT[64 * e:64 * e + 64, :, :],
                                 d["L1_wqrT"].rearrange("r (j e i) -> r j e i", j=HP, e=2)[:, :, e, :]).then_inc(came_r, 16)
                sp.wait_ge(zeroed, 1)
                for e in range(2):
                    sp.dma_start(wkrT[64 * e:64 * e + 64, :, e, :],
                                 d["L1_wkrT"].rearrange("r (j e n) -> r j e n", j=HP, e=2)[:, :, e, :]).then_inc(came_r, 16)
                sp.dma_start(wcqT[:, :, :, :], d["L1_wcqT"].rearrange("i (u h k) -> i u h k", u=2, h=NH)).then_inc(came, 16)
                sp.dma_start(wq[:, :, :], d["L1_wq"].rearrange("k (h n) -> k h n", h=NH)).then_inc(came, 16)
                sp.dma_start(wkv[:, :, :], d["L1_wkv"].rearrange("k (h n) -> k h n", h=NH)).then_inc(came_o, 16)
                sp.dma_start(wo[:, :, :], d["L1_wo"].rearrange("k (h n) -> k h n", h=NH)).then_inc(came_o, 16)

            @block.gpsimd
            def _(pool):
                pool.memset(wkrT[:, :, :, :], 0.0).then_inc(zeroed, 1)

            @block.tensor
            def _(pe):
                norm.tensor(pe)

                def fold_z(j):
                    if j >= 2:
                        pe.wait_ge(z_ready, j - 1)
                    for u in range(2):
                        last = pe.matmul(ps_z[0:IC, j % 2, u * 128:(u + 1) * 128], wqrT[:, j, u * IC:(u + 1) * IC],
                                         wkrT[:, j, :, :], start=True, stop=True)
                    last.then_inc(z_done, 1)

                def fold_y(j):
                    pe.wait_ge(z_ready, j + 1)
                    if j >= 2:
                        pe.wait_ge(y_ready, j - 1)
                    for e in range(2):
                        for u in range(2):
                            last = pe.matmul(ps_y[:, j % 2, e * 128:(e + 1) * 128], wcqT[:, u, 2 * j + e, :], z[:, j % 2, u, :, :],
                                             start=(u == 0), stop=(u == 1))
                    last.then_inc(y_done, 1)

                def fold_a(j):
                    pe.wait_ge(y_ready, j + 1)
                    if j >= 2:
                        pe.wait_ge(a_ready, j - 1)
                    for c in range(CC):
                        for e in range(2):
                            at = (2 * c + e) * 128
                            last = pe.matmul(ps_q[:, j % 2, at:at + 128], wq[:, 2 * j + e, c * 128:(c + 1) * 128],
                                             y[:, j % 2, e, :, :], start=True, stop=True)
                    last.then_inc(a_done, 1)

                pe.wait_ge(came_r, 64)
                for n in range(HP + 2):
                    if n < HP:
                        fold_z(n)
                    if 1 <= n <= HP:
                        if n == 1:
                            pe.wait_ge(came, 32)
                        fold_y(n - 1)
                    if n >= 2:
                        fold_a(n - 2)
                pe.wait_ge(came_o, 32)
                pe.wait_ge(norm.xnT_ready, NT)
                out_weights_tensor(pe, f, wkv, wo)
                pe.wait_ge(a_ready, HP)
                n = 0
                for j in range(HP):
                    for h in range(2):
                        if n >= 2:
                            pe.wait_ge(q_taken, n - 1)
                        for c in range(CC):
                            last = pe.matmul(ps_q[:, n % 2, 0:HALF], aw[:, j, c, :, :], g.xnT[:, c, h * HALF:(h + 1) * HALF],
                                             start=(c == 0), stop=(c == CC - 1))
                        last.then_inc(q_done, 1)
                        n += 1

            @block.scalar
            def _(act):
                norm.scalar(act)

                def take_z(j):
                    act.wait_ge(z_done, j + 1)
                    if j >= 2:
                        act.wait_ge(y_done, j - 1)
                    act.copy(z[:, j % 2, :, :, :].rearrange("p u e n -> p (u e n)"), ps_z[0:IC, j % 2, 0:256]).then_inc(z_ready, 1)

                def take_y(j):
                    act.wait_ge(y_done, j + 1)
                    if j >= 2:
                        act.wait_ge(a_done, j - 1)
                    act.copy(y[:, j % 2, :, :, :].rearrange("p u e n -> p (u e n)"), ps_y[:, j % 2, 0:256]).then_inc(y_ready, 1)

                def take_a(j):
                    act.wait_ge(a_done, j + 1)
                    src = ps_q[:, j % 2, :].rearrange("p (c e v n) -> p c e v n", c=CC, e=2, v=2)
                    for e in range(2):
                        last = act.copy(aw[:, j, :, e, :], src[:, :, e, e, :])
                    last.then_inc(a_ready, 1)

                for n in range(HP + 2):
                    if n < HP:
                        take_z(n)
                    if 1 <= n <= HP:
                        take_y(n - 1)
                    if n >= 2:
                        take_a(n - 2)
                out_weights_scalar(act, f, fold)
                for n in range(2 * HP):
                    j, h = n // 2, n % 2
                    act.wait_ge(q_done, n + 1)
                    act.copy(q[:, j, h * HALF:(h + 1) * HALF], ps_q[:, n % 2, 0:HALF]).then_inc(q_taken, 1)

            @block.vector
            def _(dve):
                norm.vector(dve)


def queries_roped(nc, g, d, q, fold):
    with ExitStack() as ctx:
        a = Alloc(nc, ctx, "q2")
        wq = a.sb("wq", [128, NH, C])
        wcq = a.sb("wcq", [128, NH, DQ])
        wqrT = a.sb("wqrT", [128, 2, HP, 2, DQ])
        wkrT = a.sb("wkrT", [128, HP, 2, DC])
        wkv = a.sb("wkv", [128, NH, DC])
        wo = a.sb("wo", [128, NH, C])
        rope = a.sb("rope", [128, 2, 3, S])
        G = a.sb("G", [128, CC, NH * DQ])
        z = a.sb("z", [128, HP, 3, 2, 2, DC])
        ur = a.sb("u_roped", [128, 2, 2, HALF])
        norm = Norm(nc, a, g)
        f = latent_outputs(a, norm)
        ps_g = a.ps("ps_g", [128, 2, 512])
        ps_q = a.ps("ps_q", [128, 2, 512])
        came_r, came, came_o = a.sem("came_r"), a.sem("came"), a.sem("came_o")
        zeroed, z_done, z_ready, g_done, g_ready, u_done, u_ready, q_done, q_taken, u_used = (
            a.sem(n) for n in ("zeroed", "z_done", "z_ready", "g_done", "g_ready", "u_done", "u_ready", "q_done", "q_taken", "u_used"))
        with nc.Block() as block:

            @block.sync
            def _(sp):
                sp.wait_ge(zeroed, 2)
                for e in range(2):
                    for v in range(2):
                        sp.dma_start(wqrT[64 * e:64 * e + 64, v, :, e, :],
                                     d["L2_wqrT"].rearrange("r (v j e i) -> r v j e i", v=2, j=HP, e=2)[:, v, :, e, :]).then_inc(came_r, 16)
                    sp.dma_start(wkrT[64 * e:64 * e + 64, :, e, :],
                                 d["L2_wkrT"].rearrange("r (j e n) -> r j e n", j=HP, e=2)[:, :, e, :]).then_inc(came_r, 16)
                sp.dma_start(wcq[:, :, :], d["L2_wcq"].rearrange("k (h i) -> k h i", h=NH)).then_inc(came, 16)
                sp.dma_start(wq[:, :, :], d["L2_wq"].rearrange("k (h n) -> k h n", h=NH)).then_inc(came, 16)
                sp.dma_start(rope[:, :, :, :], d["rope_q"]).then_inc(came, 16)
                sp.dma_start(wkv[:, :, :], d["L2_wkv"].rearrange("k (h n) -> k h n", h=NH)).then_inc(came_o, 16)
                sp.dma_start(wo[:, :, :], d["L2_wo"].rearrange("k (h n) -> k h n", h=NH)).then_inc(came_o, 16)

            @block.gpsimd
            def _(pool):
                pool.memset(wkrT[:, :, :, :], 0.0).then_inc(zeroed, 1)
                pool.memset(wqrT[:, :, :, :, :], 0.0).then_inc(zeroed, 1)

            @block.tensor
            def _(pe):
                norm.tensor(pe)
                pe.wait_ge(came_r, 96)
                for n in range(2 * HP):
                    j, v = n // 2, n % 2
                    if n >= 2:
                        pe.wait_ge(z_ready, n - 1)
                    for t in range(3):
                        last = pe.matmul(ps_q[:, n % 2, t * 128:(t + 1) * 128],
                                         wqrT[:, v, j, :, :].rearrange("p e i -> p (e i)")[:, t * 128:(t + 1) * 128],
                                         wkrT[:, j, :, :], start=True, stop=True)
                    last.then_inc(z_done, 1)
                pe.wait_ge(came, 48)
                for h in range(NH):
                    if h >= 2:
                        pe.wait_ge(g_ready, h - 1)
                    for c in range(CC):
                        last = pe.matmul(ps_g[:, h % 2, c * DQ:(c + 1) * DQ], wq[:, h, c * 128:(c + 1) * 128], wcq[:, h, :],
                                         start=True, stop=True)
                    last.then_inc(g_done, 1)
                pe.wait_ge(came_o, 32)
                pe.wait_ge(norm.xnT_ready, NT)
                out_weights_tensor(pe, f, wkv, wo)
                pe.wait_ge(z_ready, 2 * HP)
                pe.wait_ge(g_ready, NH)

                def wide(n):
                    j, h, t = n // 6, n // 3 % 2, n % 3
                    if n >= 2:
                        pe.wait_ge(u_ready, 2 * n - 2)
                    for c in range(CC):
                        at = (3 * j + t) * 128
                        last = pe.matmul(ps_g[:, n % 2, 0:HALF], G[:, c, at:at + 128], g.xnT[:, c, h * HALF:(h + 1) * HALF],
                                         start=(c == 0), stop=(c == CC - 1))
                    last.then_inc(u_done, 1)

                def narrow(n):
                    j, h, t = n // 6, n // 3 % 2, n % 3
                    pe.wait_ge(u_ready, 2 * n + 2)
                    if t == 0 and n // 3 >= 2:
                        pe.wait_ge(q_taken, n // 3 - 1)
                    for v in range(2):
                        last = pe.matmul(ps_q[:, n // 3 % 2, 0:HALF], z[:, j, t, v, :, :], ur[:, n % 2, v, :],
                                         start=(t == 0 and v == 0), stop=(t == 2 and v == 1))
                    last.then_inc(u_used, 1)

                for n in range(6 * HP + 1):
                    if n < 6 * HP:
                        wide(n)
                    if n >= 1:
                        narrow(n - 1)

            @block.scalar
            def _(act):
                norm.scalar(act)
                for n in range(2 * HP):
                    act.wait_ge(z_done, n + 1)
                    act.copy(z[:, n // 2, :, n % 2, :, :].rearrange("p t e n -> p t (e n)"),
                             ps_q[:, n % 2, 0:3 * 128].rearrange("p (t n) -> p t n", t=3)).then_inc(z_ready, 1)
                for h in range(NH):
                    act.wait_ge(g_done, h + 1)
                    act.copy(G[:, :, h * DQ:(h + 1) * DQ], ps_g[:, h % 2, 0:CC * DQ].rearrange("p (c n) -> p c n", c=CC)).then_inc(g_ready, 1)
                out_weights_scalar(act, f, fold)
                for n in range(2 * HP):
                    act.wait_ge(u_used, 3 * n + 3)
                    act.copy(q[:, n // 2, (n % 2) * HALF:(n % 2 + 1) * HALF], ps_q[:, n % 2, 0:HALF]).then_inc(q_taken, 1)

            @block.vector
            def _(dve):
                norm.vector(dve)
                dve.wait_ge(came, 48)
                for n in range(6 * HP):
                    dve.wait_ge(u_done, n + 1)
                    if n >= 2:
                        dve.wait_ge(u_used, n - 1)
                    for v in range(2):
                        dve.tensor_tensor(ur[:, n % 2, v, :].rearrange("p (b s) -> p b s", s=S),
                                          ps_g[:, n % 2, 0:HALF].rearrange("p (b s) -> p b s", s=S),
                                          rope[:, v, n % 3, :].unsqueeze(1).to_broadcast([128, B // 2, S]),
                                          ALU.mult).then_inc(u_ready, 1)


def latent_attention(nc, g, d, layer, q):
    G8 = NH * S
    GH = G8 // 2
    QTL = G8 // 128
    MAX_FROM = 2
    with ExitStack() as ctx:
        a = Alloc(nc, ctx, f"latent{layer}")
        rope = a.sb("rope", [KP, 2, KT, DC])
        raw = [a.sb(f"raw{u}", [KP, KT, DC]) for u in range(2)]
        turned_half = a.sb("turned_half", [KP, KT, DC])
        rows = [a.sb(f"rows{u}", [KP, KT, DC]) for u in range(2)]
        val = [a.sb(f"val{u}", [KP, KT, 128]) for u in range(2)]
        ropeT = a.sb("ropeT", [DC, 2, LK])
        rawT = [a.sb(f"rawT{u}", [DC, 2, LK]) for u in range(2)]
        kA = [a.sb(f"kA{u}", [128, LK], F32R) for u in range(2)]
        kB = [a.sb(f"kB{u}", [128, LK], F32R) for u in range(2)]
        qA = [a.sb(f"qA{u}", [128, G8], F32R) for u in range(2)]
        qB = [a.sb(f"qB{u}", [128, G8], F32R) for u in range(2)]
        w = [a.sb(f"w{u}", [KP, G8]) for u in range(2)]
        mx = a.sb("mx", [128, 2, QTL])
        osb = a.sb("osb", [128, G8])
        rec = a.sb("rec", [64, G8])
        psW = a.ps("psW", [128, 3, 512])
        psSO = a.ps("psSO", [128, 4, 512])
        psS, psO = psSO[:, 0:2, :], psSO[:, 2:4, :]
        raw_came = [a.sem(f"raw_came{u}") for u in range(2)]
        rawT_came = [a.sem(f"rawT_came{u}") for u in range(2)]
        names = ("tables", "tablesT", "filled", "ones", "roped", "val_ready", "productT", "ropedT", "first_keys", "hi_ready", "kA_ready", "kB_ready", "qA_ready", "qB_ready",
                 "max_scores", "max_ready", "row_turned", "row_ready", "scores_done", "exp_done", "av_done",
                 "o_copied", "rec_ready", "o_ready", "pool_chain")
        (tables, tablesT, filled, ones, roped, val_ready, productT, ropedT, first_keys, hi_ready, kA_ready, kB_ready, qA_ready, qB_ready,
         max_scores, max_ready, row_turned, row_ready, scores_done, exp_done, av_done,
         o_copied, rec_ready, o_ready, pool_chain) = (a.sem(n) for n in names)

        def each_batch(eng, body):
            body(0, 0)
            body(1, 1)
            with eng.Fori(1, B // 2 - 1) as i:
                body(2 * i, 0)
                body(2 * i + 1, 1)
            body(B - 2, 0)
            body(B - 1, 1)

        with nc.Block() as block:

            @block.sync
            def _(sp):
                ctx_rows = d["ctx"].rearrange("b (p n) -> p b n", p=KP)
                ctx_cols = d["ctx_cols"].rearrange("b (p n) -> p b n", p=DC)

                def load(b, u):
                    wait_from(sp, roped, b - 1)
                    sp.dma_start(raw[u][:, :, :].rearrange("p t e -> p (t e)"),
                                 ctx_rows[:, bass.ds(b, 1), :].rearrange("p b n -> p (b n)")).then_inc(raw_came[u], 16)
                    wait_from(sp, kA_ready, b - 1)
                    for to, v, at, n in ((0, 0, 0, DC), (0, 1, DC // 2, DC // 2), (DC // 2, 1, 0, DC // 2)):
                        sp.dma_start(rawT[u][to:to + n, v, :], ctx_cols[at:at + n, bass.ds(b, 1), :].rearrange("p b n -> p (b n)")).then_inc(rawT_came[u], 16)

                sp.dma_start(ropeT[:, :, :], d["rope_kT"].rearrange("(v p) n -> p v n", v=2)).then_inc(tablesT, 16)
                sp.dma_start(rope[:, :, :, :], d["rope_k"].rearrange("v p (t e) -> p v t e", t=KT)).then_inc(tables, 16)
                each_batch(sp, load)

            @block.gpsimd
            def _(pool):
                def rope_rows(b, u):
                    pool.wait_ge(raw_came[u], (b // 2 if isinstance(b, int) else (b - u) // 2) * 16 + 16)
                    wait_from(pool, val_ready, b - 1)
                    wait_from(pool, roped, b)
                    v = rows[u][:, :, :]
                    pool.tensor_tensor(v, raw[u][:, :, :], rope[:, 0, :, :], ALU.mult)
                    for lo, hi in ((0, 32), (32, 0)):
                        last = pool.tensor_tensor(turned_half[:, :, lo:lo + 32], raw[u][:, :, hi:hi + 32],
                                                  rope[:, 1, :, lo:lo + 32], ALU.mult)
                    last.then_inc(pool_chain, 1)
                    pool.wait_ge(pool_chain, b + 1)
                    pool.tensor_tensor(v, v, turned_half[:, :, :], ALU.add).then_inc(roped, 1)

                def rope_keys(b, u):
                    pool.wait_ge(rawT_came[u], (b // 2 if isinstance(b, int) else (b - u) // 2) * 48 + 48)
                    pool.tensor_tensor(rawT[u][:, :, :], rawT[u][:, :, :], ropeT[:, :, :], ALU.mult).then_inc(productT, 1)
                    pool.wait_ge(productT, b)
                    pool.tensor_tensor(rawT[u][:, 0, :], rawT[u][:, 0, :], rawT[u][:, 1, :], ALU.add).then_inc(ropedT, 1)

                def rope_batch(b, u):
                    if isinstance(b, int) and b == 0:
                        pool.wait_ge(tables, 16)
                        rope_rows(b, u)
                        for v in range(2):
                            pool.memset(val[v][:, :, DC:128], 1.0).then_inc(ones, 1)
                        pool.wait_ge(tablesT, 16)
                    else:
                        rope_keys(b, u)
                        rope_rows(b, u)

                each_batch(pool, rope_batch)

            @block.tensor
            def _(pe):
                def score_for_max(b, u, j, alone=False):
                    if j == 0:
                        wait_from(pe, row_ready, b)
                        pe.wait_ge(kA_ready, b + 1)
                        pe.wait_ge(qA_ready, b + 1)
                    else:
                        wait_from(pe, max_ready, b * QTL + j - (1 if alone else 0))
                    for m in range(3):
                        last = pe.matmul((psSO if alone and j % 2 else psW)[:, m, 0:500], qA[u][:, j * 128:(j + 1) * 128], kA[u][:, m * 500:(m + 1) * 500],
                                         start=True, stop=True)
                    last.then_inc(max_scores, 1)

                def turn_maxima(b, u):
                    pe.wait_ge(max_ready, b * QTL + QTL)
                    flat = psW[:, :, :].rearrange("p a n -> p (a n)")
                    for j in range(QTL):
                        last = pe.transpose(flat[0:1, j * 128:(j + 1) * 128], mx[:, u, j:j + 1], g.ident[:, :])
                    last.then_inc(row_turned, 1)

                def scores(b, u, t):
                    if t == 0:
                        pe.wait_ge(row_ready, b + 1)
                        pe.wait_ge(kB_ready, b + 1)
                        pe.wait_ge(qB_ready, b + 1)
                    wait_from(pe, exp_done, b * KT + t)
                    at = slice(t * KP, (t + 1) * KP)
                    for h in range(2):
                        pe.matmul(psS[0:KP, h, 0:GH], kA[u][:, at], qA[u][:, h * GH:(h + 1) * GH], start=True, stop=False)
                        last = pe.matmul(psS[0:KP, h, 0:GH], kB[u][:, at], qB[u][:, h * GH:(h + 1) * GH], start=False, stop=True)
                    last.then_inc(scores_done, 1)

                def attend(b, u, t):
                    pe.wait_ge(exp_done, b * KT + t + 1)
                    if t == 0:
                        pe.wait_ge(val_ready, b + 1)
                        pe.wait_ge(ones, 2)
                        wait_from(pe, o_copied, 2 * b)
                    for h in range(2):
                        last = pe.matmul(psO[:, h, 0:GH], val[u][:, t, :], w[t % 2][:, h * GH:(h + 1) * GH],
                                         start=(t == 0), stop=(t == KT - 1))
                    if t == KT - 1:
                        last.then_inc(av_done, 1)

                def batch(b, u):
                    ahead = not (isinstance(b, int) and b == B - 1)
                    for t in range(KT):
                        scores(b, u, t)
                        if t >= 1:
                            attend(b, u, t - 1)
                        elif not (isinstance(b, int) and b == 0):
                            attend(b - 1, 1 - u, KT - 1)
                        if ahead and MAX_FROM <= t < MAX_FROM + QTL:
                            score_for_max(b + 1, 1 - u, t - MAX_FROM)
                        if ahead and t == MAX_FROM + QTL:
                            turn_maxima(b + 1, 1 - u)

                for j in range(QTL):
                    score_for_max(0, 0, j, alone=True)
                turn_maxima(0, 0)
                each_batch(pe, batch)
                attend(B - 1, 1, KT - 1)

            @block.scalar
            def _(act):
                def copy_keys(b, u):
                    act.wait_ge(kA_ready, b + 1)
                    act.copy(kB[u][0:64, :], kA[u][0:64, :].bitcast(F32)).then_inc(kB_ready, 1)

                def take_maxima(b, u):
                    act.wait_ge(row_turned, b + 1)
                    act.wait_ge(filled, 4)
                    act.mul(qB[u][64:65, :], psW[:, :, :].rearrange("p a n -> p (a n)")[0:1, 0:G8], -1.0).then_inc(row_ready, 1)

                def copy_values(b, u):
                    act.wait_ge(roped, b + 1)
                    act.copy(val[u][:, :, 0:DC], rows[u][:, :, :]).then_inc(val_ready, 1)

                def take_attended(b):
                    act.wait_ge(av_done, b + 1)
                    wait_from(act, o_ready, 2 * b)
                    act.copy(osb[:, 0:GH], psO[:, 0, 0:GH]).then_inc(o_copied, 1)

                def exp(b, u, t):
                    act.wait_ge(scores_done, b * KT + t + 1)
                    act.activation(w[t % 2][:, :].rearrange("p (h n) -> p h n", h=2), psS[0:KP, :, 0:GH],
                                   ACT.Exp).then_inc(exp_done, 1)

                def batch(b, u):
                    ahead = not (isinstance(b, int) and b == B - 1)
                    for t in range(KT):
                        exp(b, u, t)
                        if t == 0 and not (isinstance(b, int) and b == 0):
                            take_attended(b - 1)
                        if ahead and t == 2:
                            copy_keys(b + 1, 1 - u)
                        if ahead and t == 3:
                            copy_values(b + 1, 1 - u)
                        if ahead and t == MAX_FROM + QTL:
                            take_maxima(b + 1, 1 - u)

                copy_values(0, 0)
                copy_keys(0, 0)
                take_maxima(0, 0)
                each_batch(act, batch)
                take_attended(B - 1)

            @block.vector
            def _(dve):
                for u in range(2):
                    dve.memset(kB[u][64:128, :].bitcast(F32), 0.0).then_inc(filled, 1)
                    dve.memset(qB[u][64:128, :].bitcast(F32), 0.0).then_inc(filled, 1)
                dve.wait_ge(filled, 4)
                for u in range(2):
                    dve.memset(kB[u][64:65, :].bitcast(F32), 1.0).then_inc(filled, 1)

                def split_keys(b, u):
                    wait_from(dve, ropedT, b)
                    wait_from(dve, scores_done, (b - 1) * KT)
                    wait_from(dve, kB_ready, b - 1)
                    dve.tensor_copy(kA[u][0:64, :], rawT[u][:, 0, :]).then_inc(hi_ready, 1)
                    dve.wait_ge(hi_ready, b + 1)
                    dve.tensor_tensor(kA[u][64:128, :], rawT[u][:, 0, :], kA[u][0:64, :].bitcast(F32), ALU.subtract).then_inc(kA_ready, 1)

                def spread_queries(b, u):
                    for e in range(2):
                        src = q[e * 64:e * 64 + 64, :, bass.ds(b * S, S)]
                        for r in range(2):
                            last = dve.tensor_copy(qA[u][r * 64:r * 64 + 64, :].rearrange("p (j e s) -> p j e s", e=2, s=S)[:, :, e, :], src)
                    last.then_inc(qA_ready, 1)

                def split_queries(b, u):
                    dve.wait_ge(qA_ready, b + 1)
                    for e in range(2):
                        hi = qA[u][e * 64:e * 64 + 64, :].rearrange("p (j e s) -> p j e s", e=2, s=S)[:, :, e, :]
                        last = dve.tensor_tensor(qB[u][0:64, :].rearrange("p (j e s) -> p j e s", e=2, s=S)[:, :, e, :],
                                                 q[e * 64:e * 64 + 64, :, bass.ds(b * S, S)], hi.bitcast(F32), ALU.subtract)
                    last.then_inc(qB_ready, 1)

                def maximum(b, u, j, alone=False):
                    dve.wait_ge(max_scores, b * QTL + j + 1)
                    dve.tensor_reduce(mx[:, u, j:j + 1], (psSO if alone and j % 2 else psW)[:, 0:3, 0:500], mybir.AxisListType.XY, ALU.max).then_inc(max_ready, 1)

                def empty(b):
                    dve.wait_ge(av_done, b + 1)
                    wait_from(dve, o_ready, 2 * b)
                    dve.tensor_copy(osb[:, GH:G8], psO[:, 1, 0:GH]).then_inc(o_copied, 1)

                def invert(b, j):
                    at = slice(j * 128, (j + 1) * 128)
                    if j == 0:
                        dve.wait_ge(o_copied, 2 * b + 2)
                    dve.reciprocal(rec[:, at], osb[64:128, at]).then_inc(rec_ready, 1)

                def normalise(b):
                    dve.wait_ge(rec_ready, (b + 1) * QTL)
                    for e in range(2):
                        pick = lambda v: v.rearrange("p (j e s) -> p j e s", e=2, s=S)[:, :, e, :]
                        dve.tensor_tensor(q[e * 64:e * 64 + 64, :, bass.ds(b * S, S)], pick(osb[0:64, :]), pick(rec[:, :]),
                                          ALU.mult).then_inc(o_ready, 1)

                def batch(b, u):
                    first = isinstance(b, int) and b == 0
                    ahead = not (isinstance(b, int) and b == B - 1)
                    if not first:
                        empty(b - 1)
                    if ahead:
                        split_keys(b + 1, 1 - u)
                        spread_queries(b + 1, 1 - u)
                    for j in range(QTL):
                        if ahead:
                            maximum(b + 1, 1 - u, j)
                        if not first:
                            invert(b - 1, j)
                    if ahead:
                        split_queries(b + 1, 1 - u)
                    if not first:
                        normalise(b - 1)

                dve.wait_ge(rawT_came[0], 48)
                dve.wait_ge(tablesT, 16)
                dve.tensor_tensor(rawT[0][:, :, :], rawT[0][:, :, :], ropeT[:, :, :], ALU.mult).then_inc(first_keys, 1)
                dve.wait_ge(first_keys, 1)
                dve.tensor_tensor(rawT[0][:, 0, :], rawT[0][:, 0, :], rawT[0][:, 1, :], ALU.add).then_inc(first_keys, 1)
                dve.wait_ge(first_keys, 2)
                split_keys(0, 0)
                spread_queries(0, 0)
                for j in range(QTL):
                    maximum(0, 0, j, alone=True)
                split_queries(0, 0)
                each_batch(dve, batch)
                empty(B - 1)
                for j in range(QTL):
                    invert(B - 1, j)
                normalise(B - 1)


def latent_output(nc, g, layer, q, fold):
    gate = g.gates[0:TP, layer:layer + 1]
    with ExitStack() as ctx:
        a = Alloc(nc, ctx, f"out{layer}")
        ps = a.ps("ps", [128, 2, 512])
        y_done, x_done = a.sem("y_done"), a.sem("x_done")
        with nc.Block() as block:

            @block.tensor
            def _(pe):
                for t in range(NT):
                    if t >= 2:
                        pe.wait_ge(x_done, t - 1)
                    for j in range(HP):
                        last = pe.matmul(ps[0:TP, t % 2, 0:C], q[:, j, t * TP:(t + 1) * TP], fold[:, j, :],
                                         start=(j == 0), stop=(j == HP - 1))
                    last.then_inc(y_done, 1)

            @block.vector
            def _(dve):
                for t in range(NT):
                    dve.wait_ge(y_done, t + 1)
                    dve.scalar_tensor_tensor(out=g.x[:, t, :], in0=ps[0:TP, t % 2, 0:C], scalar=gate, in1=g.x[:, t, :],
                                             op0=ALU.mult, op1=ALU.add).then_inc(x_done, 1)


def latent_layer(nc, g, d, layer, queries):
    with ExitStack() as ctx:
        a = Alloc(nc, ctx, f"layer{layer}")
        q = a.sb("q", [128, HP, T])
        fold = a.sb("fold", [128, HP, C])
        queries(nc, g, d, q, fold)
        latent_attention(nc, g, d, layer, q)
        latent_output(nc, g, layer, q, fold)



def butterflies(eng, step, v, w, done):
    src, dst = v, w
    for h in (4, 2, 1):
        pick = lambda t, k: t.rearrange("p (a u h) n -> p u a h n", u=2, h=h)[:, k, :, :, :]
        step(eng.tensor_tensor(pick(dst, 0), pick(src, 0), pick(src, 1), ALU.add))
        last = eng.tensor_tensor(pick(dst, 1), pick(src, 0), pick(src, 1), ALU.subtract)
        if h > 1:
            step(last)
        src, dst = dst, src
    last.then_inc(done, 1)


def ternary_ffn(nc, g, d):
    gate = g.gates[0:TP, 5:6]
    NF = FF // 128
    with ExitStack() as ctx:
        a = Alloc(nc, ctx, "ffn1")
        wf = a.sb("wf", [128, 3, 2 * FF])
        wb = a.sb("wb", [128, 3, 2 * FF], BF16)
        had256 = a.sb("had256", [128, CC, C])
        had128 = a.sb("had128", [128, 128])
        identb = a.sb("identb", [128, 128], BF16)
        onesm = a.sb("onesm", [128, 128])
        su_ready = a.sem("su_ready")
        part = a.sb("part", [48, 3])
        ws = a.sb("ws", [128, 3])
        rws = a.sb("rws", [128, 3])
        xh = a.sb("xh", [TP, NT, C])
        xq = a.sb("xq", [TP, NT, C], BF16)
        xqT = a.sb("xqT", [128, CC, T], BF16)
        sx = a.sb("sx", [TP, NT])
        rx = a.sb("rx", [TP, NT])
        su = a.sb("su", [TP, 2, NT])
        s2 = a.sb("s2", [TP, NT])
        r2 = a.sb("r2", [TP, NT])
        h = a.sb("h", [TP, 2, FF])
        h2 = a.sb("h2", [TP, 2, FF])
        hT = a.sb("hT", [128, NF, TP])
        yq = a.sb("yq", [TP, FF], BF16)
        yqT = a.sb("yqT", [128, NF, TP], BF16)
        ps_gu = a.ps("ps_gu", [128, 4, 512])
        ps_t = a.ps("ps_t", [128, 2, 512])
        ps_y = a.ps("ps_y", [128, 2, 512])
        norm = Norm(nc, a, g, ps_t)
        came, came_w = a.sem("came"), a.sem("came_w")
        (ready, sums, w_ready, xh_done, xh_taken, xq_ready, xq_turned, xqT_ready, gu_done, silu_done, product_done, h_ready,
         h_turned, hT_ready, y_done, yq_ready, yq_turned, yqT_ready, o_done, x_done, pool_chain, chain) = (
            a.sem(n) for n in ("ready", "sums", "w_ready", "xh_done", "xh_taken", "xq_ready", "xq_turned", "xqT_ready",
                               "gu_done", "silu_done", "product_done", "h_ready", "h_turned", "hT_ready", "y_done", "yq_ready",
                               "yq_turned", "yqT_ready", "o_done", "x_done", "pool_chain", "dve_chain"))
        with nc.Block() as block:

            @block.sync
            def _(sp):
                sp.dma_start(wf[:, 0, :].rearrange("p (c n) -> p c n", c=CC), d["L1_gate"].rearrange("(c p) n -> p c n", p=128)).then_inc(came_w, 16)
                sp.dma_start(wf[:, 1, :].rearrange("p (c n) -> p c n", c=CC), d["L1_up"].rearrange("(c p) n -> p c n", p=128)).then_inc(came_w, 16)
                sp.dma_start(wf[:, 2, :].rearrange("p (c n) -> p c n", c=NF), d["L1_down"].rearrange("(c p) n -> p c n", p=128)).then_inc(came_w, 16)
                sp.dma_start(had256[:, :, :], d["had256"].rearrange("(c p) n -> p c n", p=128)).then_inc(came, 16)
                sp.dma_start(had128[:, :], d["had128"]).then_inc(came, 16)
                sp.dma_start(part[:, :], d["lanes"]).then_inc(came, 16)

            @block.gpsimd
            def _(pool):
                pool.memset(onesm[:, :], 1.0).then_inc(ready, 1)
                pool.tensor_copy(identb[:, :], g.ident[:, :]).then_inc(ready, 1)
                step = Chain(pool, pool_chain)
                for t in range(NT):
                    pool.wait_ge(product_done, t + 1)
                    if t >= 2:
                        pool.wait_ge(h_turned, t - 1)
                    v, w = (z[:, t % 2, :].rearrange("p (k n) -> p k n", n=128) for z in (h, h2))
                    butterflies(pool, step, v, w, h_ready)

            @block.tensor
            def _(pe):
                pe.wait_ge(ready, 3)
                pe.matmul(ps_gu[:, 0, 0:3], onesm[0:48, :], part[:, :], start=True, stop=True).then_inc(sums, 1)
                norm.tensor(pe)
                pe.wait_ge(came, 48)
                for t in range(NT):
                    pe.wait_ge(norm.xnT_ready, t + 1)
                    if t >= 2:
                        pe.wait_ge(xh_taken, t - 1)
                    for c in range(CC):
                        last = pe.matmul(ps_y[0:TP, t % 2, 0:C], g.xnT[:, c, t * TP:(t + 1) * TP], had256[:, c, :],
                                         start=(c == 0), stop=(c == CC - 1))
                    last.then_inc(xh_done, 1)
                pe.wait_ge(xq_ready, 1)
                for t in range(NT):
                    if t >= 2:
                        pe.wait_ge(xqT_ready, t - 1)
                    tb = ps_t[:, t % 2, :].bitcast(BF16)
                    for c in range(CC):
                        last = pe.transpose(tb[:, c * TP:(c + 1) * TP], xq[:, t, c * 128:(c + 1) * 128], identb[0:TP, 0:TP])
                    last.then_inc(xq_turned, 1)
                pe.wait_ge(xqT_ready, NT)
                pe.wait_ge(w_ready, 2)

                def inner(t, n):
                    if t >= 1 and n == 0:
                        pe.wait_ge(product_done, t)
                    for m in range(2):
                        for c in range(CC):
                            last = pe.matmul(ps_gu[0:TP, 2 * m + n, :], xqT[:, c, t * TP:(t + 1) * TP],
                                             wb[:, m, c * FF + n * 512:c * FF + n * 512 + 512],
                                             start=(c == 0), stop=(c == CC - 1))
                    if n == 1:
                        last.then_inc(gu_done, 1)

                def turn_h(t):
                    pe.wait_ge(h_ready, t + 1)
                    if t >= 2:
                        pe.wait_ge(yqT_ready, t - 1)
                        pe.wait_ge(x_done, t - 1)
                    for k in range(NF):
                        last = pe.transpose(ps_t[:, k // 4, (k % 4) * TP:(k % 4 + 1) * TP], h2[:, t % 2, k * 128:(k + 1) * 128],
                                            g.ident[0:TP, 0:TP])
                    last.then_inc(h_turned, 1)

                def rotate(t):
                    pe.wait_ge(hT_ready, t + 1)
                    if t >= 1:
                        pe.wait_ge(yq_ready, t)
                    for k in range(NF):
                        last = pe.matmul(ps_y[0:TP, k // 4, (k % 4) * 128:(k % 4 + 1) * 128], hT[:, k, :], had128[:, :],
                                         start=True, stop=True)
                    last.then_inc(y_done, 1)

                def turn_quantised(t):
                    pe.wait_ge(yq_ready, t + 1)
                    pe.wait_ge(hT_ready, min(t + 2, NT))
                    tb = ps_t[:, 0, :].bitcast(BF16)
                    for k in range(NF):
                        last = pe.transpose(tb[:, k * TP:(k + 1) * TP], yq[:, k * 128:(k + 1) * 128], identb[0:TP, 0:TP])
                    last.then_inc(yq_turned, 1)

                def down(t):
                    if t == 0:
                        pe.wait_ge(w_ready, 3)
                    if t == NT - 1:
                        pe.wait_ge(x_done, t)
                    pe.wait_ge(yqT_ready, t + 1)
                    for k in range(NF):
                        last = pe.matmul(ps_t[0:TP, 1, 0:C], yqT[:, k, :], wb[:, 2, k * C:(k + 1) * C],
                                         start=(k == 0), stop=(k == NF - 1))
                    last.then_inc(o_done, 1)

                for i in range(NT + 3):
                    if i < NT:
                        inner(i, 0)
                    if 2 <= i < NT + 2:
                        turn_h(i - 2)
                    if i < NT:
                        inner(i, 1)
                    if i >= 3:
                        turn_quantised(i - 3)
                    if 2 <= i < NT + 2:
                        rotate(i - 2)
                    if i >= 3:
                        down(i - 3)

            @block.scalar
            def _(act):
                norm.scalar(act)
                for t in range(NT):
                    act.wait_ge(xh_done, t + 1)
                    act.copy(xh[:, t, :], ps_y[0:TP, t % 2, 0:C]).then_inc(xh_taken, 1)
                for t in range(NT):
                    act.wait_ge(xq_turned, t + 1)
                    act.copy(xqT[:, :, t * TP:(t + 1) * TP],
                             ps_t[:, t % 2, :].bitcast(BF16)[:, 0:2 * TP].rearrange("p (c n) -> p c n", c=CC)).then_inc(xqT_ready, 1)

                def silu(t):
                    act.wait_ge(gu_done, t + 1)
                    if t >= 2:
                        act.wait_ge(h_ready, t - 1)
                    act.activation(h[:, t % 2, :].rearrange("p (n m) -> p n m", n=2), ps_gu[0:TP, 0:2, :], ACT.Silu,
                                   scale=su[:, 0, t:t + 1]).then_inc(silu_done, 1)

                def take_h(t):
                    act.wait_ge(h_turned, t + 1)
                    if t >= 1:
                        act.wait_ge(y_done, t)
                    act.copy(hT[:, :, :].rearrange("p (u k) n -> p u (k n)", u=2), ps_t[:, :, 0:4 * TP]).then_inc(hT_ready, 1)

                def take_quantised(t):
                    act.wait_ge(yq_turned, t + 1)
                    if t >= 1:
                        act.wait_ge(o_done, t)
                    act.copy(yqT[:, :, :].rearrange("p k n -> p (k n)"), ps_t[:, 0, :].bitcast(BF16)[:, 0:NF * TP]).then_inc(yqT_ready, 1)

                act.wait_ge(w_ready, 2)
                act.wait_ge(su_ready, 1)
                for i in range(NT + 3):
                    if 2 <= i < NT + 2:
                        take_h(i - 2)
                    if i < NT:
                        silu(i)
                    if i >= 3:
                        take_quantised(i - 3)

            @block.vector
            def _(dve):
                step = Chain(dve, chain)
                norm.vector(dve)
                dve.wait_ge(came_w, 48)
                dve.wait_ge(came, 48)
                dve.tensor_scalar(part[:, :], part[:, :], g.magnitudes[:, :], None, ALU.mult).then_inc(ready, 1)
                dve.wait_ge(sums, 1)
                step(dve.tensor_scalar(ws[:, :], ps_gu[:, 0, 0:3], 1.0 / (FF * C), 1e-5, ALU.mult, ALU.max))
                step(dve.reciprocal(rws[:, :], ws[:, :]))

                def quantise_weights(m):
                    step(dve.tensor_scalar(wf[:, m, :], wf[:, m, :], rws[:, m:m + 1], 1.0, ALU.mult, ALU.min))
                    step(dve.tensor_scalar(wf[:, m, :], wf[:, m, :], -1.0, ROUND, ALU.max, ALU.add))
                    dve.tensor_scalar(wb[:, m, :], wf[:, m, :], -ROUND, None, ALU.add).then_inc(w_ready, 1)

                def quantise_scales(s, r, most, root):
                    step(dve.tensor_scalar(s, most, 1.0 / root, 1e-5, ALU.mult, ALU.max))
                    step(dve.reciprocal(r, s))
                    step(dve.tensor_scalar(r, r, 127.0, 1.0 / root, ALU.mult, ALU.mult))
                    step(dve.tensor_scalar(s, s, 1.0 / 127.0, None, ALU.mult))

                quantise_weights(0)
                quantise_weights(1)
                dve.wait_ge(xh_taken, NT)
                step(dve.tensor_reduce(rx[:, :], xh[:, :, :], X, ALU.max, apply_absolute_value=True))
                quantise_scales(sx[:, :], rx[:, :], rx[:, :], 16.0)
                step(dve.tensor_tensor(xh[:, :, :], xh[:, :, :], rx[:, :].unsqueeze(2).to_broadcast([TP, NT, C]), ALU.mult))
                step(dve.tensor_scalar(xh[:, :, :], xh[:, :, :], 127.0, -128.0, ALU.min, ALU.max))
                dve.tensor_scalar(xq[:, :, :], xh[:, :, :], ROUND, -ROUND, ALU.add, ALU.add).then_inc(xq_ready, 1)
                for m in range(2):
                    last = dve.tensor_scalar(su[:, m, :], sx[:, :], ws[0:TP, m:m + 1], None, ALU.mult)
                last.then_inc(su_ready, 1)
                dve.wait_ge(su_ready, 1)
                step(dve.tensor_scalar(ws[:, 2:3], ws[:, 2:3], g.gates[:, 5:6], None, ALU.mult))

                def product(t):
                    u = t % 2
                    dve.wait_ge(silu_done, t + 1)
                    dve.scalar_tensor_tensor(out=h[:, u, :].rearrange("p (n m) -> p n m", n=2), in0=ps_gu[0:TP, 2:4, :],
                                             scalar=su[:, 1, t:t + 1], in1=h[:, u, :].rearrange("p (n m) -> p n m", n=2),
                                             op0=ALU.mult, op1=ALU.mult).then_inc(product_done, 1)

                def quantise(t):
                    at = slice(t, t + 1)
                    dve.wait_ge(y_done, t + 1)
                    step(dve.tensor_reduce(r2[:, at], ps_y[0:TP, :, :], mybir.AxisListType.XY, ALU.max, apply_absolute_value=True))
                    quantise_scales(s2[:, at], r2[:, at], r2[:, at], 32.0)
                    step(dve.tensor_scalar(s2[:, at], s2[:, at], ws[0:TP, 2:3], None, ALU.mult))
                    wide = xh[:, 0:4, :].rearrange("p a n -> p (a n)")
                    step(dve.tensor_scalar(wide.rearrange("p (a n) -> p a n", a=2), ps_y[0:TP, :, :], r2[:, at], 127.0, ALU.mult, ALU.min))
                    step(dve.tensor_scalar(wide, wide, -128.0, ROUND, ALU.max, ALU.add))
                    if t >= 1:
                        dve.wait_ge(yq_turned, t)
                    dve.tensor_scalar(yq[:, :], wide, -ROUND, None, ALU.add).then_inc(yq_ready, 1)

                def add(t):
                    dve.wait_ge(o_done, t + 1)
                    dve.scalar_tensor_tensor(out=g.x[:, t, :], in0=ps_t[0:TP, 1, 0:C], scalar=s2[:, t:t + 1], in1=g.x[:, t, :],
                                             op0=ALU.mult, op1=ALU.add).then_inc(x_done, 1)

                for i in range(NT + 3):
                    if i < NT:
                        product(i)
                    if i == 1:
                        quantise_weights(2)
                    if i >= 3:
                        add(i - 3)
                    if 2 <= i < NT + 2:
                        quantise(i - 2)


def hadamard_ffn(nc, g, d):
    gate = g.gates[0:TP, 6:7]
    NF = FF // 128
    with ExitStack() as ctx:
        a = Alloc(nc, ctx, "ffn2")
        had256 = a.sb("had256", [128, CC, C])
        had128 = a.sb("had128", [128, 128])
        su_ug = a.sb("su_ug", [128, CC])
        su_dp = a.sb("su_dp", [128, NF])
        sc_ug = a.sb("sc_ug", [128, 2 * NF])
        sc_dp = a.sb("sc_dp", [128, C])
        wu = a.sb("wu", [128, CC, FF])
        wg = a.sb("wg", [128, CC, FF])
        wd = a.sb("wd", [128, NF, C])
        wd2 = a.sb("wd2", [128, NF, C])
        xr = a.sb("xr", [128, CC, T])
        s = a.sb("s", [128, 2, HALF])
        hT = a.sb("hT", [128, NF, T])
        ps_u = a.ps("ps_u", [128, 2, 512])
        ps_g = a.ps("ps_g", [128, 2, 512])
        ps_d = a.ps("ps_d", [128, 2, 512])
        norm = Norm(nc, a, g)
        came = a.sem("came")
        (had_ready, wd_ready, fold_done, fold_ready, xr_done, xr_ready, u_done, g_done, s_ready, h_ready, y_done, x_done,
         pool_chain, chain) = (a.sem(n) for n in ("had_ready", "wd_ready", "fold_done", "fold_ready", "xr_done", "xr_ready",
                                                  "u_done", "g_done", "s_ready", "h_ready", "y_done", "x_done", "pool_chain", "dve_chain"))
        with nc.Block() as block:

            @block.sync
            def _(sp):
                chunks = lambda v: v.rearrange("(c p) n -> p c n", p=128)
                for dst, src in ((wd[:, :, :], chunks(d["L2_down"])), (had128[:, :], d["had128"]), (had256[:, :, :], chunks(d["had256"])),
                                 (su_ug[:, :], d["L2_su_ug"]), (su_dp[:, :], d["L2_su_dp"]), (sc_ug[:, :], d["L2_sc_ug"]),
                                 (sc_dp[:, :], d["L2_sc_dp"].partition_broadcast(128)),
                                 (wu[:, :, :], chunks(d["L2_up"])), (wg[:, :, :], chunks(d["L2_gate"]))):
                    sp.dma_start(dst, src).then_inc(came, 16)

            @block.gpsimd
            def _(pool):
                pool.wait_ge(came, 144)
                butterflies(pool, Chain(pool, pool_chain), wd[:, :, :], wd2[:, :, :], wd_ready)

            @block.tensor
            def _(pe):
                pe.wait_ge(wd_ready, 1)
                for k in range(NF):
                    if k >= 2:
                        pe.wait_ge(fold_ready, k - 1)
                    pe.matmul(ps_d[:, k % 2, 0:C], had128[:, :], wd2[:, k, :], start=True, stop=True).then_inc(fold_done, 1)
                norm.tensor(pe)
                pe.wait_ge(norm.xnT_ready, NT)
                pe.wait_ge(had_ready, CC)
                for n in range(4):
                    m, h = n // 2, n % 2
                    if n >= 2:
                        pe.wait_ge(xr_ready, n - 1)
                    for c in range(CC):
                        last = pe.matmul(ps_u[:, n % 2, 0:HALF], had256[:, c, m * 128:(m + 1) * 128],
                                         g.xnT[:, c, h * HALF:(h + 1) * HALF], start=(c == 0), stop=(c == CC - 1))
                    last.then_inc(xr_done, 1)
                pe.wait_ge(xr_ready, 4)
                for n in range(2 * NF):
                    m, h = n // 2, n % 2
                    if n >= 2:
                        pe.wait_ge(h_ready, n - 1)
                    for w, ps, done in ((wg, ps_g, g_done), (wu, ps_u, u_done)):
                        for c in range(CC):
                            last = pe.matmul(ps[:, n % 2, 0:HALF], w[:, c, m * 128:(m + 1) * 128],
                                             xr[:, c, h * HALF:(h + 1) * HALF], start=(c == 0), stop=(c == CC - 1))
                        last.then_inc(done, 1)
                pe.wait_ge(fold_ready, NF)
                pe.wait_ge(h_ready, 2 * NF)
                for t in range(NT):
                    if t >= 2:
                        pe.wait_ge(x_done, t - 1)
                    for k in range(NF):
                        last = pe.matmul(ps_d[0:TP, t % 2, 0:C], hT[:, k, t * TP:(t + 1) * TP], wd[:, k, :],
                                         start=(k == 0), stop=(k == NF - 1))
                    last.then_inc(y_done, 1)

            @block.scalar
            def _(act):
                norm.scalar(act)
                for n in range(4):
                    m, h = n // 2, n % 2
                    act.wait_ge(xr_done, n + 1)
                    act.copy(xr[:, m, h * HALF:(h + 1) * HALF], ps_u[:, n % 2, 0:HALF]).then_inc(xr_ready, 1)
                act.wait_ge(had_ready, CC + 2)
                for n in range(2 * NF):
                    act.wait_ge(g_done, n + 1)
                    if n >= 2:
                        act.wait_ge(h_ready, n - 1)
                    act.activation(s[:, n % 2, :], ps_g[:, n % 2, 0:HALF], ACT.Silu, scale=sc_ug[:, NF + n // 2:NF + n // 2 + 1]).then_inc(s_ready, 1)

            @block.vector
            def _(dve):
                step = Chain(dve, chain)
                dve.wait_ge(came, 144)
                for c in range(CC):
                    dve.tensor_scalar(had256[:, c, :], had256[:, c, :], su_ug[:, c:c + 1], None, ALU.mult).then_inc(had_ready, 1)
                step(dve.tensor_scalar(sc_ug[:, :], sc_ug[:, :], 1.0 / 16.0, None, ALU.mult))
                dve.tensor_tensor(sc_ug[:, 0:NF], sc_ug[:, 0:NF], su_dp[:, :], ALU.mult).then_inc(had_ready, 1)
                dve.tensor_scalar(sc_dp[:, :], sc_dp[:, :], 1.0 / 32.0, None, ALU.mult).then_inc(had_ready, 1)
                dve.wait_ge(had_ready, CC + 2)
                for k in range(NF):
                    dve.wait_ge(fold_done, k + 1)
                    dve.tensor_tensor(wd[:, k, :], ps_d[:, k % 2, 0:C], sc_dp[:, :], ALU.mult).then_inc(fold_ready, 1)
                norm.vector(dve)
                dve.wait_ge(wd_ready, 1)
                for n in range(2 * NF):
                    m, h = n // 2, n % 2
                    dve.wait_ge(s_ready, n + 1)
                    dve.wait_ge(u_done, n + 1)
                    dve.scalar_tensor_tensor(out=hT[:, m, h * HALF:(h + 1) * HALF], in0=ps_u[:, n % 2, 0:HALF], scalar=sc_ug[:, m:m + 1],
                                             in1=s[:, n % 2, :], op0=ALU.mult, op1=ALU.mult).then_inc(h_ready, 1)
                for t in range(NT):
                    dve.wait_ge(y_done, t + 1)
                    dve.scalar_tensor_tensor(out=g.x[:, t, :], in0=ps_d[0:TP, t % 2, 0:C], scalar=gate, in1=g.x[:, t, :],
                                             op0=ALU.mult, op1=ALU.add).then_inc(x_done, 1)


def experts_weights(nc, g):
    a = Alloc(nc, g.ctx, "experts")
    g.wgu = a.sb("wgu", [128, NE, CC, 2 * F3])
    g.wgu_came = a.sem("wgu_came")


def load_experts(g, d, sp):
    for e in range(NE):
        sp.dma_start(g.wgu[:, e, :, :], d["L3_gu"][e].rearrange("(c p) n -> p c n", p=128)).then_inc(g.wgu_came, 16)


def experts_ffn(nc, g, d):
    F4 = F3 // 128
    gate = g.gates[0:TP, 7:8]
    with ExitStack() as ctx:
        a = Alloc(nc, ctx, "ffn3")
        rw = a.sb("rw", [128, CC, NE])
        later = a.sb("later", [128, NE])
        before = a.sb("before", [TP, TP])
        numbers = a.sb("numbers", [1, SLOT_TILES])
        ones = a.sb("ones", [TP, TP])
        lg = a.sb("lg", [TP, NT, NE])
        own = a.sb("own", [TP, NT, NE])
        top = a.sb("top", [TP, NT])
        first = a.sb("first", [TP, NT])
        cum = a.sb("cum", [TP, NT + 1, NE])
        tiles = a.sb("tiles", [TP, NE])
        ends = a.sb("ends", [TP, NE])
        base = a.sb("base", [TP, NE])
        slot = a.sb("slot", [TP, NT], mybir.dt.int32)
        passed = a.sb("passed", [1, SLOT_TILES, NE])
        of_tile = a.sb("of_tile", [1, SLOT_TILES])
        of_tile_i = a.sb("of_tile_i", [1, SLOT_TILES], mybir.dt.int32)
        sg = a.sb("sg", [TP, NT])
        wdn = a.sb("wdn", [128, NE, F4, C])
        wsgu = a.sb("wsgu", [128, CC, 2 * F3])
        wsdn = a.sb("wsdn", [128, F4, C])
        s = a.sb("s", [128, 2, 512])
        hT = a.sb("hT", [128, F4, T])
        rows = a.sb("rows", [128, SLOT_TILES, C])
        xT = a.sb("xT", [128, 2, CC, 128])
        inner = a.sb("inner", [128, 2, F3])
        innerT = a.sb("innerT", [128, 2, F4, 128])
        norm = Norm(nc, a, g)
        ps_d = a.ps("ps_d", [128, 2, 512])
        ps_u = a.ps("ps_u", [128, 2, 512])
        ps_g = a.ps("ps_g", [128, 2, 512])
        ps_t = norm.turned
        (came, shared_came, wdn_came, cleared, zero_stored, l_done, top_ready, sg_ready, xs_ready, own_ready, places_done,
         slots_ready, scattered, first_came, rest_came, g_done, u_done, s_ready, h_ready, turned, xT_ready, gate_done, up_done,
         silu_done, inner_ready, inner_turned, innerT_ready, down_done, y_ready, y_stored, o_done, x_done, chain) = (
            a.sem(n) for n in ("came", "shared_came", "wdn_came", "cleared", "zero_stored", "l_done", "top_ready", "sg_ready",
                               "xs_ready", "own_ready", "places_done", "slots_ready", "scattered", "first_came", "rest_came",
                               "g_done", "u_done", "s_ready", "h_ready", "turned", "xT_ready", "gate_done", "up_done", "silu_done",
                               "inner_ready", "inner_turned", "innerT_ready", "down_done", "y_ready", "y_stored", "o_done", "x_done", "dve_chain"))
        gathered = [a.sem(f"gathered{t}") for t in range(NT)]
        sorted_x = nc.dram_tensor("sorted_x", (SLOT_TILES * 128, C), F32).ap()
        sorted_y = nc.dram_tensor("sorted_y", (SLOT_TILES * 128, C), F32).ap()
        tiled = lambda v: v.rearrange("(j p) c -> p j c", p=128)
        UNITS = 2 * F4
        with nc.Block() as block:

            @block.sync
            def _(sp):
                sp.dma_start(rw[:, :, :], d["L3_rw"].rearrange("(c p) n -> p c n", p=128)).then_inc(came, 16)
                sp.dma_start(later[:, :], d["later"]).then_inc(came, 16)
                sp.dma_start(before[:, :], d["before"]).then_inc(came, 16)
                sp.dma_start(numbers[:, :], d["numbers"]).then_inc(came, 16)
                sp.dma_start(wsgu[:, :, :], d["L3_sgu"].rearrange("(c p) n -> p c n", p=128)).then_inc(shared_came, 16)
                sp.dma_start(wsdn[:, :, :], d["L3_sdn"].rearrange("(c p) n -> p c n", p=128)).then_inc(shared_came, 16)
                sp.wait_ge(cleared, 2)
                sp.dma_start(tiled(sorted_x), rows[:, :, :]).then_inc(zero_stored, 16)
                for e in range(NE):
                    sp.dma_start(wdn[:, e, :, :], d["L3_dn"][e].rearrange("(c p) n -> p c n", p=128)).then_inc(wdn_came, 16)
                sp.wait_ge(scattered, 16 * NT)
                sp.dma_start(rows[:, 0:2, :], tiled(sorted_x)[:, 0:2, :]).then_inc(first_came, 16)
                sp.dma_start(rows[:, 2:, :], tiled(sorted_x)[:, 2:, :]).then_inc(rest_came, 16)
                for j in range(SLOT_TILES):
                    sp.wait_ge(y_ready, j + 1)
                    sp.dma_start(tiled(sorted_y)[:, j, :], rows[:, j, :]).then_inc(y_stored, 16)

            @block.gpsimd
            def _(pool):
                pool.memset(ones[:, :], 1.0).then_inc(cleared, 1)
                pool.memset(rows[:, :, :], 0.0).then_inc(cleared, 1)
                pool.wait_ge(zero_stored, 16)
                pool.wait_ge(xs_ready, NT)
                pool.wait_ge(slots_ready, 1)
                for t in range(NT):
                    pool.indirect_dma_start(out=sorted_x, out_offset=bass.IndirectOffsetOnAxis(ap=slot[:, t:t + 1], axis=0),
                                            in_=g.xn[:, t, :], in_offset=None).then_inc(scattered, 16)
                pool.wait_ge(y_stored, 16 * SLOT_TILES)
                for t in range(NT):
                    pool.indirect_dma_start(out=g.xn[:, t, :], out_offset=None, in_=sorted_y,
                                            in_offset=bass.IndirectOffsetOnAxis(ap=slot[:, t:t + 1], axis=0)).then_inc(gathered[t], 16)

            @block.tensor
            def _(pe):
                norm.tensor(pe)
                pe.wait_ge(came, 64)
                for t in range(NT):
                    pe.wait_ge(norm.xnT_ready, t + 1)
                    for c in range(CC):
                        last = pe.matmul(ps_d[0:TP, 0, t * NE:(t + 1) * NE], g.xnT[:, c, t * TP:(t + 1) * TP], rw[:, c, :],
                                         start=(c == 0), stop=(c == CC - 1))
                last.then_inc(l_done, 1)

                def shared_unit(n):
                    m, h = n // 2, n % 2
                    if n >= 2:
                        pe.wait_ge(h_ready, n - 1)
                    for off, ps, done in ((0, ps_g, g_done), (F3, ps_u, u_done)):
                        for c in range(CC):
                            last = pe.matmul(ps[:, n % 2, 0:HALF], wsgu[:, c, off + m * 128:off + (m + 1) * 128],
                                             g.xnT[:, c, h * HALF:(h + 1) * HALF], start=(c == 0), stop=(c == CC - 1))
                        last.then_inc(done, 1)

                pe.wait_ge(shared_came, 32)
                shared_unit(0)
                shared_unit(1)
                pe.wait_ge(own_ready, 1)
                pe.wait_ge(cleared, 1)
                wide = lambda v: v.rearrange("p t e -> p (t e)")
                pe.matmul(ps_d[0:TP, 1, 0:NT * NE], before[:, :], wide(own[:, :, :]), start=True, stop=False)
                pe.matmul(ps_d[0:TP, 1, 0:NT * NE], ones[:, :], wide(cum[:, 0:NT, :]), start=False, stop=True)
                pe.matmul(ps_d[0:TP, 1, NT * NE:(NT + 1) * NE], ones[:, :], cum[:, NT, :], start=True, stop=True).then_inc(places_done, 1)
                for n in range(2, UNITS):
                    shared_unit(n)

                def turn(j):
                    pe.wait_ge(first_came if j < 2 else rest_came, 16)
                    if j >= 1:
                        pe.wait_ge(xT_ready, j)
                    for c in range(CC):
                        last = pe.transpose(ps_t[:, 0, c * 128:(c + 1) * 128], rows[:, j, c * 128:(c + 1) * 128], g.ident[:, :])
                    last.then_inc(turned, 1)

                def gate_up(j):
                    expert = pe.value_load(of_tile_i[0:1, j:j + 1], min_val=0, max_val=NE - 1)
                    pe.wait_ge(xT_ready, j + 1)
                    if j >= 2:
                        pe.wait_ge(inner_ready, j - 1)
                    for off, ps, done in ((0, ps_g, gate_done), (F3, ps_u, up_done)):
                        for c in range(CC):
                            w = g.wgu[:, bass.ds(expert, 1), c, off:off + F3].rearrange("p e n -> p (e n)")
                            last = pe.matmul(ps[:, j % 2, :], xT[:, j % 2, c, :], w, start=(c == 0), stop=(c == CC - 1))
                        last.then_inc(done, 1)
                    return expert

                def turn_inner(j):
                    pe.wait_ge(inner_ready, j + 1)
                    if j >= 1:
                        pe.wait_ge(innerT_ready, j)
                    for k in range(F4):
                        last = pe.transpose(ps_t[:, 1, k * 128:(k + 1) * 128], inner[:, j % 2, k * 128:(k + 1) * 128], g.ident[:, :])
                    last.then_inc(inner_turned, 1)

                def down(j, expert):
                    pe.wait_ge(innerT_ready, j + 1)
                    if j >= 2:
                        pe.wait_ge(y_ready, j - 1)
                    for k in range(F4):
                        w = wdn[:, bass.ds(expert, 1), k, :].rearrange("p e n -> p (e n)")
                        last = pe.matmul(ps_d[:, j % 2, 0:C], innerT[:, j % 2, k, :], w, start=(k == 0), stop=(k == F4 - 1))
                    last.then_inc(down_done, 1)

                pe.wait_ge(slots_ready, 2)
                pe.wait_ge(g.wgu_came, 16 * NE)
                pe.wait_ge(wdn_came, 16 * NE)
                pe.wait_ge(h_ready, UNITS)
                turn(0)
                experts = []
                for j in range(SLOT_TILES + 2):
                    if j + 1 < SLOT_TILES:
                        turn(j + 1)
                    if j < SLOT_TILES:
                        experts.append(gate_up(j))
                    if 1 <= j <= SLOT_TILES:
                        turn_inner(j - 1)
                    if j >= 2:
                        down(j - 2, experts[j - 2])

                for t in range(NT):
                    if t >= 2:
                        pe.wait_ge(x_done, t - 1)
                    else:
                        pe.wait_ge(y_ready, SLOT_TILES)
                    for k in range(F4):
                        last = pe.matmul(ps_d[0:TP, t % 2, 0:C], hT[:, k, t * TP:(t + 1) * TP], wsdn[:, k, :],
                                         start=(k == 0), stop=(k == F4 - 1))
                    last.then_inc(o_done, 1)

            @block.scalar
            def _(act):
                norm.scalar(act)
                act.wait_ge(top_ready, 1)
                act.activation(sg[:, :], top[:, :], ACT.Sigmoid).then_inc(sg_ready, 1)
                for n in range(UNITS):
                    act.wait_ge(g_done, n + 1)
                    if n >= 2:
                        act.wait_ge(h_ready, n - 1)
                    act.activation(s[:, n % 2, 0:HALF], ps_g[:, n % 2, 0:HALF], ACT.Silu).then_inc(s_ready, 1)
                act.wait_ge(h_ready, UNITS)

                def take_turned(j):
                    act.wait_ge(turned, j + 1)
                    if j >= 2:
                        act.wait_ge(up_done, j - 1)
                    act.copy(xT[:, j % 2, :, :], ps_t[:, 0, 0:CC * 128].rearrange("p (c n) -> p c n", c=CC)).then_inc(xT_ready, 1)

                def take_inner(j):
                    act.wait_ge(inner_turned, j + 1)
                    if j >= 2:
                        act.wait_ge(down_done, j - 1)
                    act.copy(innerT[:, j % 2, :, :], ps_t[:, 1, :].rearrange("p (k n) -> p k n", k=F4)).then_inc(innerT_ready, 1)

                take_turned(0)
                for j in range(SLOT_TILES + 1):
                    if j + 1 < SLOT_TILES:
                        take_turned(j + 1)
                    if j < SLOT_TILES:
                        act.wait_ge(gate_done, j + 1)
                        if j >= 2:
                            act.wait_ge(inner_ready, j - 1)
                        act.activation(s[:, j % 2, :], ps_g[:, j % 2, :], ACT.Silu).then_inc(silu_done, 1)
                    if j >= 1:
                        take_inner(j - 1)

            @block.vector
            def _(dve):
                step = Chain(dve, chain)
                norm.vector(dve)
                dve.wait_ge(came, 64)
                dve.wait_ge(l_done, 1)
                wide = lambda v: v.unsqueeze(2).to_broadcast([TP, NT, NE])
                lat = later[0:TP, :].unsqueeze(1).to_broadcast([TP, NT, NE])
                step(dve.tensor_copy(lg[:, :, :], ps_d[0:TP, 0, 0:NT * NE].rearrange("p (t e) -> p t e", e=NE)))
                dve.tensor_reduce(top[:, :], lg[:, :, :], X, ALU.max).then_inc(top_ready, 1)
                dve.wait_ge(top_ready, 1)
                step(dve.tensor_tensor(own[:, :, :], lg[:, :, :], wide(top[:, :]), ALU.is_lt))
                step(dve.scalar_tensor_tensor(out=own[:, :, :], in0=own[:, :, :], scalar=float(NE), in1=lat, op0=ALU.mult, op1=ALU.add))
                step(dve.tensor_reduce(first[:, :], own[:, :, :], X, ALU.min))
                step(dve.memset(cum[:, 0, :], 0.0))
                step(dve.tensor_tensor(own[:, :, :], lat, wide(first[:, :]), ALU.is_equal))
                for t in range(NT - 1):
                    step(dve.tensor_tensor(cum[:, t + 1, :], cum[:, t, :], own[:, t, :], ALU.add))
                dve.tensor_tensor(cum[:, NT, :], cum[:, NT - 1, :], own[:, NT - 1, :], ALU.add).then_inc(own_ready, 1)
                dve.wait_ge(sg_ready, 1)
                for t in range(NT):
                    dve.tensor_scalar(g.xn[:, t, :], g.xn[:, t, :], sg[:, t:t + 1], None, ALU.mult).then_inc(xs_ready, 1)

                def shared_unit(n):
                    m, h = n // 2, n % 2
                    dve.wait_ge(s_ready, n + 1)
                    dve.wait_ge(u_done, n + 1)
                    dve.tensor_tensor(hT[:, m, h * HALF:(h + 1) * HALF], ps_u[:, n % 2, 0:HALF], s[:, n % 2, 0:HALF],
                                      ALU.mult).then_inc(h_ready, 1)

                shared_unit(0)
                shared_unit(1)
                dve.wait_ge(places_done, 1)
                counts = ps_d[0:TP, 1, NT * NE:(NT + 1) * NE]
                step(dve.tensor_scalar(tiles[:, :], counts, 1.0 / 128, 127.0 / 256, ALU.mult, ALU.add))
                step(dve.tensor_scalar(tiles[:, :], tiles[:, :], ROUND, -ROUND, ALU.add, ALU.add))
                step(dve.tensor_copy(ends[:, 0:1], tiles[:, 0:1]))
                for e in range(1, NE):
                    step(dve.tensor_tensor(ends[:, e:e + 1], ends[:, e - 1:e], tiles[:, e:e + 1], ALU.add))
                step(dve.tensor_tensor(base[:, :], ends[:, :], tiles[:, :], ALU.subtract))
                step(dve.tensor_scalar(base[:, :], base[:, :], 128.0, None, ALU.mult))
                step(dve.tensor_tensor(lg[:, :, :], ps_d[0:TP, 1, 0:NT * NE].rearrange("p (t e) -> p t e", e=NE),
                                       base[:, :].unsqueeze(1).to_broadcast([TP, NT, NE]), ALU.add))
                step(dve.tensor_tensor(lg[:, :, :], lg[:, :, :], own[:, :, :], ALU.mult))
                step(dve.tensor_reduce(first[:, :], lg[:, :, :], X, ALU.add))
                dve.tensor_copy(slot[:, :], first[:, :]).then_inc(slots_ready, 1)
                step(dve.tensor_tensor(passed[:, :, :], ends[0:1, :].unsqueeze(1).to_broadcast([1, SLOT_TILES, NE]),
                                       numbers[:, :].unsqueeze(2).to_broadcast([1, SLOT_TILES, NE]), ALU.is_le))
                step(dve.tensor_reduce(of_tile[:, :], passed[:, :, :], X, ALU.add))
                dve.tensor_scalar(of_tile_i[:, :], of_tile[:, :], float(NE - 1), None, ALU.min).then_inc(slots_ready, 1)
                for n in range(2, UNITS):
                    shared_unit(n)

                def take_down(j):
                    dve.wait_ge(down_done, j + 1)
                    dve.wait_ge(turned, j + 1)
                    dve.tensor_copy(rows[:, j, :], ps_d[:, j % 2, 0:C]).then_inc(y_ready, 1)

                for j in range(SLOT_TILES):
                    dve.wait_ge(silu_done, j + 1)
                    dve.wait_ge(up_done, j + 1)
                    if j >= 2:
                        dve.wait_ge(inner_turned, j - 1)
                    dve.tensor_tensor(inner[:, j % 2, :], ps_u[:, j % 2, :], s[:, j % 2, :],
                                      ALU.mult).then_inc(inner_ready, 1)
                    if j >= 2:
                        take_down(j - 2)
                take_down(SLOT_TILES - 2)
                take_down(SLOT_TILES - 1)
                for t in range(NT):
                    dve.wait_ge(o_done, t + 1)
                    dve.scalar_tensor_tensor(out=g.x[:, t, :], in0=ps_d[0:TP, t % 2, 0:C], scalar=gate, in1=g.x[:, t, :],
                                             op0=ALU.mult, op1=ALU.add).then_inc(x_done, 1)
                for t in range(NT):
                    dve.wait_ge(gathered[t], 16)
                    dve.wait_ge(x_done, t + 1)
                    dve.scalar_tensor_tensor(out=g.x[:, t, :], in0=g.xn[:, t, :], scalar=gate, in1=g.x[:, t, :],
                                             op0=ALU.mult, op1=ALU.add).then_inc(x_done, 1)



def program(nc, d, out, upto=8):
    USED.clear()
    with ExitStack() as ctx:
        g = Shared()
        g.ctx = ctx
        a = Alloc(nc, ctx, "all")
        g.x = a.sb("x", [TP, NT, C])
        g.xn = a.sb("xn", [TP, NT, C])
        g.xnT = a.sb("xnT", [128, CC, T])
        g.ident = a.sb("ident", [128, 128])
        g.gates = a.sb("gates", [128, 8])
        g.eps = a.sb("eps", [128, 1])
        g.magnitudes = a.sb("magnitudes", [48, 1])
        begin(nc, g, d)
        stages = [lambda: causal_attention(nc, g, d, 0, g.magnitudes[:, :]), lambda: top8_ffn(nc, g, d),
                  lambda: latent_layer(nc, g, d, 1, queries_plain),
                  lambda: ternary_ffn(nc, g, d),
                  lambda: latent_layer(nc, g, d, 2, queries_roped), lambda: hadamard_ffn(nc, g, d),
                  lambda: causal_attention(nc, g, d, 3, ahead=lambda sp: load_experts(g, d, sp)),
                  lambda: experts_ffn(nc, g, d)]
        for n, stage in enumerate(stages[:upto]):
            stage()
            if n in (2, 5):
                clear_semaphores(nc)
            if n == 5:
                experts_weights(nc, g)
        finish(nc, g, out)


class Shared:
    pass


def layouts(i):
    f = lambda v: np.ascontiguousarray(v)
    r = {"x": f(i["x"].reshape(T, C)), "g_xattn": f(i["g_xattn"].reshape(1, 4)), "g_ffn": f(i["g_ffn"].reshape(1, 4))}
    first = i["ctx_512"][:, :SK].transpose(2, 0, 1)
    r["ctx_first"] = f(np.stack([first, first], 2).reshape(DC, B * 2 * SK))
    for n in (0, 3):
        r[f"L{n}_wq"] = f(i[f"L{n}_xattn_Wq"].T)
        r[f"L{n}_kv"] = f(i[f"L{n}_xattn_Wkv_expand"].T)
        r[f"L{n}_wo"] = f(i[f"L{n}_xattn_Wout"].T)
    r["L0_rw"] = f(i["L0_ffn_router_weight"].T)
    r["L0_rb"] = f(i["L0_ffn_router_bias"].reshape(1, 64))
    r["L0_eb"] = f(i["L0_ffn_expert_bias"])
    r["ctx_cols"] = f(i["ctx_512"].reshape(B, KP, KT, DC).transpose(0, 3, 2, 1).reshape(B, DC * LK))
    r["ctx"] = f(i["ctx_512"].reshape(B, LK * DC))
    for n in (1, 2):
        w = {k: i[f"L{n}_xattn_{k}"] for k in ("Wq", "w_kc_q", "w_kc_kv", "W_qr", "W_kr", "Wo")}
        r[f"L{n}_wq"] = f(w["Wq"].reshape(NH, HK, C).transpose(1, 0, 2).reshape(HK, NH * C))
        r[f"L{n}_wkrT"] = f(w["W_kr"].transpose(2, 0, 1).reshape(64, NH * DC))
        r[f"L{n}_wkv"] = f(w["w_kc_kv"].transpose(1, 0, 2).reshape(HK, NH * DC))
        r[f"L{n}_wo"] = f(w["Wo"].reshape(C, NH, HK).transpose(2, 1, 0).reshape(HK, NH * C))
        wqrT = w["W_qr"].transpose(2, 0, 1)
        if n == 1:
            r["L1_wqrT"] = f(wqrT.reshape(64, NH * DQ))
            r["L1_wcqT"] = f(w["w_kc_q"].transpose(2, 0, 1).reshape(2, DQ // 2, NH, HK).transpose(1, 0, 2, 3).reshape(DQ // 2, 2 * NH * HK))
        else:
            half = DQ // 2
            turned = np.concatenate([wqrT[:, :, half:], wqrT[:, :, :half]], 2)
            r["L2_wqrT"] = f(np.stack([wqrT, turned], 1).reshape(64, 2 * NH * DQ))
            r["L2_wcq"] = f(w["w_kc_q"].transpose(1, 0, 2).reshape(HK, NH * DQ))
    r["L1_gate"], r["L1_up"], r["L1_down"] = (f(i[f"L1_ffn_w_{k}"].T) for k in ("gate", "up", "down"))
    r["L1_lanes"] = f(np.concatenate([i[f"L1_ffn_w_{k}"].reshape(-1, 16).T for k in ("gate", "up", "down")]))
    r["L2_gate"], r["L2_up"], r["L2_down"] = (f(i[f"L2_ffn_W_{k}"].T) for k in ("gate", "up", "down"))
    r["L2_su_ug"] = f(i["L2_ffn_SU_ug"].reshape(CC, 128).T)
    r["L2_su_dp"] = f(i["L2_ffn_SU_dp"].reshape(FF // 128, 128).T)
    r["L2_sc_ug"] = f(i["L2_ffn_Wscale_ug"].reshape(2 * FF // 128, 128).T)
    r["L2_sc_dp"] = f(i["L2_ffn_Wscale_dp"].reshape(1, C))
    r["L3_rw"] = f(i["L3_ffn_router_w"].T)
    r["L3_gu"], r["L3_dn"] = f(i["L3_ffn_w_gate_up"]), f(i["L3_ffn_w_down"])
    r["L3_sgu"], r["L3_sdn"] = f(i["L3_ffn_shared_gate_up"]), f(i["L3_ffn_shared_down"])
    return r


def kernel(**inputs):
    import concourse.bacc as bacc
    from concourse.bass_utils import run_bass_kernel_spmd

    nc = bacc.Bacc("TRN2", target_bir_lowering=False, num_devices=1)
    arrays = layouts({k: np.asarray(v) for k, v in inputs.items()}) | constants()
    d = {k: nc.dram_tensor(f"in_{k}", v.shape, mybir.dt.from_np(v.dtype), kind="ExternalInput").ap()
         for k, v in arrays.items()}
    out = nc.dram_tensor("out_x", (T, C), F32, kind="ExternalOutput").ap()
    program(nc, d, out)
    r = run_bass_kernel_spmd(nc, [{f"in_{k}": v for k, v in arrays.items()}], core_ids=[0])
    return r.results[0]["out_x"].reshape(B, S, C)
```

```python
from contextlib import ExitStack

import numpy as np

import concourse.bass as bass
from concourse import mybir

F32 = mybir.dt.float32
F32R = mybir.dt.float32r
BF16 = mybir.dt.bfloat16
ACT = mybir.ActivationFunctionType
ALU = mybir.AluOpType
X = mybir.AxisListType.X

B, S, C = 16, 56, 256
T = B * S
TP = 2 * S
NT = T // TP
HALF = T // 2
CC = C // 128
LK, DC = 1500, 64
NH = 16
HP = NH // 2
HD = C // NH
SK = 64
KT, KP = 12, 125
DQ = 192
QT = NH * DQ // 128
HK = 128
NE, F3 = 8, 512
SLOT_TILES = (T - NE) // 128 + NE
FF = 1024
EPS = 1e-5
MASKED = -3.0e38
ROUND = 12582912.0


SHARED_WORDS = 37600
LAST_WORDS = 46600


def constants():
    def tables(length, dim):
        inv = (1.0 / 10000.0 ** (np.arange(0, dim, 2, dtype=np.float32) / np.float32(dim))).astype(np.float32)
        f = np.arange(length, dtype=np.float32)[:, None] * inv[None, :]
        return np.repeat(np.cos(f), 2, -1).astype(np.float32), np.repeat(np.sin(f), 2, -1).astype(np.float32)

    def hadamard(n):
        h = np.ones((1, 1), np.float32)
        while h.shape[0] < n:
            h = np.block([[h, h], [h, -h]])
        return np.ascontiguousarray(h, np.float32)

    c = {"ident": np.eye(128, dtype=np.float32), "had256": hadamard(256), "had128": hadamard(128)}
    cos, sin = tables(LK, DC)
    signed = np.concatenate([-sin[:, :DC // 2], sin[:, DC // 2:]], 1)
    c["rope_kT"] = np.ascontiguousarray(
        np.concatenate([cos.T, signed.T]).reshape(2 * DC, KP, KT).transpose(0, 2, 1).reshape(2 * DC, LK))
    c["rope_k"] = np.stack([cos, signed]).reshape(2, KP, KT * DC)
    cos, sin = tables(S, DQ)
    i = np.arange(QT * 128) % DQ
    turned = np.where(i < DQ // 2, 1, -1).astype(np.float32) * sin[:, (i + DQ // 2) % DQ]
    c["rope_q"] = np.ascontiguousarray(
        np.stack([cos[:, i], turned])[:, :, :3 * 128].reshape(2, S, 3, 128).transpose(3, 0, 2, 1)).astype(np.float32)
    q, k = np.arange(128)[:, None] % 64, np.arange(SK)[None, :]
    c["causal"] = np.where(k <= q, 0.0, MASKED).astype(np.float32)
    c["headmask"] = (np.arange(128)[:, None] // HD == np.arange(8)[None, :]).astype(np.float32)
    c["lanes"] = (np.arange(48)[:, None] // 16 == np.arange(3)[None, :]).astype(np.float32)
    c["before"] = (np.arange(TP)[:, None] < np.arange(TP)[None, :]).astype(np.float32)
    c["numbers"] = np.arange(SLOT_TILES, dtype=np.float32).reshape(1, SLOT_TILES)
    c["later"] = np.tile(np.arange(8, dtype=np.float32), (128, 1))
    return c


class Chain:

    def __init__(self, eng, sem):
        self.eng, self.sem, self.n = eng, sem, 0

    def __call__(self, ins):
        self.n += 1
        ins.then_inc(self.sem, 1)
        self.eng.wait_ge(self.sem, self.n)


class Arena:

    def __init__(self, nc, name, words):
        self.ctx, self.words = ExitStack(), words
        self.mem = self.ctx.enter_context(nc.sbuf_tensor(name, [128, words], F32))
        self.taken = []

    def place(self, shape, dt):
        elements = int(np.prod(shape[1:]))
        words = (elements * mybir.dt.size(dt) + 3) // 4
        at = 0
        for first, n in self.taken:
            if first - at >= words:
                break
            at = first + n
        assert at + words <= self.words, f"the arena is full: {at} + {words} words"
        self.taken = sorted(self.taken + [(at, words)])
        view = self.mem[0:shape[0], at:at + words]
        if dt != F32:
            view = view.bitcast(dt)[:, 0:elements]
        if len(shape) > 2:
            names = [f"d{n}" for n in range(1, len(shape))]
            view = view.rearrange(f"p ({' '.join(names)}) -> p {' '.join(names)}", **dict(zip(names, shape[1:])))
        return view, (at, words)

    def free(self, where):
        self.taken.remove(where)


class Alloc:
    def __init__(self, nc, ctx, stage, arena):
        self.nc, self.ctx, self.stage, self.arena = nc, ctx, stage, arena

    def sb(self, name, shape, dt=F32):
        if self.arena is None:
            return self.ctx.enter_context(self.nc.sbuf_tensor(f"{self.stage}_{name}", shape, dt))
        view, where = self.arena.place(shape, dt)
        self.ctx.callback(self.arena.free, where)
        return view

    def ps(self, name, shape, dt=F32):
        return self.ctx.enter_context(self.nc.psum_tensor(f"{self.stage}_{name}", shape, dt))

    def sem(self, name):
        s = self.nc.alloc_semaphore(f"{self.stage}_{name}")
        USED.append(s)
        return s


class Weights:

    def __init__(self, nc, g, stage):
        self.ctx = ExitStack()
        self.a = Alloc(nc, self.ctx, stage, g.arena)
        self.loads, self.zeros = [], []
        self.cleared = self.a.sem("cleared")
        self.came = self.a.sem("came")

    def put(self, shape, *loads):
        buffer = self.a.sb("", shape)
        self.loads += [(buffer if part is None else part(buffer), src) for part, src in loads]
        return buffer

    def clear(self, pool):
        for part in self.zeros:
            pool.memset(part, 0.0).then_inc(self.cleared, 1)

    def load(self, sp):
        if self.zeros:
            sp.wait_ge(self.cleared, len(self.zeros))
        for dst, src in self.loads:
            sp.dma_start(dst, src).then_inc(self.came, 16)

    def wait(self, engine):
        engine.wait_ge(self.came, 16 * len(self.loads))


class Nothing:
    clear = load = wait = staticmethod(lambda engine: None)


USED = []


def clear_semaphores(nc):
    nc.clear_and_free_semaphores(list(USED))
    USED.clear()
    nc.all_engine_barrier()


class Norm:

    def __init__(self, nc, a, g, turned=None, moments=False):
        self.nc, self.g, self.moments = nc, g, moments
        self.stats_done = a.sem("ln_stats_done")
        self.mv_ready = a.sem("ln_mv_ready")
        self.std = a.sb("ln_std", [TP, NT])
        self.rstd = a.sb("ln_rstd", [TP, NT])
        self.shift = a.sb("ln_shift", [TP, NT])
        self.turned = turned or a.ps("ln_turned", [128, 2, 512])
        self.std_ready = a.sem("ln_std_ready")
        self.scale_ready = a.sem("ln_scale_ready")
        self.xn_ready = a.sem("ln_xn_ready")
        self.turned_ready = a.sem("ln_turned_ready")
        self.xnT_ready = a.sem("ln_xnT_ready")

    def vector(self, dve):
        g = self.g
        if self.moments:
            for t in range(NT):
                dve.bn_stats(g.stats[:, t, :], g.x[:, t, :]).then_inc(self.stats_done, 1)
            for t in range(NT):
                dve.wait_ge(self.stats_done, t + 1)
                dve.bn_aggr(g.mv[:, t, :], g.stats[:, t, :]).then_inc(self.mv_ready, 1)
        dve.wait_ge(self.std_ready, 1)
        dve.reciprocal(self.rstd[:, :], self.std[:, :]).then_inc(self.scale_ready, 1)
        dve.wait_ge(self.scale_ready, 1)
        dve.scalar_tensor_tensor(out=self.shift[:, :], in0=g.mv[:, :, 0], scalar=-1.0,
                                 in1=self.rstd[:, :], op0=ALU.mult, op1=ALU.mult).then_inc(self.scale_ready, 1)
        dve.wait_ge(self.scale_ready, 2)
        for t in range(NT):
            dve.tensor_scalar(g.xn[:, t, :], g.x[:, t, :], self.rstd[:, t:t + 1], self.shift[:, t:t + 1],
                              ALU.mult, ALU.add).then_inc(self.xn_ready, 1)

    def scalar(self, act):
        g = self.g
        if self.moments:
            act.wait_ge(self.mv_ready, NT)
        act.activation(self.std[:, :], g.mv[:, :, 1], ACT.Sqrt, bias=g.eps[0:TP, 0:1]).then_inc(self.std_ready, 1)
        for t in range(NT):
            self.scalar_tile(act, t)

    def scalar_tile(self, act, t):
        act.wait_ge(self.turned_ready, t + 1)
        act.copy(self.g.xnT[:, :, t * TP:(t + 1) * TP],
                 self.turned[:, t % 2, 0:2 * TP].rearrange("p (c n) -> p c n", c=CC)).then_inc(self.xnT_ready, 1)

    def tensor(self, pe):
        for t in range(NT):
            self.tensor_tile(pe, t)

    def tensor_tile(self, pe, t):
        g = self.g
        pe.wait_ge(self.xn_ready, t + 1)
        if t >= 2:
            pe.wait_ge(self.xnT_ready, t - 1)
        for c in range(CC):
            last = pe.transpose(self.turned[:, t % 2, c * TP:(c + 1) * TP],
                                g.xn[:, t, c * 128:(c + 1) * 128], g.ident[0:TP, 0:TP])
        last.then_inc(self.turned_ready, 1)

    def root_tile(self, act, t):
        act.wait_ge(self.mv_ready, t + 1)
        act.activation(self.std[:, t:t + 1], self.g.mv[:, t, 1:2], ACT.Sqrt, bias=self.g.eps[0:TP, 0:1]).then_inc(self.std_ready, 1)

    def vector_tile(self, dve, t):
        g, at = self.g, slice(t, t + 1)
        dve.wait_ge(self.std_ready, t + 1)
        dve.reciprocal(self.rstd[:, at], self.std[:, at]).then_inc(self.scale_ready, 1)
        dve.wait_ge(self.scale_ready, 2 * t + 1)
        dve.scalar_tensor_tensor(out=self.shift[:, at], in0=g.mv[:, t, 0:1], scalar=-1.0,
                                 in1=self.rstd[:, at], op0=ALU.mult, op1=ALU.mult).then_inc(self.scale_ready, 1)
        dve.wait_ge(self.scale_ready, 2 * t + 2)
        dve.tensor_scalar(g.xn[:, t, :], g.x[:, t, :], self.rstd[:, at], self.shift[:, at],
                          ALU.mult, ALU.add).then_inc(self.xn_ready, 1)


def take_moments(dve, g, t, x_done, count, stats_done):
    dve.wait_ge(x_done, count)
    dve.bn_stats(g.stats[:, t, :], g.x[:, t, :]).then_inc(stats_done, 1)
    dve.wait_ge(stats_done, t + 1)
    return dve.bn_aggr(g.mv[:, t, :], g.stats[:, t, :])


def begin(nc, g, d, ahead):
    with ExitStack() as ctx:
        a = Alloc(nc, ctx, "begin", g.arena)
        came = a.sem("came")
        stats_done = a.sem("stats_done")
        done = a.sem("done")
        raw = a.sb("gates_raw", [128, 8])
        with nc.Block() as block:

            @block.sync
            def _(sp):
                sp.dma_start(g.x[:, :, :], d["x"].rearrange("(t p) c -> p t c", p=TP)).then_inc(came, 16)
                sp.dma_start(g.ident[:, :], d["ident"]).then_inc(came, 16)
                sp.dma_start(raw[:, 0:4], d["g_xattn"].partition_broadcast(128)).then_inc(came, 16)
                sp.dma_start(raw[:, 4:8], d["g_ffn"].partition_broadcast(128)).then_inc(came, 16)
                ahead.load(sp)
                ahead.wait(sp)

            @block.vector
            def _(dve):
                dve.memset(g.eps[:, :], EPS)
                for t in range(NT):
                    take_moments(dve, g, t, came, 64, stats_done)

            @block.scalar
            def _(act):
                act.wait_ge(came, 64)
                act.activation(g.gates[:, :], raw[:, :], ACT.Tanh).then_inc(done, 1)


def causal_weights(nc, g, d, layer, magnitudes=False):
    w = Weights(nc, g, f"xattn{layer}_w")
    w.wkv = w.put([DC, 2 * C], (None, d[f"L{layer}_kv"]))
    w.ctxT = w.put([DC, B, 2, SK], (None, d["ctx_first"].rearrange("d (b e k) -> d b e k", b=B, e=2)))
    w.wq = w.put([128, CC, C], (None, d[f"L{layer}_wq"].rearrange("(c p) n -> p c n", p=128)))
    w.wo = w.put([128, CC, C], (None, d[f"L{layer}_wo"].rearrange("(c p) n -> p c n", p=128)))
    w.causal = w.put([128, SK], (None, d["causal"]))
    w.headmask = w.put([128, 8], (None, d["headmask"]))
    return w


def causal_attention(nc, g, d, layer, weights, ahead, magnitudes=None, loads=None, loaded=True):
    gate = g.gates[0:TP, layer:layer + 1]
    NP = B // 2
    with ExitStack() as ctx:
        a = Alloc(nc, ctx, f"xattn{layer}", g.arena)
        wq, wkv, wo, ctxT, causal, headmask = weights.wq, weights.wkv, weights.wo, weights.ctxT, weights.causal, weights.headmask
        kT = a.sb("kT", [128, CC, B, SK])
        values = a.sb("values", [128, B, HP, 2, HD])
        qT = a.sb("qT", [128, CC, T + 8])
        if layer:
            keys, sc = a.sb("keys", [128, 8, 8, SK]), a.sb("scores", [128, 3, NH, SK])
        else:
            place = g.q[:, :, :].rearrange("p j t -> p (j t)")
            keys = place[:, 0:64 * SK].rearrange("p (n h k) -> p n h k", n=8, h=8)
            sc = place[:, 64 * SK:64 * SK + 3 * NH * SK].rearrange("p (n h k) -> p n h k", n=3, h=NH)
        mx = a.sb("mx", [128, 2, NH])
        den = a.sb("den", [128, 2, NH])
        wT = a.sb("weightsT", [128, 2, HP, 128])
        oT = a.sb("outT", [128, CC, T]) if layer else g.fold[:, :, :].rearrange("p j n -> p (j n)")[:, 0:CC * T].rearrange("p (c n) -> p c n", c=CC)
        if magnitudes is not None:
            lanes = a.sb("lanes", [48, FF * C // 16])
            lanes_came = a.sem("lanes_came")
            lanes_summed = a.sem("lanes_summed")
        norm = Norm(nc, a, g)
        maskb = a.sb("maskb", [128, 8, SK], BF16)
        identb = a.sb("identb", [128, 128], BF16)
        ps_a = a.ps("ps_a", [128, 2, 512])
        ps_s = (ps_a, norm.turned)
        ps_t = a.ps("ps_t", [128, 2, 512])
        ps_o = a.ps("ps_o", [128, 512])
        ps_y = a.ps("ps_y", [128, 512])
        zeroed = a.sem("zeroed")
        prod = a.sem("prod")
        taken = a.sem("taken")
        keys_ready = a.sem("keys_ready")
        scores_done = a.sem("scores_done")
        shifted = a.sem("shifted")
        exp_done = a.sem("exp_done")
        weights_ready = a.sem("weights_ready")
        turned = a.sem("turned")
        wT_ready = a.sem("wT_ready")
        o_done = a.sem("o_done")
        o_taken = a.sem("o_taken")
        y_done = a.sem("y_done")
        x_done = a.sem("x_done")
        chain = a.sem("dve_chain")
        KV, VV, QQ = 4, 16, 4
        with nc.Block() as block:

            @block.sync
            def _(sp):
                if not loaded:
                    weights.load(sp)
                if magnitudes is not None:
                    sp.dma_start(lanes[:, :], d["L1_lanes"]).then_inc(lanes_came, 16)
                ahead.load(sp)
                if loads is not None:
                    loads(sp)
                ahead.wait(sp)

            @block.gpsimd
            def _(pool):
                pool.memset(values[:, :, :, :, :], 0.0).then_inc(zeroed, 1)
                pool.memset(qT[:, :, T:T + 8], 0.0).then_inc(zeroed, 1)
                pool.tensor_copy(identb[:, :], g.ident[:, :]).then_inc(zeroed, 1)
                weights.wait(pool)
                pool.tensor_copy(maskb[:, :, :], causal[:, :].unsqueeze(1).to_broadcast([128, 8, SK])).then_inc(zeroed, 1)
                ahead.clear(pool)
                pool.wait_ge(taken, KV)
                for n in range(2 * B):
                    b, c = n // 2, n % 2
                    if n >= 8:
                        pool.wait_ge(scores_done, (n - 8) // 4 + 1)
                    pool.tensor_tensor(keys[:, n % 8, :, :],
                                       kT[:, c, b, :].unsqueeze(1).to_broadcast([128, 8, SK]),
                                       headmask[:, :].unsqueeze(2).to_broadcast([128, 8, SK]),
                                       ALU.mult).then_inc(keys_ready, 1)

            @block.tensor
            def _(pe):
                weights.wait(pe)
                n = 0
                for c in range(CC):
                    for h in range(2):
                        if n >= 2:
                            pe.wait_ge(taken, n - 1)
                        pe.matmul(ps_a[:, n % 2, :], wkv[:, c * 128:(c + 1) * 128],
                                  ctxT[:, 8 * h:8 * h + 8, 0, :], start=True, stop=True).then_inc(prod, 1)
                        n += 1
                for b in range(B):
                    pe.wait_ge(taken, n - 1)
                    pe.matmul(ps_a[:, n % 2, 0:C], ctxT[:, b, :, :], wkv[:, C:2 * C],
                              start=True, stop=True).then_inc(prod, 1)
                    n += 1
                norm.tensor(pe)
                pe.wait_ge(norm.xnT_ready, NT)
                for m in range(CC):
                    for h in range(2):
                        pe.wait_ge(taken, n - 1)
                        for c in range(CC):
                            last = pe.matmul(ps_a[:, n % 2, 0:HALF], wq[:, c, m * 128:(m + 1) * 128],
                                             g.xnT[:, c, h * HALF:(h + 1) * HALF], start=(c == 0), stop=(c == CC - 1))
                        last.then_inc(prod, 1)
                        n += 1
                pe.wait_ge(taken, n)
                pe.wait_ge(zeroed, 4)

                def scores(p):
                    pe.wait_ge(keys_ready, 4 * p + 4)
                    if p >= 2:
                        pe.wait_ge(shifted, p - 1)
                    for c in range(CC):
                        pe.matmul(ps_s[p % 2][:, c, :], identb[:, :], maskb[:, :, :], start=True, stop=False)
                    for e in range(2):
                        b = 2 * p + e
                        for c in range(CC):
                            last = pe.matmul(ps_s[p % 2][64 * e:64 * e + 64, c, :], qT[:, c, b * S:b * S + 64],
                                             keys[:, (4 * p + 2 * e + c) % 8, :, :], start=False, stop=True)
                    last.then_inc(scores_done, 1)

                def output(p):
                    pe.wait_ge(weights_ready, p + 1)
                    for j in range(HP):
                        if j % 4 == 0 and p >= 1:
                            pe.wait_ge(wT_ready, 2 * p)
                        last = pe.transpose(ps_t[:, j // 4, (j % 4) * 128:(j % 4) * 128 + 128],
                                            sc[:, p % 3, 2 * j:2 * j + 2, :], g.ident[:, :])
                        if j % 4 == 3:
                            last.then_inc(turned, 1)
                    pe.wait_ge(wT_ready, 2 * p + 2)
                    if p >= 1:
                        pe.wait_ge(o_taken, p)
                    for e in range(2):
                        for j in range(HP):
                            c, r = j // 4, 32 * (j % 4)
                            last = pe.matmul(ps_o[r:r + 32, c * 128 + e * 64:c * 128 + e * 64 + 64],
                                             values[:, 2 * p + e, j, :, :], wT[:, p % 2, j, e * 64:e * 64 + 64],
                                             start=True, stop=True, tile_position=(0, r))
                    last.then_inc(o_done, 1)

                def project(p):
                    pe.wait_ge(o_taken, p + 1)
                    if p >= 1:
                        pe.wait_ge(x_done, p)
                    for c in range(CC):
                        last = pe.matmul(ps_y[0:TP, 0:C], oT[:, c, p * TP:(p + 1) * TP], wo[:, c, :],
                                         start=(c == 0), stop=(c == CC - 1))
                    last.then_inc(y_done, 1)

                for p in range(NP + 3):
                    if p < NP:
                        scores(p)
                    if 2 <= p < NP + 2:
                        output(p - 2)
                    if p >= 3:
                        project(p - 3)

            @block.scalar
            def _(act):
                n = 0
                for c in range(CC):
                    for h in range(2):
                        act.wait_ge(prod, n + 1)
                        act.copy(kT[:, c, 8 * h:8 * h + 8, :],
                                 ps_a[:, n % 2, :].rearrange("p (b k) -> p b k", k=SK)).then_inc(taken, 1)
                        n += 1
                act.wait_ge(zeroed, 1)
                for b in range(B):
                    act.wait_ge(prod, n + 1)
                    v = ps_a[:, n % 2, 0:C].rearrange("p (j e k) -> p j e k", j=HP, e=2)
                    act.copy(values[0:64, b, :, 0, :], v[0:64, :, 0, :])
                    act.copy(values[64:128, b, :, 1, :], v[64:128, :, 1, :]).then_inc(taken, 1)
                    n += 1
                norm.scalar(act)
                for m in range(CC):
                    for h in range(2):
                        act.wait_ge(prod, n + 1)
                        act.mul(qT[:, m, h * HALF:(h + 1) * HALF], ps_a[:, n % 2, 0:HALF], HD ** -0.5).then_inc(taken, 1)
                        n += 1

                def exp(p):
                    act.wait_ge(shifted, p + 1)
                    act.activation(sc[:, p % 3, :, :], sc[:, p % 3, :, :], ACT.Exp).then_inc(exp_done, 1)

                def take(p):
                    for h in range(2):
                        act.wait_ge(turned, 2 * p + h + 1)
                        if p >= 2 and h == 0:
                            act.wait_ge(o_done, p - 1)
                        act.copy(wT[:, p % 2, 4 * h:4 * h + 4, :],
                                 ps_t[:, h, :].rearrange("p (j n) -> p j n", j=4)).then_inc(wT_ready, 1)
                    act.wait_ge(o_done, p + 1)
                    act.copy(oT[:, :, p * TP:(p + 1) * TP].rearrange("q c (e s) -> q c e s", e=2),
                             ps_o[:, 0:256].rearrange("q (c e s) -> q c e s", c=2, e=2)[:, :, :, 0:S]).then_inc(o_taken, 1)

                for p in range(NP + 2):
                    if p >= 2:
                        take(p - 2)
                    if p < NP:
                        exp(p)

            @block.vector
            def _(dve):
                norm.vector(dve)
                step = Chain(dve, chain)
                if magnitudes is not None:
                    dve.wait_ge(lanes_came, 16)
                    dve.tensor_reduce(magnitudes, lanes[:, :], X, ALU.add, apply_absolute_value=True).then_inc(lanes_summed, 1)

                def soft(p):
                    u = p % 2
                    dve.wait_ge(scores_done, p + 1)
                    if p >= 3:
                        dve.wait_ge(turned, 2 * p - 4)
                    if p >= 2:
                        dve.wait_ge(weights_ready, p - 1)
                    scores = ps_s[p % 2][:, :, :].rearrange("p c (h k) -> p (c h) k", k=SK)
                    step(dve.tensor_reduce(mx[:, u, :], scores, X, ALU.max))
                    dve.tensor_tensor(sc[:, p % 3, :, :], scores, mx[:, u, :].unsqueeze(2).to_broadcast([128, NH, SK]),
                                      ALU.subtract).then_inc(shifted, 1)

                def normalise(p):
                    u = p % 2
                    dve.wait_ge(exp_done, p + 1)
                    step(dve.tensor_reduce(den[:, u, :], sc[:, p % 3, :, :], X, ALU.add))
                    step(dve.reciprocal(mx[:, u, :], den[:, u, :]))
                    dve.tensor_tensor(sc[:, p % 3, :, :], sc[:, p % 3, :, :],
                                      mx[:, u, :].unsqueeze(2).to_broadcast([128, NH, SK]),
                                      ALU.mult).then_inc(weights_ready, 1)

                def add(p):
                    dve.wait_ge(y_done, p + 1)
                    dve.scalar_tensor_tensor(out=g.x[:, p, :], in0=ps_y[0:TP, 0:C], scalar=gate, in1=g.x[:, p, :],
                                             op0=ALU.mult, op1=ALU.add).then_inc(x_done, 1)

                for p in range(NP + 4):
                    if p >= 4:
                        add(p - 4)
                    if p < NP:
                        soft(p)
                    if 1 <= p <= NP:
                        normalise(p - 1)


def top8_weights(nc, g, d):
    w = Weights(nc, g, "ffn0_w")
    w.rw = w.put([128, CC, 64], (None, d["L0_rw"].rearrange("(c p) n -> p c n", p=128)))
    w.bias = w.put([TP, 64], (None, d["L0_rb"].partition_broadcast(TP)))
    w.eb = w.put([64, C], (None, d["L0_eb"]))
    return w


def top8_ffn(nc, g, weights, ahead):
    E = 64
    gate = g.gates[0:TP, 4:5]
    with ExitStack() as ctx:
        a = Alloc(nc, ctx, "ffn0", g.arena)
        rw, bias, eb = weights.rw, weights.bias, weights.eb
        e = a.sb("e", [TP, NT, E])
        rest = a.sb("rest", [TP, NT, E])
        m8 = a.sb("m8", [TP, NT, 8])
        mx = a.sb("mx", [TP, NT])
        den = a.sb("den", [TP, NT])
        top = a.sb("top", [TP, NT])
        wT = a.sb("wT", [E, NT, TP])
        y = a.sb("y", [TP, NT, C])
        norm = Norm(nc, a, g, moments=True)
        ps_l = a.ps("ps_l", [128, 512])
        ps_t = a.ps("ps_t", [128, 2, 512])
        ps_y = a.ps("ps_y", [128, 2, 512])
        logits = a.sem("logits")
        shifted = a.sem("shifted")
        exp_done = a.sem("exp_done")
        w_ready = a.sem("w_ready")
        turned = a.sem("turned")
        wT_ready = a.sem("wT_ready")
        y_done = a.sem("y_done")
        y_taken = a.sem("y_taken")
        x_done = a.sem("x_done")
        chain = a.sem("dve_chain")
        with nc.Block() as block:

            @block.sync
            def _(sp):
                ahead.load(sp)
                ahead.wait(sp)

            @block.gpsimd
            def _(pool):
                ahead.clear(pool)

            @block.tensor
            def _(pe):
                norm.tensor(pe)
                for t in range(NT):
                    pe.wait_ge(norm.xnT_ready, t + 1)
                    for c in range(CC):
                        last = pe.matmul(ps_l[0:TP, t * E:(t + 1) * E], g.xnT[:, c, t * TP:(t + 1) * TP], rw[:, c, :],
                                         start=(c == 0), stop=(c == CC - 1))
                last.then_inc(logits, 1)
                pe.wait_ge(w_ready, 1)
                for t in range(NT):
                    if t >= 2:
                        pe.wait_ge(wT_ready, t - 1)
                    pe.transpose(ps_t[0:E, t % 2, 0:TP], e[:, t, :], g.ident[0:TP, 0:TP]).then_inc(turned, 1)
                    pe.wait_ge(wT_ready, t + 1)
                    if t >= 2:
                        pe.wait_ge(y_taken, t - 1)
                    pe.matmul(ps_y[0:TP, t % 2, 0:C], wT[:, t, :], eb[:, :], start=True, stop=True).then_inc(y_done, 1)

            @block.scalar
            def _(act):
                norm.scalar(act)
                act.wait_ge(shifted, 1)
                act.activation(e[:, :, :], e[:, :, :], ACT.Exp).then_inc(exp_done, 1)
                for t in range(NT):
                    act.wait_ge(turned, t + 1)
                    act.copy(wT[:, t, :], ps_t[0:E, t % 2, 0:TP]).then_inc(wT_ready, 1)

            @block.vector
            def _(dve):
                norm.vector(dve)
                step = Chain(dve, chain)
                wide = lambda v: v.unsqueeze(2).to_broadcast([TP, NT, E])
                dve.wait_ge(logits, 1)
                step(dve.tensor_tensor(e[:, :, :], ps_l[0:TP, :].rearrange("p (t e) -> p t e", e=E),
                                       bias[:, :].unsqueeze(1).to_broadcast([TP, NT, E]), ALU.add))
                step(dve.tensor_reduce(mx[:, :], e[:, :, :], X, ALU.max))
                dve.tensor_tensor(e[:, :, :], e[:, :, :], wide(mx[:, :]), ALU.subtract).then_inc(shifted, 1)
                dve.wait_ge(exp_done, 1)
                step(dve.tensor_reduce(den[:, :], e[:, :, :], X, ALU.add))
                step(dve.reciprocal(mx[:, :], den[:, :]))
                for t in range(NT):
                    step(dve.max(m8[:, t, :], e[:, t, :]))
                    step(dve.match_replace(rest[:, t, :], m8[:, t, :], e[:, t, :], 0.0))
                step(dve.tensor_tensor(e[:, :, :], e[:, :, :], rest[:, :, :], ALU.subtract))
                dve.tensor_tensor(e[:, :, :], e[:, :, :], wide(mx[:, :]), ALU.mult).then_inc(w_ready, 1)
                step(dve.tensor_reduce(top[:, :], m8[:, :, :], X, ALU.add))
                step(dve.tensor_tensor(top[:, :], top[:, :], mx[:, :], ALU.mult))
                for t in range(NT):
                    dve.wait_ge(y_done, t + 1)
                    ins = dve.scalar_tensor_tensor(out=y[:, t, :], in0=g.xn[:, t, :], scalar=top[:, t:t + 1],
                                                   in1=ps_y[0:TP, t % 2, 0:C], op0=ALU.mult, op1=ALU.add)
                    ins.then_inc(y_taken, 1)
                    dve.wait_ge(y_taken, t + 1)
                    dve.scalar_tensor_tensor(out=g.x[:, t, :], in0=y[:, t, :], scalar=gate, in1=g.x[:, t, :],
                                             op0=ALU.mult, op1=ALU.add).then_inc(x_done, 1)


def wait_from(eng, sem, value):
    if not (isinstance(value, int) and value <= 0):
        eng.wait_ge(sem, value)


def latent_outputs(a, norm):
    return dict(ps=norm.turned, folded=a.sem("folded"), taken=a.sem("folded_taken"))


def out_weights_tensor(pe, f, wkv, wo):
    for j in range(HP):
        if j >= 2:
            pe.wait_ge(f["taken"], j - 1)
        for e in range(2):
            last = pe.matmul(f["ps"][64 * e:64 * e + 64, j % 2, 0:C], wkv[:, 2 * j + e, :], wo[:, 2 * j + e, :],
                             start=True, stop=True)
        last.then_inc(f["folded"], 1)


def out_weights_scalar(act, f, fold):
    for j in range(HP):
        act.wait_ge(f["folded"], j + 1)
        act.copy(fold[:, j, :], f["ps"][:, j % 2, 0:C]).then_inc(f["taken"], 1)


def plain_weights(nc, g, d):
    w = Weights(nc, g, "q1_w")
    both = lambda name, n: [d[name].rearrange("r (j e i) -> r j e i", j=HP, e=2)[:, :, e, :] for e in range(2)]
    w.wqrT = w.put([128, HP, DQ], *((lambda v, e=e: v[64 * e:64 * e + 64, :, :], both("L1_wqrT", DQ)[e]) for e in range(2)))
    w.wkrT = w.put([128, HP, 2, DC], *((lambda v, e=e: v[64 * e:64 * e + 64, :, e, :], both("L1_wkrT", DC)[e]) for e in range(2)))
    w.zeros = [w.wkrT]
    w.wcqT = w.put([DQ // 2, 2, NH, HK], (None, d["L1_wcqT"].rearrange("i (u h k) -> i u h k", u=2, h=NH)))
    w.wq = w.put([128, NH, C], (None, d["L1_wq"].rearrange("k (h n) -> k h n", h=NH)))
    w.wkv = w.put([128, NH, DC], (None, d["L1_wkv"].rearrange("k (h n) -> k h n", h=NH)))
    w.wo = w.put([128, NH, C], (None, d["L1_wo"].rearrange("k (h n) -> k h n", h=NH)))
    return w


def queries_plain(nc, g, d, q, fold, w):
    IC = DQ // 2
    with ExitStack() as ctx:
        a = Alloc(nc, ctx, "q1", g.arena)
        wqrT, wkrT, wcqT, wq, wkv, wo = w.wqrT, w.wkrT, w.wcqT, w.wq, w.wkv, w.wo
        z = a.sb("z", [IC, 2, 2, 2, DC])
        y = a.sb("y", [128, 2, 2, 2, DC])
        aw = a.sb("a", [128, HP, CC, 2, DC])
        norm = Norm(nc, a, g, moments=True)
        f = latent_outputs(a, norm)
        ps_z = a.ps("ps_z", [128, 2, 512])
        ps_y = a.ps("ps_y", [128, 2, 512])
        ps_q = a.ps("ps_q", [128, 2, 512])
        z_done, z_ready, y_done, y_ready, a_done, a_ready, q_done, q_taken = (
            a.sem(n) for n in ("z_done", "z_ready", "y_done", "y_ready", "a_done", "a_ready", "q_done", "q_taken"))
        with nc.Block() as block:

            @block.tensor
            def _(pe):
                def fold_z(j):
                    if j >= 2:
                        pe.wait_ge(z_ready, j - 1)
                    for u in range(2):
                        last = pe.matmul(ps_z[0:IC, j % 2, u * 128:(u + 1) * 128], wqrT[:, j, u * IC:(u + 1) * IC],
                                         wkrT[:, j, :, :], start=True, stop=True)
                    last.then_inc(z_done, 1)

                def fold_y(j):
                    pe.wait_ge(z_ready, j + 1)
                    if j >= 2:
                        pe.wait_ge(y_ready, j - 1)
                    for e in range(2):
                        for u in range(2):
                            last = pe.matmul(ps_y[:, j % 2, e * 128:(e + 1) * 128], wcqT[:, u, 2 * j + e, :], z[:, j % 2, u, :, :],
                                             start=(u == 0), stop=(u == 1))
                    last.then_inc(y_done, 1)

                def fold_a(j):
                    pe.wait_ge(y_ready, j + 1)
                    if j >= 2:
                        pe.wait_ge(a_ready, j - 1)
                    for c in range(CC):
                        for e in range(2):
                            at = (2 * c + e) * 128
                            last = pe.matmul(ps_q[:, j % 2, at:at + 128], wq[:, 2 * j + e, c * 128:(c + 1) * 128],
                                             y[:, j % 2, e, :, :], start=True, stop=True)
                    last.then_inc(a_done, 1)

                for n in range(HP + 2):
                    if n < HP:
                        fold_z(n)
                    if 1 <= n <= HP:
                        fold_y(n - 1)
                    if n >= 2:
                        fold_a(n - 2)
                norm.tensor(pe)
                pe.wait_ge(norm.xnT_ready, NT)
                out_weights_tensor(pe, f, wkv, wo)
                pe.wait_ge(a_ready, HP)
                n = 0
                for j in range(HP):
                    for h in range(2):
                        if n >= 2:
                            pe.wait_ge(q_taken, n - 1)
                        for c in range(CC):
                            last = pe.matmul(ps_q[:, n % 2, 0:HALF], aw[:, j, c, :, :], g.xnT[:, c, h * HALF:(h + 1) * HALF],
                                             start=(c == 0), stop=(c == CC - 1))
                        last.then_inc(q_done, 1)
                        n += 1

            @block.scalar
            def _(act):
                def take_z(j):
                    act.wait_ge(z_done, j + 1)
                    if j >= 2:
                        act.wait_ge(y_done, j - 1)
                    act.copy(z[:, j % 2, :, :, :].rearrange("p u e n -> p (u e n)"), ps_z[0:IC, j % 2, 0:256]).then_inc(z_ready, 1)

                def take_y(j):
                    act.wait_ge(y_done, j + 1)
                    if j >= 2:
                        act.wait_ge(a_done, j - 1)
                    act.copy(y[:, j % 2, :, :, :].rearrange("p u e n -> p (u e n)"), ps_y[:, j % 2, 0:256]).then_inc(y_ready, 1)

                def take_a(j):
                    act.wait_ge(a_done, j + 1)
                    src = ps_q[:, j % 2, :].rearrange("p (c e v n) -> p c e v n", c=CC, e=2, v=2)
                    for e in range(2):
                        last = act.copy(aw[:, j, :, e, :], src[:, :, e, e, :])
                    last.then_inc(a_ready, 1)

                for n in range(HP + 2):
                    if n < HP:
                        take_z(n)
                    if 1 <= n <= HP:
                        take_y(n - 1)
                    if n >= 2:
                        take_a(n - 2)
                norm.scalar(act)
                out_weights_scalar(act, f, fold)
                for n in range(2 * HP):
                    j, h = n // 2, n % 2
                    act.wait_ge(q_done, n + 1)
                    act.copy(q[:, j, h * HALF:(h + 1) * HALF], ps_q[:, n % 2, 0:HALF]).then_inc(q_taken, 1)

            @block.vector
            def _(dve):
                norm.vector(dve)


def roped_weights(nc, g, d):
    w = Weights(nc, g, "q2_w")
    wqr = d["L2_wqrT"].rearrange("r (v j e i) -> r v j e i", v=2, j=HP, e=2)
    wkr = d["L2_wkrT"].rearrange("r (j e n) -> r j e n", j=HP, e=2)
    w.wqrT = w.put([128, 2, HP, 2, DQ], *((lambda b, e=e, v=v: b[64 * e:64 * e + 64, v, :, e, :], wqr[:, v, :, e, :])
                                          for e in range(2) for v in range(2)))
    w.wkrT = w.put([128, HP, 2, DC], *((lambda b, e=e: b[64 * e:64 * e + 64, :, e, :], wkr[:, :, e, :]) for e in range(2)))
    w.zeros = [w.wqrT, w.wkrT]
    w.wcq = w.put([128, NH, DQ], (None, d["L2_wcq"].rearrange("k (h i) -> k h i", h=NH)))
    w.wq = w.put([128, NH, C], (None, d["L2_wq"].rearrange("k (h n) -> k h n", h=NH)))
    w.rope = w.put([128, 2, 3, S], (None, d["rope_q"]))
    return w


def queries_roped(nc, g, d, q, fold, w):
    with ExitStack() as ctx:
        a = Alloc(nc, ctx, "q2", g.arena)
        wqrT, wkrT, wcq, wq, rope = w.wqrT, w.wkrT, w.wcq, w.wq, w.rope
        wkv = a.sb("wkv", [128, NH, DC])
        wo = a.sb("wo", [128, NH, C])
        came_o = a.sem("came_o")
        G = a.sb("G", [128, CC, NH * DQ])
        z = a.sb("z", [128, HP, 3, 2, 2, DC])
        ur = a.sb("u_roped", [128, 2, 2, HALF])
        norm = Norm(nc, a, g, moments=True)
        f = latent_outputs(a, norm)
        ps_g = a.ps("ps_g", [128, 2, 512])
        ps_q = a.ps("ps_q", [128, 2, 512])
        z_done, z_ready, g_done, g_ready, u_done, u_ready, q_done, q_taken, u_used = (
            a.sem(n) for n in ("z_done", "z_ready", "g_done", "g_ready", "u_done", "u_ready", "q_done", "q_taken", "u_used"))
        with nc.Block() as block:

            @block.sync
            def _(sp):
                sp.dma_start(wkv[:, :, :], d["L2_wkv"].rearrange("k (h n) -> k h n", h=NH)).then_inc(came_o, 16)
                sp.dma_start(wo[:, :, :], d["L2_wo"].rearrange("k (h n) -> k h n", h=NH)).then_inc(came_o, 16)

            @block.tensor
            def _(pe):
                for n in range(2 * HP):
                    j, v = n // 2, n % 2
                    if n >= 2:
                        pe.wait_ge(z_ready, n - 1)
                    for t in range(3):
                        last = pe.matmul(ps_q[:, n % 2, t * 128:(t + 1) * 128],
                                         wqrT[:, v, j, :, :].rearrange("p e i -> p (e i)")[:, t * 128:(t + 1) * 128],
                                         wkrT[:, j, :, :], start=True, stop=True)
                    last.then_inc(z_done, 1)
                for h in range(NH):
                    if h >= 2:
                        pe.wait_ge(g_ready, h - 1)
                    for c in range(CC):
                        last = pe.matmul(ps_g[:, h % 2, c * DQ:(c + 1) * DQ], wq[:, h, c * 128:(c + 1) * 128], wcq[:, h, :],
                                         start=True, stop=True)
                    last.then_inc(g_done, 1)
                norm.tensor(pe)
                pe.wait_ge(norm.xnT_ready, NT)
                pe.wait_ge(came_o, 32)
                out_weights_tensor(pe, f, wkv, wo)
                pe.wait_ge(z_ready, 2 * HP)
                pe.wait_ge(g_ready, NH)

                def wide(n):
                    j, h, t = n // 6, n // 3 % 2, n % 3
                    if n >= 2:
                        pe.wait_ge(u_ready, 2 * n - 2)
                    for c in range(CC):
                        at = (3 * j + t) * 128
                        last = pe.matmul(ps_g[:, n % 2, 0:HALF], G[:, c, at:at + 128], g.xnT[:, c, h * HALF:(h + 1) * HALF],
                                         start=(c == 0), stop=(c == CC - 1))
                    last.then_inc(u_done, 1)

                def narrow(n):
                    j, h, t = n // 6, n // 3 % 2, n % 3
                    pe.wait_ge(u_ready, 2 * n + 2)
                    if t == 0 and n // 3 >= 2:
                        pe.wait_ge(q_taken, n // 3 - 1)
                    for v in range(2):
                        last = pe.matmul(ps_q[:, n // 3 % 2, 0:HALF], z[:, j, t, v, :, :], ur[:, n % 2, v, :],
                                         start=(t == 0 and v == 0), stop=(t == 2 and v == 1))
                    last.then_inc(u_used, 1)

                for n in range(6 * HP + 1):
                    if n < 6 * HP:
                        wide(n)
                    if n >= 1:
                        narrow(n - 1)

            @block.scalar
            def _(act):
                for n in range(2 * HP):
                    act.wait_ge(z_done, n + 1)
                    act.copy(z[:, n // 2, :, n % 2, :, :].rearrange("p t e n -> p t (e n)"),
                             ps_q[:, n % 2, 0:3 * 128].rearrange("p (t n) -> p t n", t=3)).then_inc(z_ready, 1)
                for h in range(NH):
                    act.wait_ge(g_done, h + 1)
                    act.copy(G[:, :, h * DQ:(h + 1) * DQ], ps_g[:, h % 2, 0:CC * DQ].rearrange("p (c n) -> p c n", c=CC)).then_inc(g_ready, 1)
                norm.scalar(act)
                out_weights_scalar(act, f, fold)
                for n in range(2 * HP):
                    act.wait_ge(u_used, 3 * n + 3)
                    act.copy(q[:, n // 2, (n % 2) * HALF:(n % 2 + 1) * HALF], ps_q[:, n % 2, 0:HALF]).then_inc(q_taken, 1)

            @block.vector
            def _(dve):
                norm.vector(dve)
                for n in range(6 * HP):
                    dve.wait_ge(u_done, n + 1)
                    if n >= 2:
                        dve.wait_ge(u_used, n - 1)
                    for v in range(2):
                        dve.tensor_tensor(ur[:, n % 2, v, :].rearrange("p (b s) -> p b s", s=S),
                                          ps_g[:, n % 2, 0:HALF].rearrange("p (b s) -> p b s", s=S),
                                          rope[:, v, n % 3, :].unsqueeze(1).to_broadcast([128, B // 2, S]),
                                          ALU.mult).then_inc(u_ready, 1)


def latent_attention(nc, g, d, layer, q):
    G8 = NH * S
    GH = G8 // 2
    QTL = G8 // 128
    MAX_FROM = 2
    with ExitStack() as ctx:
        a = Alloc(nc, ctx, f"latent{layer}", None)
        rope = a.sb("rope", [KP, 2, KT, DC])
        raw = [a.sb(f"raw{u}", [KP, KT, DC]) for u in range(2)]
        turned_half = a.sb("turned_half", [KP, KT, DC])
        rows = [a.sb(f"rows{u}", [KP, KT, DC]) for u in range(2)]
        val = [a.sb(f"val{u}", [KP, KT, 128]) for u in range(2)]
        ropeT = a.sb("ropeT", [DC, 2, LK])
        rawT = [a.sb(f"rawT{u}", [DC, 2, LK]) for u in range(2)]
        kA = [a.sb(f"kA{u}", [128, LK], F32R) for u in range(2)]
        kB = [a.sb(f"kB{u}", [128, LK], F32R) for u in range(2)]
        qA = [a.sb(f"qA{u}", [128, G8], F32R) for u in range(2)]
        qB = [a.sb(f"qB{u}", [128, G8], F32R) for u in range(2)]
        w = [a.sb(f"w{u}", [KP, G8]) for u in range(2)]
        mx = a.sb("mx", [128, 2, QTL])
        osb = a.sb("osb", [128, G8])
        rec = a.sb("rec", [64, G8])
        psW = a.ps("psW", [128, 3, 512])
        psSO = a.ps("psSO", [128, 4, 512])
        psS, psO = psSO[:, 0:2, :], psSO[:, 2:4, :]
        raw_came = [a.sem(f"raw_came{u}") for u in range(2)]
        rawT_came = [a.sem(f"rawT_came{u}") for u in range(2)]
        names = ("tables", "tablesT", "filled", "ones", "roped", "val_ready", "productT", "ropedT", "first_keys", "hi_ready", "kA_ready", "kB_ready", "qA_ready", "qB_ready",
                 "max_scores", "max_ready", "row_turned", "row_ready", "scores_done", "exp_done", "av_done",
                 "o_copied", "rec_ready", "o_ready", "pool_chain")
        (tables, tablesT, filled, ones, roped, val_ready, productT, ropedT, first_keys, hi_ready, kA_ready, kB_ready, qA_ready, qB_ready,
         max_scores, max_ready, row_turned, row_ready, scores_done, exp_done, av_done,
         o_copied, rec_ready, o_ready, pool_chain) = (a.sem(n) for n in names)

        def each_batch(eng, body):
            body(0, 0)
            body(1, 1)
            with eng.Fori(1, B // 2 - 1) as i:
                body(2 * i, 0)
                body(2 * i + 1, 1)
            body(B - 2, 0)
            body(B - 1, 1)

        with nc.Block() as block:

            @block.sync
            def _(sp):
                ctx_rows = d["ctx"].rearrange("b (p n) -> p b n", p=KP)
                ctx_cols = d["ctx_cols"].rearrange("b (p n) -> p b n", p=DC)

                def load_rows(b, u):
                    wait_from(sp, roped, b - 1)
                    sp.dma_start(raw[u][:, :, :].rearrange("p t e -> p (t e)"),
                                 ctx_rows[:, bass.ds(b, 1), :].rearrange("p b n -> p (b n)")).then_inc(raw_came[u], 16)

                def load_columns(b, u):
                    wait_from(sp, kA_ready, b - 1)
                    for to, v, at, n in ((0, 0, 0, DC), (0, 1, DC // 2, DC // 2), (DC // 2, 1, 0, DC // 2)):
                        sp.dma_start(rawT[u][to:to + n, v, :], ctx_cols[at:at + n, bass.ds(b, 1), :].rearrange("p b n -> p (b n)")).then_inc(rawT_came[u], 16)

                def load(b, u):
                    if not (isinstance(b, int) and b == 0):
                        load_rows(b, u)
                        load_columns(b, u)

                load_columns(0, 0)
                sp.dma_start(ropeT[:, :, :], d["rope_kT"].rearrange("(v p) n -> p v n", v=2)).then_inc(tablesT, 16)
                load_rows(0, 0)
                sp.dma_start(rope[:, :, :, :], d["rope_k"].rearrange("v p (t e) -> p v t e", t=KT)).then_inc(tables, 16)
                each_batch(sp, load)

            @block.gpsimd
            def _(pool):
                def rope_rows(b, u):
                    pool.wait_ge(raw_came[u], (b // 2 if isinstance(b, int) else (b - u) // 2) * 16 + 16)
                    wait_from(pool, val_ready, b - 1)
                    wait_from(pool, roped, b)
                    v = rows[u][:, :, :]
                    pool.tensor_tensor(v, raw[u][:, :, :], rope[:, 0, :, :], ALU.mult)
                    for lo, hi in ((0, 32), (32, 0)):
                        last = pool.tensor_tensor(turned_half[:, :, lo:lo + 32], raw[u][:, :, hi:hi + 32],
                                                  rope[:, 1, :, lo:lo + 32], ALU.mult)
                    last.then_inc(pool_chain, 1)
                    pool.wait_ge(pool_chain, b + 1)
                    pool.tensor_tensor(v, v, turned_half[:, :, :], ALU.add).then_inc(roped, 1)

                def rope_keys(b, u):
                    pool.wait_ge(rawT_came[u], (b // 2 if isinstance(b, int) else (b - u) // 2) * 48 + 48)
                    pool.tensor_tensor(rawT[u][:, :, :], rawT[u][:, :, :], ropeT[:, :, :], ALU.mult).then_inc(productT, 1)
                    pool.wait_ge(productT, b)
                    pool.tensor_tensor(rawT[u][:, 0, :], rawT[u][:, 0, :], rawT[u][:, 1, :], ALU.add).then_inc(ropedT, 1)

                def rope_batch(b, u):
                    if isinstance(b, int) and b == 0:
                        for v in range(2):
                            pool.memset(kB[v][64:128, :].bitcast(F32), 0.0).then_inc(filled, 1)
                            pool.memset(qB[v][64:128, :].bitcast(F32), 0.0).then_inc(filled, 1)
                        pool.wait_ge(filled, 4)
                        for v in range(2):
                            pool.memset(kB[v][64:65, :].bitcast(F32), 1.0).then_inc(filled, 1)
                        pool.wait_ge(filled, 6)
                        pool.wait_ge(tables, 16)
                        rope_rows(b, u)
                        for v in range(2):
                            pool.memset(val[v][:, :, DC:128], 1.0).then_inc(ones, 1)
                        pool.wait_ge(tablesT, 16)
                    else:
                        rope_keys(b, u)
                        rope_rows(b, u)

                each_batch(pool, rope_batch)

            @block.tensor
            def _(pe):
                def score_for_max(b, u, j, alone=False):
                    if j == 0:
                        wait_from(pe, row_ready, b)
                        pe.wait_ge(kA_ready, b + 1)
                        pe.wait_ge(qA_ready, b + 1)
                    else:
                        wait_from(pe, max_ready, b * QTL + j - (1 if alone else 0))
                    for m in range(3):
                        last = pe.matmul((psSO if alone and j % 2 else psW)[:, m, 0:500], qA[u][:, j * 128:(j + 1) * 128], kA[u][:, m * 500:(m + 1) * 500],
                                         start=True, stop=True)
                    last.then_inc(max_scores, 1)

                def turn_maxima(b, u):
                    pe.wait_ge(max_ready, b * QTL + QTL)
                    flat = psW[:, :, :].rearrange("p a n -> p (a n)")
                    for j in range(QTL):
                        last = pe.transpose(flat[0:1, j * 128:(j + 1) * 128], mx[:, u, j:j + 1], g.ident[:, :])
                    last.then_inc(row_turned, 1)

                def scores(b, u, t):
                    if t == 0:
                        pe.wait_ge(filled, 6)
                        pe.wait_ge(row_ready, b + 1)
                        pe.wait_ge(kB_ready, b + 1)
                        pe.wait_ge(qB_ready, b + 1)
                    wait_from(pe, exp_done, b * KT + t)
                    at = slice(t * KP, (t + 1) * KP)
                    for h in range(2):
                        pe.matmul(psS[0:KP, h, 0:GH], kA[u][:, at], qA[u][:, h * GH:(h + 1) * GH], start=True, stop=False)
                        last = pe.matmul(psS[0:KP, h, 0:GH], kB[u][:, at], qB[u][:, h * GH:(h + 1) * GH], start=False, stop=True)
                    last.then_inc(scores_done, 1)

                def attend(b, u, t):
                    pe.wait_ge(exp_done, b * KT + t + 1)
                    if t == 0:
                        pe.wait_ge(val_ready, b + 1)
                        pe.wait_ge(ones, 2)
                        wait_from(pe, o_copied, 2 * b)
                    for h in range(2):
                        last = pe.matmul(psO[:, h, 0:GH], val[u][:, t, :], w[t % 2][:, h * GH:(h + 1) * GH],
                                         start=(t == 0), stop=(t == KT - 1))
                    if t == KT - 1:
                        last.then_inc(av_done, 1)

                def batch(b, u):
                    ahead = not (isinstance(b, int) and b == B - 1)
                    for t in range(KT):
                        scores(b, u, t)
                        if t >= 1:
                            attend(b, u, t - 1)
                        elif not (isinstance(b, int) and b == 0):
                            attend(b - 1, 1 - u, KT - 1)
                        if ahead and MAX_FROM <= t < MAX_FROM + QTL:
                            score_for_max(b + 1, 1 - u, t - MAX_FROM)
                        if ahead and t == MAX_FROM + QTL:
                            turn_maxima(b + 1, 1 - u)

                for j in range(QTL):
                    score_for_max(0, 0, j, alone=True)
                turn_maxima(0, 0)
                each_batch(pe, batch)
                attend(B - 1, 1, KT - 1)

            @block.scalar
            def _(act):
                def copy_keys(b, u):
                    act.wait_ge(kA_ready, b + 1)
                    act.copy(kB[u][0:64, :], kA[u][0:64, :].bitcast(F32)).then_inc(kB_ready, 1)

                def take_maxima(b, u):
                    act.wait_ge(row_turned, b + 1)
                    act.wait_ge(filled, 4)
                    act.mul(qB[u][64:65, :], psW[:, :, :].rearrange("p a n -> p (a n)")[0:1, 0:G8], -1.0).then_inc(row_ready, 1)

                def copy_values(b, u):
                    act.wait_ge(roped, b + 1)
                    act.copy(val[u][:, :, 0:DC], rows[u][:, :, :]).then_inc(val_ready, 1)

                def take_attended(b):
                    act.wait_ge(av_done, b + 1)
                    wait_from(act, o_ready, 2 * b)
                    act.copy(osb[:, 0:GH], psO[:, 0, 0:GH]).then_inc(o_copied, 1)

                def exp(b, u, t):
                    act.wait_ge(scores_done, b * KT + t + 1)
                    act.activation(w[t % 2][:, :].rearrange("p (h n) -> p h n", h=2), psS[0:KP, :, 0:GH],
                                   ACT.Exp).then_inc(exp_done, 1)

                def batch(b, u):
                    ahead = not (isinstance(b, int) and b == B - 1)
                    for t in range(KT):
                        exp(b, u, t)
                        if t == 0 and not (isinstance(b, int) and b == 0):
                            take_attended(b - 1)
                        if ahead and t == 2:
                            copy_keys(b + 1, 1 - u)
                        if ahead and t == 3:
                            copy_values(b + 1, 1 - u)
                        if ahead and t == MAX_FROM + QTL:
                            take_maxima(b + 1, 1 - u)

                copy_values(0, 0)
                copy_keys(0, 0)
                take_maxima(0, 0)
                each_batch(act, batch)
                take_attended(B - 1)

            @block.vector
            def _(dve):
                def split_keys(b, u):
                    wait_from(dve, ropedT, b)
                    wait_from(dve, scores_done, (b - 1) * KT)
                    wait_from(dve, kB_ready, b - 1)
                    dve.tensor_copy(kA[u][0:64, :], rawT[u][:, 0, :]).then_inc(hi_ready, 1)
                    dve.wait_ge(hi_ready, b + 1)
                    dve.tensor_tensor(kA[u][64:128, :], rawT[u][:, 0, :], kA[u][0:64, :].bitcast(F32), ALU.subtract).then_inc(kA_ready, 1)

                def spread_queries(b, u):
                    for e in range(2):
                        src = q[e * 64:e * 64 + 64, :, bass.ds(b * S, S)]
                        for r in range(2):
                            last = dve.tensor_copy(qA[u][r * 64:r * 64 + 64, :].rearrange("p (j e s) -> p j e s", e=2, s=S)[:, :, e, :], src)
                    last.then_inc(qA_ready, 1)

                def split_queries(b, u):
                    dve.wait_ge(qA_ready, b + 1)
                    for e in range(2):
                        hi = qA[u][e * 64:e * 64 + 64, :].rearrange("p (j e s) -> p j e s", e=2, s=S)[:, :, e, :]
                        last = dve.tensor_tensor(qB[u][0:64, :].rearrange("p (j e s) -> p j e s", e=2, s=S)[:, :, e, :],
                                                 q[e * 64:e * 64 + 64, :, bass.ds(b * S, S)], hi.bitcast(F32), ALU.subtract)
                    last.then_inc(qB_ready, 1)

                def maximum(b, u, j, alone=False):
                    dve.wait_ge(max_scores, b * QTL + j + 1)
                    dve.tensor_reduce(mx[:, u, j:j + 1], (psSO if alone and j % 2 else psW)[:, 0:3, 0:500], mybir.AxisListType.XY, ALU.max).then_inc(max_ready, 1)

                def empty(b):
                    dve.wait_ge(av_done, b + 1)
                    wait_from(dve, o_ready, 2 * b)
                    dve.tensor_copy(osb[:, GH:G8], psO[:, 1, 0:GH]).then_inc(o_copied, 1)

                def invert(b, j):
                    at = slice(j * 128, (j + 1) * 128)
                    if j == 0:
                        dve.wait_ge(o_copied, 2 * b + 2)
                    dve.reciprocal(rec[:, at], osb[64:128, at]).then_inc(rec_ready, 1)

                def normalise(b):
                    dve.wait_ge(rec_ready, (b + 1) * QTL)
                    for e in range(2):
                        pick = lambda v: v.rearrange("p (j e s) -> p j e s", e=2, s=S)[:, :, e, :]
                        dve.tensor_tensor(q[e * 64:e * 64 + 64, :, bass.ds(b * S, S)], pick(osb[0:64, :]), pick(rec[:, :]),
                                          ALU.mult).then_inc(o_ready, 1)

                def batch(b, u):
                    first = isinstance(b, int) and b == 0
                    ahead = not (isinstance(b, int) and b == B - 1)
                    if not first:
                        empty(b - 1)
                    if ahead:
                        split_keys(b + 1, 1 - u)
                        spread_queries(b + 1, 1 - u)
                    for j in range(QTL):
                        if ahead:
                            maximum(b + 1, 1 - u, j)
                        if not first:
                            invert(b - 1, j)
                    if ahead:
                        split_queries(b + 1, 1 - u)
                    if not first:
                        normalise(b - 1)

                dve.wait_ge(rawT_came[0], 48)
                dve.wait_ge(tablesT, 16)
                dve.tensor_tensor(rawT[0][:, :, :], rawT[0][:, :, :], ropeT[:, :, :], ALU.mult).then_inc(first_keys, 1)
                dve.wait_ge(first_keys, 1)
                dve.tensor_tensor(rawT[0][:, 0, :], rawT[0][:, 0, :], rawT[0][:, 1, :], ALU.add).then_inc(first_keys, 1)
                dve.wait_ge(first_keys, 2)
                split_keys(0, 0)
                spread_queries(0, 0)
                for j in range(QTL):
                    maximum(0, 0, j, alone=True)
                split_queries(0, 0)
                each_batch(dve, batch)
                empty(B - 1)
                for j in range(QTL):
                    invert(B - 1, j)
                normalise(B - 1)


def latent_output(nc, g, layer, q, fold, ahead):
    gate = g.gates[0:TP, layer:layer + 1]
    with ExitStack() as ctx:
        a = Alloc(nc, ctx, f"out{layer}", g.arena)
        ps = a.ps("ps", [128, 2, 512])
        y_done, x_done, stats_done = a.sem("y_done"), a.sem("x_done"), a.sem("stats_done")
        norm = Norm(nc, a, g)
        with nc.Block() as block:

            @block.sync
            def _(sp):
                ahead.load(sp)
                ahead.wait(sp)

            @block.tensor
            def _(pe):
                for t in range(NT):
                    if t >= 2:
                        pe.wait_ge(x_done, t - 1)
                    for j in range(HP):
                        last = pe.matmul(ps[0:TP, t % 2, 0:C], q[:, j, t * TP:(t + 1) * TP], fold[:, j, :],
                                         start=(j == 0), stop=(j == HP - 1))
                    last.then_inc(y_done, 1)
                    if t >= 2:
                        norm.tensor_tile(pe, t - 2)
                norm.tensor_tile(pe, NT - 2)
                norm.tensor_tile(pe, NT - 1)

            @block.scalar
            def _(act):
                for t in range(NT):
                    norm.root_tile(act, t)
                    if t >= 2:
                        norm.scalar_tile(act, t - 2)
                norm.scalar_tile(act, NT - 2)
                norm.scalar_tile(act, NT - 1)

            @block.vector
            def _(dve):
                for t in range(NT):
                    dve.wait_ge(y_done, t + 1)
                    dve.scalar_tensor_tensor(out=g.x[:, t, :], in0=ps[0:TP, t % 2, 0:C], scalar=gate, in1=g.x[:, t, :],
                                             op0=ALU.mult, op1=ALU.add).then_inc(x_done, 1)
                    take_moments(dve, g, t, x_done, t + 1, stats_done).then_inc(norm.mv_ready, 1)
                    if t >= 1:
                        norm.vector_tile(dve, t - 1)
                norm.vector_tile(dve, NT - 1)


def latent_layer(nc, g, d, layer, queries, weights, following):
    queries(nc, g, d, g.q, g.fold, weights)
    weights.ctx.close()
    g.arena.ctx.close()
    latent_attention(nc, g, d, layer, g.q)
    g.arena = Arena(nc, f"arena{layer}", SHARED_WORDS)
    ahead = following(nc, g, d)
    latent_output(nc, g, layer, g.q, g.fold, ahead)
    return ahead


def butterflies(eng, step, v, w, done, levels=(4, 2, 1)):
    src, dst = v, w
    for h in levels:
        pick = lambda t, k: t.rearrange("p (a u h) n -> p u a h n", u=2, h=h)[:, k, :, :, :]
        step(eng.tensor_tensor(pick(dst, 0), pick(src, 0), pick(src, 1), ALU.add))
        last = eng.tensor_tensor(pick(dst, 1), pick(src, 0), pick(src, 1), ALU.subtract)
        if h != levels[-1]:
            step(last)
        src, dst = dst, src
    last.then_inc(done, 1)


def ternary_weights(nc, g, d):
    w = Weights(nc, g, "ffn1_w")
    split = lambda m, n: lambda v: v[:, m, :].rearrange("p (c n) -> p c n", c=n)
    w.wf = w.put([128, 3, 2 * FF], *((split(m, n), d[name].rearrange("(c p) n -> p c n", p=128))
                                     for m, (name, n) in enumerate((("L1_gate", CC), ("L1_up", CC), ("L1_down", FF // 128)))))
    w.had256 = w.put([128, CC, C], (None, d["had256"].rearrange("(c p) n -> p c n", p=128)))
    w.had128 = w.put([128, 128], (None, d["had128"]))
    w.part = w.put([48, 3], (None, d["lanes"]))
    return w


def ternary_ffn(nc, g, w, ahead):
    gate = g.gates[0:TP, 5:6]
    NF = FF // 128
    with ExitStack() as ctx:
        a = Alloc(nc, ctx, "ffn1", g.arena)
        wf, had256, had128, part = w.wf, w.had256, w.had128, w.part
        wb = a.sb("wb", [128, 3, 2 * FF], BF16)
        identb = a.sb("identb", [128, 128], BF16)
        onesm = a.sb("onesm", [128, 128])
        su_ready = a.sem("su_ready")
        y_taken = a.sem("y_taken")
        first_level = a.sem("first_level")
        ws = a.sb("ws", [128, 3])
        rws = a.sb("rws", [128, 3])
        xh = a.sb("xh", [TP, NT, C])
        xq = a.sb("xq", [TP, NT, C], BF16)
        xqT = a.sb("xqT", [128, CC, T], BF16)
        sx = a.sb("sx", [TP, NT])
        rx = a.sb("rx", [TP, NT])
        su = a.sb("su", [TP, 2, NT])
        s2 = a.sb("s2", [TP, NT])
        r2 = a.sb("r2", [TP, NT])
        h = a.sb("h", [TP, 2, FF])
        h2 = a.sb("h2", [TP, 2, FF])
        hT = a.sb("hT", [128, NF, TP])
        yq = a.sb("yq", [TP, FF], BF16)
        yqT = a.sb("yqT", [128, NF, TP], BF16)
        ps_gu = a.ps("ps_gu", [128, 4, 512])
        ps_t = a.ps("ps_t", [128, 2, 512])
        ps_y = a.ps("ps_y", [128, 2, 512])
        (ready, sums, w_ready, xh_done, xh_taken, xq_ready, xq_turned, xqT_ready, gu_done, silu_done, product_done, h_ready,
         h_turned, hT_ready, y_done, yq_ready, yq_turned, yqT_ready, o_done, x_done, pool_chain, chain) = (
            a.sem(n) for n in ("ready", "sums", "w_ready", "xh_done", "xh_taken", "xq_ready", "xq_turned", "xqT_ready",
                               "gu_done", "silu_done", "product_done", "h_ready", "h_turned", "hT_ready", "y_done", "yq_ready",
                               "yq_turned", "yqT_ready", "o_done", "x_done", "pool_chain", "dve_chain"))
        with nc.Block() as block:

            @block.sync
            def _(sp):
                ahead.load(sp)
                ahead.wait(sp)

            @block.gpsimd
            def _(pool):
                pool.memset(onesm[:, :], 1.0).then_inc(ready, 1)
                pool.tensor_copy(identb[:, :], g.ident[:, :]).then_inc(ready, 1)
                ahead.clear(pool)
                step = Chain(pool, pool_chain)
                for t in range(NT):
                    pool.wait_ge(first_level, t + 1)
                    v, w = (z[:, t % 2, :].rearrange("p (k n) -> p k n", n=128) for z in (h2, h))
                    butterflies(pool, step, v, w, h_ready, (2, 1))

            @block.tensor
            def _(pe):
                pe.wait_ge(ready, 3)
                pe.matmul(ps_gu[:, 0, 0:3], onesm[0:48, :], part[:, :], start=True, stop=True).then_inc(sums, 1)
                for t in range(NT):
                    if t >= 2:
                        pe.wait_ge(xh_taken, t - 1)
                    for c in range(CC):
                        last = pe.matmul(ps_y[0:TP, t % 2, 0:C], g.xnT[:, c, t * TP:(t + 1) * TP], had256[:, c, :],
                                         start=(c == 0), stop=(c == CC - 1))
                    last.then_inc(xh_done, 1)
                pe.wait_ge(xq_ready, 1)
                for t in range(NT):
                    if t >= 2:
                        pe.wait_ge(xqT_ready, t - 1)
                    tb = ps_t[:, t % 2, :].bitcast(BF16)
                    for c in range(CC):
                        last = pe.transpose(tb[:, c * TP:(c + 1) * TP], xq[:, t, c * 128:(c + 1) * 128], identb[0:TP, 0:TP])
                    last.then_inc(xq_turned, 1)
                pe.wait_ge(xqT_ready, NT)
                pe.wait_ge(w_ready, 2)

                def inner(t):
                    if t >= 1:
                        pe.wait_ge(product_done, t)
                    for m in range(2):
                        for n in range(2):
                            for c in range(CC):
                                last = pe.matmul(ps_gu[0:TP, 2 * m + n, :], xqT[:, c, t * TP:(t + 1) * TP],
                                                 wb[:, m, c * FF + n * 512:c * FF + n * 512 + 512],
                                                 start=(c == 0), stop=(c == CC - 1))
                    last.then_inc(gu_done, 1)

                def turn_h(t):
                    pe.wait_ge(h_ready, t + 1)
                    if t >= 2:
                        pe.wait_ge(yqT_ready, t - 1)
                        pe.wait_ge(x_done, t - 1)
                    for k in range(NF):
                        last = pe.transpose(ps_t[:, k // 4, (k % 4) * TP:(k % 4 + 1) * TP], h2[:, t % 2, k * 128:(k + 1) * 128],
                                            g.ident[0:TP, 0:TP])
                    last.then_inc(h_turned, 1)

                def rotate(t):
                    pe.wait_ge(hT_ready, t + 1)
                    if t >= 1:
                        pe.wait_ge(y_taken, t)
                    for k in range(NF):
                        last = pe.matmul(ps_y[0:TP, k // 4, (k % 4) * 128:(k % 4 + 1) * 128], hT[:, k, :], had128[:, :],
                                         start=True, stop=True)
                    last.then_inc(y_done, 1)

                def turn_quantised(t):
                    pe.wait_ge(yq_ready, t + 1)
                    pe.wait_ge(hT_ready, min(t + 2, NT))
                    tb = ps_t[:, 0, :].bitcast(BF16)
                    for k in range(NF):
                        last = pe.transpose(tb[:, k * TP:(k + 1) * TP], yq[:, k * 128:(k + 1) * 128], identb[0:TP, 0:TP])
                    last.then_inc(yq_turned, 1)

                def down(t):
                    if t == 0:
                        pe.wait_ge(w_ready, 3)
                    if t == NT - 1:
                        pe.wait_ge(x_done, t)
                    pe.wait_ge(yqT_ready, t + 1)
                    for k in range(NF):
                        last = pe.matmul(ps_t[0:TP, 1, 0:C], yqT[:, k, :], wb[:, 2, k * C:(k + 1) * C],
                                         start=(k == 0), stop=(k == NF - 1))
                    last.then_inc(o_done, 1)

                for i in range(NT + 3):
                    if i < NT:
                        inner(i)
                    if 2 <= i < NT + 2:
                        turn_h(i - 2)
                    if 2 <= i < NT + 2:
                        rotate(i - 2)
                    if i >= 3:
                        turn_quantised(i - 3)
                        down(i - 3)

            @block.scalar
            def _(act):
                for t in range(NT):
                    act.wait_ge(xh_done, t + 1)
                    act.copy(xh[:, t, :], ps_y[0:TP, t % 2, 0:C]).then_inc(xh_taken, 1)
                for t in range(NT):
                    act.wait_ge(xq_turned, t + 1)
                    act.copy(xqT[:, :, t * TP:(t + 1) * TP],
                             ps_t[:, t % 2, :].bitcast(BF16)[:, 0:2 * TP].rearrange("p (c n) -> p c n", c=CC)).then_inc(xqT_ready, 1)

                def silu(t):
                    act.wait_ge(gu_done, t + 1)
                    if t >= 2:
                        act.wait_ge(h_ready, t - 1)
                    act.activation(h[:, t % 2, :].rearrange("p (n m) -> p n m", n=2), ps_gu[0:TP, 0:2, :], ACT.Silu,
                                   scale=su[:, 0, t:t + 1]).then_inc(silu_done, 1)

                def take_h(t):
                    act.wait_ge(h_turned, t + 1)
                    if t >= 1:
                        act.wait_ge(y_done, t)
                    act.copy(hT[:, :, :].rearrange("p (u k) n -> p u (k n)", u=2), ps_t[:, :, 0:4 * TP]).then_inc(hT_ready, 1)

                def take_quantised(t):
                    act.wait_ge(yq_turned, t + 1)
                    if t >= 1:
                        act.wait_ge(o_done, t)
                    act.copy(yqT[:, :, :].rearrange("p k n -> p (k n)"), ps_t[:, 0, :].bitcast(BF16)[:, 0:NF * TP]).then_inc(yqT_ready, 1)

                act.wait_ge(w_ready, 2)
                act.wait_ge(su_ready, 1)
                for i in range(NT + 3):
                    if i < NT:
                        silu(i)
                    if 2 <= i < NT + 2:
                        take_h(i - 2)
                    if i >= 3:
                        take_quantised(i - 3)

            @block.vector
            def _(dve):
                step = Chain(dve, chain)
                dve.tensor_scalar(part[:, :], part[:, :], g.magnitudes[:, :], None, ALU.mult).then_inc(ready, 1)
                dve.wait_ge(sums, 1)
                step(dve.tensor_scalar(ws[:, :], ps_gu[:, 0, 0:3], 1.0 / (FF * C), 1e-5, ALU.mult, ALU.max))
                step(dve.reciprocal(rws[:, :], ws[:, :]))

                def quantise_weights(m):
                    step(dve.tensor_scalar(wf[:, m, :], wf[:, m, :], rws[:, m:m + 1], 1.0, ALU.mult, ALU.min))
                    step(dve.tensor_scalar(wf[:, m, :], wf[:, m, :], -1.0, ROUND, ALU.max, ALU.add))
                    dve.tensor_scalar(wb[:, m, :], wf[:, m, :], -ROUND, None, ALU.add).then_inc(w_ready, 1)

                def quantise_scales(s, r, most, root):
                    step(dve.tensor_scalar(s, most, 1.0 / root, 1e-5, ALU.mult, ALU.max))
                    step(dve.reciprocal(r, s))
                    step(dve.tensor_scalar(r, r, 127.0, 1.0 / root, ALU.mult, ALU.mult))
                    step(dve.tensor_scalar(s, s, 1.0 / 127.0, None, ALU.mult))

                quantise_weights(0)
                quantise_weights(1)
                dve.wait_ge(xh_taken, NT)
                step(dve.tensor_reduce(rx[:, :], xh[:, :, :], X, ALU.max, apply_absolute_value=True))
                quantise_scales(sx[:, :], rx[:, :], rx[:, :], 16.0)
                step(dve.tensor_tensor(xh[:, :, :], xh[:, :, :], rx[:, :].unsqueeze(2).to_broadcast([TP, NT, C]), ALU.mult))
                step(dve.tensor_scalar(xh[:, :, :], xh[:, :, :], 127.0, -128.0, ALU.min, ALU.max))
                dve.tensor_scalar(xq[:, :, :], xh[:, :, :], ROUND, -ROUND, ALU.add, ALU.add).then_inc(xq_ready, 1)
                for m in range(2):
                    last = dve.tensor_scalar(su[:, m, :], sx[:, :], ws[0:TP, m:m + 1], None, ALU.mult)
                last.then_inc(su_ready, 1)
                dve.wait_ge(su_ready, 1)
                step(dve.tensor_scalar(ws[:, 2:3], ws[:, 2:3], g.gates[:, 5:6], None, ALU.mult))

                def product(t):
                    u = t % 2
                    dve.wait_ge(silu_done, t + 1)
                    dve.scalar_tensor_tensor(out=h[:, u, :].rearrange("p (n m) -> p n m", n=2), in0=ps_gu[0:TP, 2:4, :],
                                             scalar=su[:, 1, t:t + 1], in1=h[:, u, :].rearrange("p (n m) -> p n m", n=2),
                                             op0=ALU.mult, op1=ALU.mult).then_inc(product_done, 1)
                    dve.wait_ge(product_done, t + 1)
                    if t >= 2:
                        dve.wait_ge(h_turned, t - 1)
                    v, w = (z[:, u, :].rearrange("p (k n) -> p k n", n=128) for z in (h, h2))
                    butterflies(dve, step, v, w, first_level, (4,))

                def quantise(t, between):
                    at = slice(t, t + 1)
                    dve.wait_ge(y_done, t + 1)
                    step(dve.tensor_reduce(r2[:, at], ps_y[0:TP, :, :], mybir.AxisListType.XY, ALU.max, apply_absolute_value=True))
                    quantise_scales(s2[:, at], r2[:, at], r2[:, at], 32.0)
                    step(dve.tensor_scalar(s2[:, at], s2[:, at], ws[0:TP, 2:3], None, ALU.mult))
                    wide = xh[:, 0:4, :].rearrange("p a n -> p (a n)")
                    dve.tensor_scalar(wide.rearrange("p (a n) -> p a n", a=2), ps_y[0:TP, :, :], r2[:, at], 127.0,
                                      ALU.mult, ALU.min).then_inc(y_taken, 1)
                    between()
                    dve.wait_ge(y_taken, t + 1)
                    step(dve.tensor_scalar(wide, wide, -128.0, ROUND, ALU.max, ALU.add))
                    if t >= 1:
                        dve.wait_ge(yq_turned, t)
                    dve.tensor_scalar(yq[:, :], wide, -ROUND, None, ALU.add).then_inc(yq_ready, 1)

                def add(t):
                    dve.wait_ge(o_done, t + 1)
                    dve.scalar_tensor_tensor(out=g.x[:, t, :], in0=ps_t[0:TP, 1, 0:C], scalar=s2[:, t:t + 1], in1=g.x[:, t, :],
                                             op0=ALU.mult, op1=ALU.add).then_inc(x_done, 1)

                for i in range(NT + 3):
                    if i < NT:
                        product(i)
                    if i == 1:
                        quantise_weights(2)
                    before = (lambda: add(i - 3)) if i >= 3 else (lambda: None)
                    if 2 <= i < NT + 2:
                        quantise(i - 2, before)
                    else:
                        before()


def hadamard_weights(nc, g, d):
    w = Weights(nc, g, "ffn2_w")
    chunks = lambda v: v.rearrange("(c p) n -> p c n", p=128)
    w.wd = w.put([128, FF // 128, C], (None, chunks(d["L2_down"])))
    w.had128 = w.put([128, 128], (None, d["had128"]))
    w.had256 = w.put([128, CC, C], (None, chunks(d["had256"])))
    w.su_ug = w.put([128, CC], (None, d["L2_su_ug"]))
    w.su_dp = w.put([128, FF // 128], (None, d["L2_su_dp"]))
    w.sc_ug = w.put([128, 2 * FF // 128], (None, d["L2_sc_ug"]))
    w.sc_dp = w.put([128, C], (None, d["L2_sc_dp"].partition_broadcast(128)))
    w.wu = w.put([128, CC, FF], (None, chunks(d["L2_up"])))
    w.wg = w.put([128, CC, FF], (None, chunks(d["L2_gate"])))
    return w


def hadamard_ffn(nc, g, weights, ahead):
    gate = g.gates[0:TP, 6:7]
    NF = FF // 128
    with ExitStack() as ctx:
        a = Alloc(nc, ctx, "ffn2", g.arena)
        had256, had128, su_ug, su_dp, sc_ug, sc_dp, wu, wg, wd = (
            weights.had256, weights.had128, weights.su_ug, weights.su_dp, weights.sc_ug, weights.sc_dp, weights.wu, weights.wg, weights.wd)
        wd2 = a.sb("wd2", [128, NF, C])
        xr = a.sb("xr", [128, CC, T])
        s = a.sb("s", [128, 2, HALF])
        hT = a.sb("hT", [128, NF, T])
        ps_u = a.ps("ps_u", [128, 2, 512])
        ps_g = a.ps("ps_g", [128, 2, 512])
        ps_d = a.ps("ps_d", [128, 2, 512])
        stats_done = a.sem("stats_done")
        (had_ready, wd_ready, fold_done, fold_ready, xr_done, xr_ready, u_done, g_done, s_ready, h_ready, y_done, x_done,
         pool_chain, chain) = (a.sem(n) for n in ("had_ready", "wd_ready", "fold_done", "fold_ready", "xr_done", "xr_ready",
                                                  "u_done", "g_done", "s_ready", "h_ready", "y_done", "x_done", "pool_chain", "dve_chain"))
        with nc.Block() as block:

            @block.sync
            def _(sp):
                ahead.load(sp)
                ahead.wait(sp)

            @block.gpsimd
            def _(pool):
                butterflies(pool, Chain(pool, pool_chain), wd[:, :, :], wd2[:, :, :], wd_ready)

            @block.tensor
            def _(pe):
                pe.wait_ge(had_ready, CC)
                for n in range(4):
                    m, h = n // 2, n % 2
                    if n >= 2:
                        pe.wait_ge(xr_ready, n - 1)
                    for c in range(CC):
                        last = pe.matmul(ps_u[:, n % 2, 0:HALF], had256[:, c, m * 128:(m + 1) * 128],
                                         g.xnT[:, c, h * HALF:(h + 1) * HALF], start=(c == 0), stop=(c == CC - 1))
                    last.then_inc(xr_done, 1)
                pe.wait_ge(xr_ready, 4)
                for n in range(2 * NF):
                    m, h = n // 2, n % 2
                    if n >= 2:
                        pe.wait_ge(h_ready, n - 1)
                    for w, ps, done in ((wg, ps_g, g_done), (wu, ps_u, u_done)):
                        for c in range(CC):
                            last = pe.matmul(ps[:, n % 2, 0:HALF], w[:, c, m * 128:(m + 1) * 128],
                                             xr[:, c, h * HALF:(h + 1) * HALF], start=(c == 0), stop=(c == CC - 1))
                        last.then_inc(done, 1)
                pe.wait_ge(wd_ready, 1)
                for k in range(NF):
                    if k >= 2:
                        pe.wait_ge(fold_ready, k - 1)
                    pe.matmul(ps_d[:, k % 2, 0:C], had128[:, :], wd2[:, k, :], start=True, stop=True).then_inc(fold_done, 1)
                pe.wait_ge(fold_ready, NF)
                pe.wait_ge(h_ready, 2 * NF)
                for t in range(NT):
                    if t >= 2:
                        pe.wait_ge(x_done, t - 1)
                    for k in range(NF):
                        last = pe.matmul(ps_d[0:TP, t % 2, 0:C], hT[:, k, t * TP:(t + 1) * TP], wd[:, k, :],
                                         start=(k == 0), stop=(k == NF - 1))
                    last.then_inc(y_done, 1)

            @block.scalar
            def _(act):
                for n in range(4):
                    m, h = n // 2, n % 2
                    act.wait_ge(xr_done, n + 1)
                    act.copy(xr[:, m, h * HALF:(h + 1) * HALF], ps_u[:, n % 2, 0:HALF]).then_inc(xr_ready, 1)
                act.wait_ge(had_ready, CC + 2)
                for n in range(2 * NF):
                    act.wait_ge(g_done, n + 1)
                    if n >= 2:
                        act.wait_ge(h_ready, n - 1)
                    act.activation(s[:, n % 2, :], ps_g[:, n % 2, 0:HALF], ACT.Silu, scale=sc_ug[:, NF + n // 2:NF + n // 2 + 1]).then_inc(s_ready, 1)

            @block.vector
            def _(dve):
                step = Chain(dve, chain)
                for c in range(CC):
                    dve.tensor_scalar(had256[:, c, :], had256[:, c, :], su_ug[:, c:c + 1], None, ALU.mult).then_inc(had_ready, 1)
                step(dve.tensor_scalar(sc_ug[:, :], sc_ug[:, :], 1.0 / 16.0, None, ALU.mult))
                dve.tensor_tensor(sc_ug[:, 0:NF], sc_ug[:, 0:NF], su_dp[:, :], ALU.mult).then_inc(had_ready, 1)
                dve.tensor_scalar(sc_dp[:, :], sc_dp[:, :], 1.0 / 32.0, None, ALU.mult).then_inc(had_ready, 1)
                dve.wait_ge(had_ready, CC + 2)
                for n in range(2 * NF):
                    m, h = n // 2, n % 2
                    dve.wait_ge(s_ready, n + 1)
                    dve.wait_ge(u_done, n + 1)
                    dve.scalar_tensor_tensor(out=hT[:, m, h * HALF:(h + 1) * HALF], in0=ps_u[:, n % 2, 0:HALF], scalar=sc_ug[:, m:m + 1],
                                             in1=s[:, n % 2, :], op0=ALU.mult, op1=ALU.mult).then_inc(h_ready, 1)
                for k in range(NF):
                    dve.wait_ge(fold_done, k + 1)
                    dve.tensor_tensor(wd[:, k, :], ps_d[:, k % 2, 0:C], sc_dp[:, :], ALU.mult).then_inc(fold_ready, 1)
                for t in range(NT):
                    dve.wait_ge(y_done, t + 1)
                    dve.scalar_tensor_tensor(out=g.x[:, t, :], in0=ps_d[0:TP, t % 2, 0:C], scalar=gate, in1=g.x[:, t, :],
                                             op0=ALU.mult, op1=ALU.add).then_inc(x_done, 1)
                    take_moments(dve, g, t, x_done, t + 1, stats_done)


def experts_weights(nc, g, d):
    w = Weights(nc, g, "ffn3_w")
    w.rw = w.put([128, CC, NE], (None, d["L3_rw"].rearrange("(c p) n -> p c n", p=128)))
    w.later = w.put([128, NE], (None, d["later"]))
    w.before = w.put([TP, TP], (None, d["before"]))
    w.numbers = w.put([1, SLOT_TILES], (None, d["numbers"]))
    w.wsgu = w.put([128, CC, 2 * F3], (None, d["L3_sgu"].rearrange("(c p) n -> p c n", p=128)))
    w.wsdn = w.put([128, F3 // 128, C], (None, d["L3_sdn"].rearrange("(c p) n -> p c n", p=128)))
    a = Alloc(nc, w.ctx, "experts", g.arena)
    g.wgu = a.sb("wgu", [128, NE, CC, 2 * F3])
    g.wgu_came = a.sem("wgu_came")
    return w


def load_experts(g, d, sp):
    for e in range(NE):
        sp.dma_start(g.wgu[:, e, :, :], d["L3_gu"][e].rearrange("(c p) n -> p c n", p=128)).then_inc(g.wgu_came, 16)


def experts_ffn(nc, g, d, weights, out):
    F4 = F3 // 128
    gate = g.gates[0:TP, 7:8]
    with ExitStack() as ctx:
        a = Alloc(nc, ctx, "ffn3", g.arena)
        rw, later, before, numbers, wsgu, wsdn = weights.rw, weights.later, weights.before, weights.numbers, weights.wsgu, weights.wsdn
        ones = a.sb("ones", [TP, TP])
        lg = a.sb("lg", [TP, NT, NE])
        own = a.sb("own", [TP, NT, NE])
        top = a.sb("top", [TP, NT])
        first = a.sb("first", [TP, NT])
        cum = a.sb("cum", [TP, NT + 1, NE])
        tiles = a.sb("tiles", [TP, NE])
        ends = a.sb("ends", [TP, NE])
        base = a.sb("base", [TP, NE])
        slot = a.sb("slot", [TP, NT], mybir.dt.int32)
        passed = a.sb("passed", [1, SLOT_TILES, NE])
        of_tile = a.sb("of_tile", [1, SLOT_TILES])
        of_tile_i = a.sb("of_tile_i", [1, SLOT_TILES], mybir.dt.int32)
        sg = a.sb("sg", [TP, NT])
        wdn = a.sb("wdn", [128, NE, F4, C])
        s = a.sb("s", [128, 2, 512])
        hT = a.sb("hT", [128, F4, T])
        rows = a.sb("rows", [128, SLOT_TILES, C])
        xT = a.sb("xT", [128, 2, CC, 128])
        inner = a.sb("inner", [128, 2, F3])
        innerT = a.sb("innerT", [128, 2, F4, 128])
        norm = Norm(nc, a, g, moments=True)
        ps_d = a.ps("ps_d", [128, 2, 512])
        ps_u = a.ps("ps_u", [128, 2, 512])
        ps_g = a.ps("ps_g", [128, 2, 512])
        ps_t = norm.turned
        (wdn_came, cleared, zero_stored, l_done, top_ready, sg_ready, xs_ready, own_ready, places_done,
         slots_ready, scattered, first_came, rest_came, g_done, u_done, s_ready, h_ready, turned, xT_ready, gate_done, up_done,
         silu_done, inner_ready, inner_turned, innerT_ready, down_done, y_ready, y_stored, o_done, x_done, chain) = (
            a.sem(n) for n in ("wdn_came", "cleared", "zero_stored", "l_done", "top_ready", "sg_ready",
                               "xs_ready", "own_ready", "places_done", "slots_ready", "scattered", "first_came", "rest_came",
                               "g_done", "u_done", "s_ready", "h_ready", "turned", "xT_ready", "gate_done", "up_done", "silu_done",
                               "inner_ready", "inner_turned", "innerT_ready", "down_done", "y_ready", "y_stored", "o_done", "x_done", "dve_chain"))
        stored = a.sem("stored")
        gathered = [a.sem(f"gathered{t}") for t in range(NT)]
        sorted_x = nc.dram_tensor("sorted_x", (SLOT_TILES * 128, C), F32).ap()
        sorted_y = nc.dram_tensor("sorted_y", (SLOT_TILES * 128, C), F32).ap()
        tiled = lambda v: v.rearrange("(j p) c -> p j c", p=128)
        UNITS = 2 * F4
        with nc.Block() as block:

            @block.sync
            def _(sp):
                sp.wait_ge(cleared, 2)
                sp.dma_start(tiled(sorted_x), rows[:, :, :]).then_inc(zero_stored, 16)
                for e in range(NE):
                    sp.dma_start(wdn[:, e, :, :], d["L3_dn"][e].rearrange("(c p) n -> p c n", p=128)).then_inc(wdn_came, 16)
                sp.wait_ge(scattered, 16 * NT)
                sp.dma_start(rows[:, 0:2, :], tiled(sorted_x)[:, 0:2, :]).then_inc(first_came, 16)
                sp.dma_start(rows[:, 2:, :], tiled(sorted_x)[:, 2:, :]).then_inc(rest_came, 16)
                for j in range(SLOT_TILES):
                    sp.wait_ge(y_ready, j + 1)
                    sp.dma_start(tiled(sorted_y)[:, j, :], rows[:, j, :]).then_inc(y_stored, 16)
                for t in range(NT):
                    sp.wait_ge(x_done, NT + t + 1)
                    sp.dma_start(out.rearrange("(t p) c -> p t c", p=TP)[:, t, :], g.x[:, t, :]).then_inc(stored, 16)
                sp.wait_ge(stored, 16 * NT)

            @block.gpsimd
            def _(pool):
                pool.memset(ones[:, :], 1.0).then_inc(cleared, 1)
                pool.memset(rows[:, :, :], 0.0).then_inc(cleared, 1)
                pool.wait_ge(zero_stored, 16)
                pool.wait_ge(xs_ready, NT)
                pool.wait_ge(slots_ready, 1)
                for t in range(NT):
                    pool.indirect_dma_start(out=sorted_x, out_offset=bass.IndirectOffsetOnAxis(ap=slot[:, t:t + 1], axis=0),
                                            in_=g.xn[:, t, :], in_offset=None).then_inc(scattered, 16)
                pool.wait_ge(y_stored, 16 * SLOT_TILES)
                for t in range(NT):
                    pool.indirect_dma_start(out=g.xn[:, t, :], out_offset=None, in_=sorted_y,
                                            in_offset=bass.IndirectOffsetOnAxis(ap=slot[:, t:t + 1], axis=0)).then_inc(gathered[t], 16)

            @block.tensor
            def _(pe):
                norm.tensor(pe)
                for t in range(NT):
                    pe.wait_ge(norm.xnT_ready, t + 1)
                    for c in range(CC):
                        last = pe.matmul(ps_d[0:TP, 0, t * NE:(t + 1) * NE], g.xnT[:, c, t * TP:(t + 1) * TP], rw[:, c, :],
                                         start=(c == 0), stop=(c == CC - 1))
                last.then_inc(l_done, 1)

                def shared_unit(n):
                    m, h = n // 2, n % 2
                    if n >= 2:
                        pe.wait_ge(h_ready, n - 1)
                    for off, ps, done in ((0, ps_g, g_done), (F3, ps_u, u_done)):
                        for c in range(CC):
                            last = pe.matmul(ps[:, n % 2, 0:HALF], wsgu[:, c, off + m * 128:off + (m + 1) * 128],
                                             g.xnT[:, c, h * HALF:(h + 1) * HALF], start=(c == 0), stop=(c == CC - 1))
                        last.then_inc(done, 1)

                shared_unit(0)
                shared_unit(1)
                pe.wait_ge(own_ready, 1)
                pe.wait_ge(cleared, 1)
                wide = lambda v: v.rearrange("p t e -> p (t e)")
                pe.matmul(ps_d[0:TP, 1, 0:NT * NE], before[:, :], wide(own[:, :, :]), start=True, stop=False)
                pe.matmul(ps_d[0:TP, 1, 0:NT * NE], ones[:, :], wide(cum[:, 0:NT, :]), start=False, stop=True)
                pe.matmul(ps_d[0:TP, 1, NT * NE:(NT + 1) * NE], ones[:, :], cum[:, NT, :], start=True, stop=True).then_inc(places_done, 1)
                for n in range(2, UNITS):
                    shared_unit(n)

                def turn(j):
                    pe.wait_ge(first_came if j < 2 else rest_came, 16)
                    if j >= 1:
                        pe.wait_ge(xT_ready, j)
                    for c in range(CC):
                        last = pe.transpose(ps_t[:, 0, c * 128:(c + 1) * 128], rows[:, j, c * 128:(c + 1) * 128], g.ident[:, :])
                    last.then_inc(turned, 1)

                def gate_up(j):
                    expert = pe.value_load(of_tile_i[0:1, j:j + 1], min_val=0, max_val=NE - 1)
                    pe.wait_ge(xT_ready, j + 1)
                    if j >= 2:
                        pe.wait_ge(inner_ready, j - 1)
                    for off, ps, done in ((0, ps_g, gate_done), (F3, ps_u, up_done)):
                        for c in range(CC):
                            w = g.wgu[:, bass.ds(expert, 1), c, off:off + F3].rearrange("p e n -> p (e n)")
                            last = pe.matmul(ps[:, j % 2, :], xT[:, j % 2, c, :], w, start=(c == 0), stop=(c == CC - 1))
                        last.then_inc(done, 1)
                    return expert

                def turn_inner(j):
                    pe.wait_ge(inner_ready, j + 1)
                    if j >= 1:
                        pe.wait_ge(innerT_ready, j)
                    for k in range(F4):
                        last = pe.transpose(ps_t[:, 1, k * 128:(k + 1) * 128], inner[:, j % 2, k * 128:(k + 1) * 128], g.ident[:, :])
                    last.then_inc(inner_turned, 1)

                def down(j, expert):
                    pe.wait_ge(innerT_ready, j + 1)
                    if j >= 2:
                        pe.wait_ge(y_ready, j - 1)
                    for k in range(F4):
                        w = wdn[:, bass.ds(expert, 1), k, :].rearrange("p e n -> p (e n)")
                        last = pe.matmul(ps_d[:, j % 2, 0:C], innerT[:, j % 2, k, :], w, start=(k == 0), stop=(k == F4 - 1))
                    last.then_inc(down_done, 1)

                pe.wait_ge(slots_ready, 2)
                pe.wait_ge(g.wgu_came, 16 * NE)
                pe.wait_ge(wdn_came, 16 * NE)
                pe.wait_ge(h_ready, UNITS)
                turn(0)
                experts = []
                for j in range(SLOT_TILES + 2):
                    if j + 1 < SLOT_TILES:
                        turn(j + 1)
                    if j < SLOT_TILES:
                        experts.append(gate_up(j))
                    if 1 <= j <= SLOT_TILES:
                        turn_inner(j - 1)
                    if j >= 2:
                        down(j - 2, experts[j - 2])

                for t in range(NT):
                    if t >= 2:
                        pe.wait_ge(x_done, t - 1)
                    else:
                        pe.wait_ge(y_ready, SLOT_TILES)
                    for k in range(F4):
                        last = pe.matmul(ps_d[0:TP, t % 2, 0:C], hT[:, k, t * TP:(t + 1) * TP], wsdn[:, k, :],
                                         start=(k == 0), stop=(k == F4 - 1))
                    last.then_inc(o_done, 1)

            @block.scalar
            def _(act):
                norm.scalar(act)
                act.wait_ge(top_ready, 1)
                act.activation(sg[:, :], top[:, :], ACT.Sigmoid).then_inc(sg_ready, 1)
                for n in range(UNITS):
                    act.wait_ge(g_done, n + 1)
                    if n >= 2:
                        act.wait_ge(h_ready, n - 1)
                    act.activation(s[:, n % 2, 0:HALF], ps_g[:, n % 2, 0:HALF], ACT.Silu).then_inc(s_ready, 1)
                act.wait_ge(h_ready, UNITS)

                def take_turned(j):
                    act.wait_ge(turned, j + 1)
                    if j >= 2:
                        act.wait_ge(up_done, j - 1)
                    act.copy(xT[:, j % 2, :, :], ps_t[:, 0, 0:CC * 128].rearrange("p (c n) -> p c n", c=CC)).then_inc(xT_ready, 1)

                def take_inner(j):
                    act.wait_ge(inner_turned, j + 1)
                    if j >= 2:
                        act.wait_ge(down_done, j - 1)
                    act.copy(innerT[:, j % 2, :, :], ps_t[:, 1, :].rearrange("p (k n) -> p k n", k=F4)).then_inc(innerT_ready, 1)

                take_turned(0)
                for j in range(SLOT_TILES + 1):
                    if j + 1 < SLOT_TILES:
                        take_turned(j + 1)
                    if j < SLOT_TILES:
                        act.wait_ge(gate_done, j + 1)
                        if j >= 2:
                            act.wait_ge(inner_ready, j - 1)
                        act.activation(s[:, j % 2, :], ps_g[:, j % 2, :], ACT.Silu).then_inc(silu_done, 1)
                    if j >= 1:
                        take_inner(j - 1)

            @block.vector
            def _(dve):
                step = Chain(dve, chain)
                norm.vector(dve)
                dve.wait_ge(l_done, 1)
                wide = lambda v: v.unsqueeze(2).to_broadcast([TP, NT, NE])
                lat = later[0:TP, :].unsqueeze(1).to_broadcast([TP, NT, NE])
                step(dve.tensor_copy(lg[:, :, :], ps_d[0:TP, 0, 0:NT * NE].rearrange("p (t e) -> p t e", e=NE)))
                dve.tensor_reduce(top[:, :], lg[:, :, :], X, ALU.max).then_inc(top_ready, 1)
                dve.wait_ge(top_ready, 1)
                step(dve.tensor_tensor(own[:, :, :], lg[:, :, :], wide(top[:, :]), ALU.is_lt))
                step(dve.scalar_tensor_tensor(out=own[:, :, :], in0=own[:, :, :], scalar=float(NE), in1=lat, op0=ALU.mult, op1=ALU.add))
                step(dve.tensor_reduce(first[:, :], own[:, :, :], X, ALU.min))
                step(dve.memset(cum[:, 0, :], 0.0))
                step(dve.tensor_tensor(own[:, :, :], lat, wide(first[:, :]), ALU.is_equal))
                for t in range(NT - 1):
                    step(dve.tensor_tensor(cum[:, t + 1, :], cum[:, t, :], own[:, t, :], ALU.add))
                dve.tensor_tensor(cum[:, NT, :], cum[:, NT - 1, :], own[:, NT - 1, :], ALU.add).then_inc(own_ready, 1)
                dve.wait_ge(sg_ready, 1)
                for t in range(NT):
                    dve.tensor_scalar(g.xn[:, t, :], g.xn[:, t, :], sg[:, t:t + 1], None, ALU.mult).then_inc(xs_ready, 1)

                def shared_unit(n):
                    m, h = n // 2, n % 2
                    dve.wait_ge(s_ready, n + 1)
                    dve.wait_ge(u_done, n + 1)
                    dve.tensor_tensor(hT[:, m, h * HALF:(h + 1) * HALF], ps_u[:, n % 2, 0:HALF], s[:, n % 2, 0:HALF],
                                      ALU.mult).then_inc(h_ready, 1)

                shared_unit(0)
                shared_unit(1)
                dve.wait_ge(places_done, 1)
                counts = ps_d[0:TP, 1, NT * NE:(NT + 1) * NE]
                step(dve.tensor_scalar(tiles[:, :], counts, 1.0 / 128, 127.0 / 256, ALU.mult, ALU.add))
                step(dve.tensor_scalar(tiles[:, :], tiles[:, :], ROUND, -ROUND, ALU.add, ALU.add))
                step(dve.tensor_copy(ends[:, 0:1], tiles[:, 0:1]))
                for e in range(1, NE):
                    step(dve.tensor_tensor(ends[:, e:e + 1], ends[:, e - 1:e], tiles[:, e:e + 1], ALU.add))
                step(dve.tensor_tensor(base[:, :], ends[:, :], tiles[:, :], ALU.subtract))
                step(dve.tensor_scalar(base[:, :], base[:, :], 128.0, None, ALU.mult))
                step(dve.tensor_tensor(lg[:, :, :], ps_d[0:TP, 1, 0:NT * NE].rearrange("p (t e) -> p t e", e=NE),
                                       base[:, :].unsqueeze(1).to_broadcast([TP, NT, NE]), ALU.add))
                step(dve.tensor_tensor(lg[:, :, :], lg[:, :, :], own[:, :, :], ALU.mult))
                step(dve.tensor_reduce(first[:, :], lg[:, :, :], X, ALU.add))
                dve.tensor_copy(slot[:, :], first[:, :]).then_inc(slots_ready, 1)
                step(dve.tensor_tensor(passed[:, :, :], ends[0:1, :].unsqueeze(1).to_broadcast([1, SLOT_TILES, NE]),
                                       numbers[:, :].unsqueeze(2).to_broadcast([1, SLOT_TILES, NE]), ALU.is_le))
                step(dve.tensor_reduce(of_tile[:, :], passed[:, :, :], X, ALU.add))
                dve.tensor_scalar(of_tile_i[:, :], of_tile[:, :], float(NE - 1), None, ALU.min).then_inc(slots_ready, 1)
                for n in range(2, UNITS):
                    shared_unit(n)

                def take_down(j):
                    dve.wait_ge(down_done, j + 1)
                    dve.wait_ge(turned, j + 1)
                    dve.tensor_copy(rows[:, j, :], ps_d[:, j % 2, 0:C]).then_inc(y_ready, 1)

                for j in range(SLOT_TILES):
                    dve.wait_ge(silu_done, j + 1)
                    dve.wait_ge(up_done, j + 1)
                    if j >= 2:
                        dve.wait_ge(inner_turned, j - 1)
                    dve.tensor_tensor(inner[:, j % 2, :], ps_u[:, j % 2, :], s[:, j % 2, :],
                                      ALU.mult).then_inc(inner_ready, 1)
                    if j >= 2:
                        take_down(j - 2)
                take_down(SLOT_TILES - 2)
                take_down(SLOT_TILES - 1)
                for t in range(NT):
                    dve.wait_ge(o_done, t + 1)
                    dve.scalar_tensor_tensor(out=g.x[:, t, :], in0=ps_d[0:TP, t % 2, 0:C], scalar=gate, in1=g.x[:, t, :],
                                             op0=ALU.mult, op1=ALU.add).then_inc(x_done, 1)
                for t in range(NT):
                    dve.wait_ge(gathered[t], 16)
                    dve.wait_ge(x_done, t + 1)
                    dve.scalar_tensor_tensor(out=g.x[:, t, :], in0=g.xn[:, t, :], scalar=gate, in1=g.x[:, t, :],
                                             op0=ALU.mult, op1=ALU.add).then_inc(x_done, 1)


def program(nc, d, out):
    USED.clear()
    with ExitStack() as ctx:
        g = Shared()
        a = Alloc(nc, ctx, "all", None)
        g.x = a.sb("x", [TP, NT, C])
        g.xn = a.sb("xn", [TP, NT, C])
        g.xnT = a.sb("xnT", [128, CC, T])
        g.ident = a.sb("ident", [128, 128])
        g.gates = a.sb("gates", [128, 8])
        g.eps = a.sb("eps", [128, 1])
        g.stats = a.sb("stats", [TP, NT, 6])
        g.mv = a.sb("mv", [TP, NT, 2])
        g.magnitudes = a.sb("magnitudes", [48, 1])
        with ExitStack() as latent:
            a = Alloc(nc, latent, "latent", None)
            g.q = a.sb("q", [128, HP, T])
            g.fold = a.sb("fold", [128, HP, C])
            g.arena = Arena(nc, "arena0", SHARED_WORDS)
            w = causal_weights(nc, g, d, 0)
            begin(nc, g, d, w)

            ahead = top8_weights(nc, g, d)
            causal_attention(nc, g, d, 0, w, ahead, magnitudes=g.magnitudes[:, :])
            w.ctx.close()

            w, ahead = ahead, plain_weights(nc, g, d)
            top8_ffn(nc, g, w, ahead)
            w.ctx.close()

            w = latent_layer(nc, g, d, 1, queries_plain, ahead, ternary_weights)
            clear_semaphores(nc)

            ahead = roped_weights(nc, g, d)
            ternary_ffn(nc, g, w, ahead)
            w.ctx.close()

            w = latent_layer(nc, g, d, 2, queries_roped, ahead, hadamard_weights)
            hadamard_ffn(nc, g, w, Nothing)
            clear_semaphores(nc)
            w.ctx.close()
            g.arena.ctx.close()

        g.arena = Arena(nc, "arena3", LAST_WORDS)
        w = causal_weights(nc, g, d, 3)
        ahead = experts_weights(nc, g, d)
        causal_attention(nc, g, d, 3, w, ahead, loads=lambda sp: load_experts(g, d, sp), loaded=False)
        w.ctx.close()
        experts_ffn(nc, g, d, ahead, out)
        ahead.ctx.close()
        g.arena.ctx.close()


class Shared:
    pass


def layouts(i):
    f = lambda v: np.ascontiguousarray(v)
    r = {"x": f(i["x"].reshape(T, C)), "g_xattn": f(i["g_xattn"].reshape(1, 4)), "g_ffn": f(i["g_ffn"].reshape(1, 4))}
    first = i["ctx_512"][:, :SK].transpose(2, 0, 1)
    r["ctx_first"] = f(np.stack([first, first], 2).reshape(DC, B * 2 * SK))
    for n in (0, 3):
        r[f"L{n}_wq"] = f(i[f"L{n}_xattn_Wq"].T)
        r[f"L{n}_kv"] = f(i[f"L{n}_xattn_Wkv_expand"].T)
        r[f"L{n}_wo"] = f(i[f"L{n}_xattn_Wout"].T)
    r["L0_rw"] = f(i["L0_ffn_router_weight"].T)
    r["L0_rb"] = f(i["L0_ffn_router_bias"].reshape(1, 64))
    r["L0_eb"] = f(i["L0_ffn_expert_bias"])
    r["ctx_cols"] = f(i["ctx_512"].reshape(B, KP, KT, DC).transpose(0, 3, 2, 1).reshape(B, DC * LK))
    r["ctx"] = f(i["ctx_512"].reshape(B, LK * DC))
    for n in (1, 2):
        w = {k: i[f"L{n}_xattn_{k}"] for k in ("Wq", "w_kc_q", "w_kc_kv", "W_qr", "W_kr", "Wo")}
        r[f"L{n}_wq"] = f(w["Wq"].reshape(NH, HK, C).transpose(1, 0, 2).reshape(HK, NH * C))
        r[f"L{n}_wkrT"] = f(w["W_kr"].transpose(2, 0, 1).reshape(64, NH * DC))
        r[f"L{n}_wkv"] = f(w["w_kc_kv"].transpose(1, 0, 2).reshape(HK, NH * DC))
        r[f"L{n}_wo"] = f(w["Wo"].reshape(C, NH, HK).transpose(2, 1, 0).reshape(HK, NH * C))
        wqrT = w["W_qr"].transpose(2, 0, 1)
        if n == 1:
            r["L1_wqrT"] = f(wqrT.reshape(64, NH * DQ))
            r["L1_wcqT"] = f(w["w_kc_q"].transpose(2, 0, 1).reshape(2, DQ // 2, NH, HK).transpose(1, 0, 2, 3).reshape(DQ // 2, 2 * NH * HK))
        else:
            half = DQ // 2
            turned = np.concatenate([wqrT[:, :, half:], wqrT[:, :, :half]], 2)
            r["L2_wqrT"] = f(np.stack([wqrT, turned], 1).reshape(64, 2 * NH * DQ))
            r["L2_wcq"] = f(w["w_kc_q"].transpose(1, 0, 2).reshape(HK, NH * DQ))
    r["L1_gate"], r["L1_up"], r["L1_down"] = (f(i[f"L1_ffn_w_{k}"].T) for k in ("gate", "up", "down"))
    r["L1_lanes"] = f(np.concatenate([i[f"L1_ffn_w_{k}"].reshape(-1, 16).T for k in ("gate", "up", "down")]))
    r["L2_gate"], r["L2_up"], r["L2_down"] = (f(i[f"L2_ffn_W_{k}"].T) for k in ("gate", "up", "down"))
    r["L2_su_ug"] = f(i["L2_ffn_SU_ug"].reshape(CC, 128).T)
    r["L2_su_dp"] = f(i["L2_ffn_SU_dp"].reshape(FF // 128, 128).T)
    r["L2_sc_ug"] = f(i["L2_ffn_Wscale_ug"].reshape(2 * FF // 128, 128).T)
    r["L2_sc_dp"] = f(i["L2_ffn_Wscale_dp"].reshape(1, C))
    r["L3_rw"] = f(i["L3_ffn_router_w"].T)
    r["L3_gu"], r["L3_dn"] = f(i["L3_ffn_w_gate_up"]), f(i["L3_ffn_w_down"])
    r["L3_sgu"], r["L3_sdn"] = f(i["L3_ffn_shared_gate_up"]), f(i["L3_ffn_shared_down"])
    return r


def kernel(**inputs):
    import concourse.bacc as bacc
    from concourse.bass_utils import run_bass_kernel_spmd

    nc = bacc.Bacc("TRN2", target_bir_lowering=False, num_devices=1)
    arrays = layouts({k: np.asarray(v) for k, v in inputs.items()}) | constants()
    d = {k: nc.dram_tensor(f"in_{k}", v.shape, mybir.dt.from_np(v.dtype), kind="ExternalInput").ap()
         for k, v in arrays.items()}
    out = nc.dram_tensor("out_x", (T, C), F32, kind="ExternalOutput").ap()
    program(nc, d, out)
    r = run_bass_kernel_spmd(nc, [{f"in_{k}": v for k, v in arrays.items()}], core_ids=[0])
    return r.results[0]["out_x"].reshape(B, S, C)
```
